# Optimizing a Trainium2 kernel written in Bass

```python
import numpy as np
import jax
import jax.numpy as jnp

def _softmax(x, axis=-1):
    return jax.nn.softmax(x, axis=axis)

def _gelu(x):
    return jax.nn.gelu(x, approximate=True)

def _silu(x):
    return jax.nn.silu(x)

def _sigmoid(x):
    return jax.nn.sigmoid(x)

def _layernorm(x, axis=-1, eps=1e-05):
    m = jnp.mean(x, axis=axis, keepdims=True)
    v = jnp.var(x, axis=axis, keepdims=True)
    return (x - m) / jnp.sqrt(v + eps)

def _scatter_add(tgt, idx, src, axis=0):
    return tgt.at[idx].add(src)

def _segment_sum(src, seg, n):
    return jax.ops.segment_sum(src, seg, n)
kernel_name = 'mk_metaformer_d4_conv_nchw256_r4_7f0809'

def setup_inputs(seed: int=0):
    np.random.seed(seed)
    _w = jnp.asarray

    def _rec_inputs():
        import jax
        import jax.numpy as jnp
        _gk = jax.random.key(seed)
        x = -0.000125 + 0.9999 * jax.random.normal(jax.random.fold_in(_gk, 1), (8, 64, 32, 32), jnp.float32)
        return x
    x = _rec_inputs()

    def _L0_conv_setup():
        import jax, jax.numpy as jnp
        import numpy as np
        HEADS = 8
        DIM = 32
        key = jax.random.key(seed)
        k1, k2, k3, k4 = jax.random.split(key, 4)
        b, c, h, w = (8, 64, 32, 32)
        hidden = HEADS * DIM
        x = jax.random.normal(k1, (b, c, h, w), dtype=jnp.float32)
        w_qkv = jax.random.normal(k2, (3 * hidden, c), dtype=jnp.float32) * 0.05
        w_out = jax.random.normal(k3, (c, hidden), dtype=jnp.float32) * 0.05
        b_out = jax.random.normal(k4, (c,), dtype=jnp.float32) * 0.05
        return {'x': x, 'w_qkv': w_qkv, 'w_out': w_out, 'b_out': b_out}
    _L0_conv_all = _L0_conv_setup()
    _L0_conv_in = {k: v for k, v in _L0_conv_all.items() if k in ('w_qkv', 'w_out', 'b_out')}
    del _L0_conv_all

    def _L0_ffn_setup():
        import jax, jax.numpy as jnp
        import numpy as np
        TOP_K = 2
        key = jax.random.key(seed)
        ks = jax.random.split(key, 4)
        B, L, D, H, E = (8, 1024, 64, 256, 8)
        s = 0.02
        return {'x': jax.random.normal(ks[0], (B, L, D), jnp.float32), 'Wg': jax.random.normal(ks[1], (D, E), jnp.float32) * s, 'bg': jnp.zeros((E,), jnp.float32), 'W1': jax.random.normal(ks[2], (E, D, H), jnp.float32) * s, 'b1': jnp.zeros((E, H), jnp.float32), 'W2': jax.random.normal(ks[3], (E, H, D), jnp.float32) * s, 'b2': jnp.zeros((E, D), jnp.float32)}
    _L0_ffn_all = _L0_ffn_setup()
    _L0_ffn_in = {k: v for k, v in _L0_ffn_all.items() if k in ('Wg', 'bg', 'W1', 'b1', 'W2', 'b2')}
    del _L0_ffn_all

    def _L1_conv_setup():
        import jax, jax.numpy as jnp
        import numpy as np
        GAMMA = 2.0
        EPS = 1e-08
        key = jax.random.key(seed)
        k1, k2, k3 = jax.random.split(key, 3)
        B, C, H, W_ = (4, 64, 16, 16)
        x = jax.random.normal(k1, (B, C, H, W_), dtype=jnp.float32)
        W = jax.random.normal(k2, (C, C), dtype=jnp.float32) * (1.0 / np.sqrt(C))
        b = jax.random.normal(k3, (C,), dtype=jnp.float32) * 0.01
        return {'x': x, 'W': W, 'b': b}
    _L1_conv_all = _L1_conv_setup()
    _L1_conv_in = {k: v for k, v in _L1_conv_all.items() if k in ('W', 'b')}
    del _L1_conv_all

    def _L1_ffn_setup():
        import jax, jax.numpy as jnp
        import numpy as np
        B, T, D, H, E = (16, 1024, 64, 128, 8)
        key = jax.random.key(seed)
        ks = jax.random.split(key, 5)
        x = jax.random.normal(ks[0], (B, T, D), dtype=jnp.float32)
        gate_w = jax.random.normal(ks[1], (D, E), dtype=jnp.float32) * 0.02
        gate_b = jnp.zeros((E,), dtype=jnp.float32)
        W1 = jax.random.normal(ks[2], (E, D, H), dtype=jnp.float32) * 0.02
        b1 = jnp.zeros((E, H), dtype=jnp.float32)
        W2 = jax.random.normal(ks[3], (E, H, D), dtype=jnp.float32) * 0.02
        b2 = jnp.zeros((E, D), dtype=jnp.float32)
        return {'x': x, 'gate_w': gate_w, 'gate_b': gate_b, 'W1': W1, 'b1': b1, 'W2': W2, 'b2': b2}
    _L1_ffn_all = _L1_ffn_setup()
    _L1_ffn_in = {k: v for k, v in _L1_ffn_all.items() if k in ('gate_w', 'gate_b', 'W1', 'b1', 'W2', 'b2')}
    del _L1_ffn_all

    def _L2_conv_setup():
        import jax, jax.numpy as jnp
        import numpy as np
        B0, CIN, Hh, Ww = (8, 64, 24, 24)
        SPLIT = 8
        DM = CIN // SPLIT
        EXPAND = 2
        DIN = EXPAND * DM
        DSTATE = 16
        DCONV = 3
        HEADDIM = 8
        NH = DIN // HEADDIM
        DOUT = 64
        CHUNK = 32
        D_IN_PROJ = 2 * DIN + 2 * DSTATE + NH
        CONV_CH = DIN + 2 * DSTATE

        def _layernorm(x, w, b, eps=1e-05):
            mu = jnp.mean(x, -1, keepdims=True)
            xc = x - mu
            var = jnp.mean(xc * xc, -1, keepdims=True)
            return xc * jax.lax.rsqrt(var + eps) * w + b

        def _ssd(x, A, Bm, Cm, chunk):
            b, l, h, p = x.shape
            n = Bm.shape[-1]
            nc = l // chunk
            xc = x.reshape(b, nc, chunk, h, p)
            Ac = A.reshape(b, nc, chunk, h).transpose(0, 3, 1, 2)
            Bc = Bm.reshape(b, nc, chunk, n)
            Cc = Cm.reshape(b, nc, chunk, n)
            ac = jnp.cumsum(Ac, -1)
            seg = ac[..., :, None] - ac[..., None, :]
            mask = jnp.tril(jnp.ones((chunk, chunk), bool))
            L = jnp.where(mask, jnp.exp(jnp.where(mask, seg, 0.0)), 0.0)
            Yd = jnp.einsum('bcln,bcsn,bhcls,bcshp->bclhp', Cc, Bc, L, xc)
            decay_states = jnp.exp(ac[..., -1:] - ac)
            states = jnp.einsum('bcln,bhcl,bclhp->bchpn', Bc, decay_states, xc)
            chunk_decay = jnp.exp(ac[..., -1])

            def step(carry, inp):
                s, d = inp
                return (carry * d[..., None, None] + s, carry)
            states_t = jnp.moveaxis(states, 1, 0)
            dec_t = jnp.moveaxis(chunk_decay, 2, 0)
            _, prev = jax.lax.scan(step, jnp.zeros_like(states_t[0]), (states_t, dec_t))
            prev = jnp.moveaxis(prev, 0, 1)
            Yo = jnp.einsum('bcln,bchpn,bhcl->bclhp', Cc, prev, jnp.exp(ac))
            return (Yd + Yo).reshape(b, l, h, p)

        def _mamba2(u, W_in, conv_w, conv_b, dt_bias, A_log, D, rms_w, W_out):
            b, l, _ = u.shape
            zxbcdt = u @ W_in
            z = zxbcdt[..., :DIN]
            xBC = zxbcdt[..., DIN:DIN + CONV_CH]
            dt = jax.nn.softplus(zxbcdt[..., -NH:] + dt_bias)
            conv = jax.lax.conv_general_dilated(xBC.transpose(0, 2, 1), conv_w, (1,), [(DCONV - 1, 0)], dimension_numbers=('NCH', 'OIH', 'NCH'), feature_group_count=CONV_CH)
            xBC = jax.nn.silu(conv + conv_b[None, :, None]).transpose(0, 2, 1)
            xs = xBC[..., :DIN].reshape(b, l, NH, HEADDIM)
            Bm = xBC[..., DIN:DIN + DSTATE]
            Cm = xBC[..., DIN + DSTATE:]
            A = -jnp.exp(A_log)
            y = _ssd(xs * dt[..., None], dt * A, Bm, Cm, CHUNK)
            y = y + xs * D[None, None, :, None]
            y = y.reshape(b, l, DIN) * jax.nn.silu(z)
            y = y * jax.lax.rsqrt(jnp.mean(y * y, -1, keepdims=True) + 1e-05) * rms_w
            return y @ W_out
        key = jax.random.key(seed)
        ks = jax.random.split(key, 10)
        x = jax.random.normal(ks[0], (B0, CIN, Hh, Ww), jnp.float32)
        inp = {'x': x, 'ln_w': jnp.ones((CIN,), jnp.float32), 'ln_b': jnp.zeros((CIN,), jnp.float32), 'skip_scale': jnp.ones((1,), jnp.float32), 'proj_w': jax.random.normal(ks[1], (CIN, DOUT), jnp.float32) / np.sqrt(CIN), 'proj_b': jnp.zeros((DOUT,), jnp.float32), 'W_in': jax.random.normal(ks[2], (DM, D_IN_PROJ), jnp.float32) / np.sqrt(DM), 'conv_w': jax.random.normal(ks[3], (CONV_CH, 1, DCONV), jnp.float32) * 0.3, 'conv_b': jnp.zeros((CONV_CH,), jnp.float32), 'dt_bias': jax.random.normal(ks[4], (NH,), jnp.float32) * 0.5, 'A_log': jnp.log(jnp.arange(1.0, NH + 1.0, dtype=jnp.float32)), 'D': jax.random.normal(ks[5], (NH,), jnp.float32) * 0.5, 'rms_w': jnp.ones((DIN,), jnp.float32), 'W_out': jax.random.normal(ks[6], (DIN, DM), jnp.float32) / np.sqrt(DIN)}
        return inp
    _L2_conv_all = _L2_conv_setup()
    _L2_conv_in = {k: v for k, v in _L2_conv_all.items() if k in ('ln_w', 'ln_b', 'skip_scale', 'proj_w', 'proj_b', 'W_in', 'conv_w', 'conv_b', 'dt_bias', 'A_log', 'D', 'rms_w', 'W_out')}
    del _L2_conv_all

    def _L2_ffn_setup():
        import jax, jax.numpy as jnp
        import numpy as np
        TOP_K = 2
        key = jax.random.key(seed)
        ks = jax.random.split(key, 4)
        B, L, D, H, E = (8, 1024, 64, 256, 8)
        s = 0.02
        return {'x': jax.random.normal(ks[0], (B, L, D), jnp.float32), 'Wg': jax.random.normal(ks[1], (D, E), jnp.float32) * s, 'bg': jnp.zeros((E,), jnp.float32), 'W1': jax.random.normal(ks[2], (E, D, H), jnp.float32) * s, 'b1': jnp.zeros((E, H), jnp.float32), 'W2': jax.random.normal(ks[3], (E, H, D), jnp.float32) * s, 'b2': jnp.zeros((E, D), jnp.float32)}
    _L2_ffn_all = _L2_ffn_setup()
    _L2_ffn_in = {k: v for k, v in _L2_ffn_all.items() if k in ('Wg', 'bg', 'W1', 'b1', 'W2', 'b2')}
    del _L2_ffn_all

    def _L3_conv_setup():
        import jax, jax.numpy as jnp
        import numpy as np
        C = 64
        K = 3
        BN_EPS = 1e-05

        def _involution(x, w_reduce, w_span, gamma, beta):
            B, Ch, H, W = x.shape
            r = jnp.einsum('bchw,oc->bohw', x, w_reduce)
            mean = jnp.mean(r, axis=(0, 2, 3), keepdims=True)
            var = jnp.var(r, axis=(0, 2, 3), keepdims=True)
            r = (r - mean) * jax.lax.rsqrt(var + BN_EPS)
            r = r * gamma[None, :, None, None] + beta[None, :, None, None]
            r = jax.nn.relu(r)
            kern = jnp.einsum('bchw,kc->bkhw', r, w_span)
            xp = jnp.pad(x, ((0, 0), (0, 0), (1, 1), (1, 1)))
            patches = jnp.stack([xp[:, :, i:i + H, j:j + W] for i in range(K) for j in range(K)], axis=2)
            return jnp.einsum('bckhw,bkhw->bchw', patches, kern)
        key = jax.random.key(seed)
        k1, k2, k3 = jax.random.split(key, 3)
        x = jax.random.normal(k1, (4, C, 24, 24), dtype=jnp.float32)
        w_reduce = jax.random.normal(k2, (C, C), dtype=jnp.float32) * (1.0 / np.sqrt(C))
        w_span = jax.random.normal(k3, (K * K, C), dtype=jnp.float32) * (1.0 / np.sqrt(C))
        gamma = jnp.ones((C,), dtype=jnp.float32)
        beta = jnp.zeros((C,), dtype=jnp.float32)
        return {'x': x, 'w_reduce': w_reduce, 'w_span': w_span, 'gamma': gamma, 'beta': beta}
    _L3_conv_all = _L3_conv_setup()
    _L3_conv_in = {k: v for k, v in _L3_conv_all.items() if k in ('w_reduce', 'w_span', 'gamma', 'beta')}
    del _L3_conv_all

    def _L3_ffn_setup():
        import jax, jax.numpy as jnp
        import numpy as np
        TOP_K = 2
        LN_EPS = 1e-05
        key = jax.random.key(seed)
        ks = jax.random.split(key, 8)
        B, S, D, E, H = (16, 256, 64, 8, 256)
        x = jax.random.normal(ks[0], (B, S, D), dtype=jnp.float32)
        Wr = jax.random.normal(ks[1], (D, E), dtype=jnp.float32) * 0.1
        br = jnp.zeros((E,), dtype=jnp.float32)
        ln_g = jnp.ones((E, D), dtype=jnp.float32)
        ln_b = jnp.zeros((E, D), dtype=jnp.float32)
        W1 = jax.random.normal(ks[2], (E, D, H), dtype=jnp.float32) * (1.0 / np.sqrt(D))
        b1 = jnp.zeros((E, H), dtype=jnp.float32)
        W2 = jax.random.normal(ks[3], (E, H, D), dtype=jnp.float32) * (1.0 / np.sqrt(H))
        b2 = jnp.zeros((E, D), dtype=jnp.float32)
        return {'x': x, 'Wr': Wr, 'br': br, 'ln_g': ln_g, 'ln_b': ln_b, 'W1': W1, 'b1': b1, 'W2': W2, 'b2': b2}
    _L3_ffn_all = _L3_ffn_setup()
    _L3_ffn_in = {k: v for k, v in _L3_ffn_all.items() if k in ('Wr', 'br', 'ln_g', 'ln_b', 'W1', 'b1', 'W2', 'b2')}
    del _L3_ffn_all
    return {'x': x, 'L0_conv_w_qkv': _L0_conv_in['w_qkv'], 'L0_conv_w_out': _L0_conv_in['w_out'], 'L0_conv_b_out': _L0_conv_in['b_out'], 'L0_ffn_Wg': _L0_ffn_in['Wg'], 'L0_ffn_bg': _L0_ffn_in['bg'], 'L0_ffn_W1': _L0_ffn_in['W1'], 'L0_ffn_b1': _L0_ffn_in['b1'], 'L0_ffn_W2': _L0_ffn_in['W2'], 'L0_ffn_b2': _L0_ffn_in['b2'], 'L1_conv_W': _L1_conv_in['W'], 'L1_conv_b': _L1_conv_in['b'], 'L1_ffn_gate_w': _L1_ffn_in['gate_w'], 'L1_ffn_gate_b': _L1_ffn_in['gate_b'], 'L1_ffn_W1': _L1_ffn_in['W1'], 'L1_ffn_b1': _L1_ffn_in['b1'], 'L1_ffn_W2': _L1_ffn_in['W2'], 'L1_ffn_b2': _L1_ffn_in['b2'], 'L2_conv_ln_w': _L2_conv_in['ln_w'], 'L2_conv_ln_b': _L2_conv_in['ln_b'], 'L2_conv_skip_scale': _L2_conv_in['skip_scale'], 'L2_conv_proj_w': _L2_conv_in['proj_w'], 'L2_conv_proj_b': _L2_conv_in['proj_b'], 'L2_conv_W_in': _L2_conv_in['W_in'], 'L2_conv_conv_w': _L2_conv_in['conv_w'], 'L2_conv_conv_b': _L2_conv_in['conv_b'], 'L2_conv_dt_bias': _L2_conv_in['dt_bias'], 'L2_conv_A_log': _L2_conv_in['A_log'], 'L2_conv_D': _L2_conv_in['D'], 'L2_conv_rms_w': _L2_conv_in['rms_w'], 'L2_conv_W_out': _L2_conv_in['W_out'], 'L2_ffn_Wg': _L2_ffn_in['Wg'], 'L2_ffn_bg': _L2_ffn_in['bg'], 'L2_ffn_W1': _L2_ffn_in['W1'], 'L2_ffn_b1': _L2_ffn_in['b1'], 'L2_ffn_W2': _L2_ffn_in['W2'], 'L2_ffn_b2': _L2_ffn_in['b2'], 'L3_conv_w_reduce': _L3_conv_in['w_reduce'], 'L3_conv_w_span': _L3_conv_in['w_span'], 'L3_conv_gamma': _L3_conv_in['gamma'], 'L3_conv_beta': _L3_conv_in['beta'], 'L3_ffn_Wr': _L3_ffn_in['Wr'], 'L3_ffn_br': _L3_ffn_in['br'], 'L3_ffn_ln_g': _L3_ffn_in['ln_g'], 'L3_ffn_ln_b': _L3_ffn_in['ln_b'], 'L3_ffn_W1': _L3_ffn_in['W1'], 'L3_ffn_b1': _L3_ffn_in['b1'], 'L3_ffn_W2': _L3_ffn_in['W2'], 'L3_ffn_b2': _L3_ffn_in['b2']}

def reference(x, L0_conv_w_qkv, L0_conv_w_out, L0_conv_b_out, L0_ffn_Wg, L0_ffn_bg, L0_ffn_W1, L0_ffn_b1, L0_ffn_W2, L0_ffn_b2, L1_conv_W, L1_conv_b, L1_ffn_gate_w, L1_ffn_gate_b, L1_ffn_W1, L1_ffn_b1, L1_ffn_W2, L1_ffn_b2, L2_conv_ln_w, L2_conv_ln_b, L2_conv_skip_scale, L2_conv_proj_w, L2_conv_proj_b, L2_conv_W_in, L2_conv_conv_w, L2_conv_conv_b, L2_conv_dt_bias, L2_conv_A_log, L2_conv_D, L2_conv_rms_w, L2_conv_W_out, L2_ffn_Wg, L2_ffn_bg, L2_ffn_W1, L2_ffn_b1, L2_ffn_W2, L2_ffn_b2, L3_conv_w_reduce, L3_conv_w_span, L3_conv_gamma, L3_conv_beta, L3_ffn_Wr, L3_ffn_br, L3_ffn_ln_g, L3_ffn_ln_b, L3_ffn_W1, L3_ffn_b1, L3_ffn_W2, L3_ffn_b2):
    import jax
    import jax.numpy as jnp

    def _L0_conv_ref(x, w_qkv, w_out, b_out):
        import jax, jax.numpy as jnp
        import numpy as np
        HEADS = 8
        DIM = 32
        b, c, h, w = x.shape
        n = h * w
        qkv = jnp.einsum('bchw,oc->bohw', x, w_qkv)
        qkv = qkv.reshape(b, 3, HEADS, DIM, n)
        q, k, v = (qkv[:, 0], qkv[:, 1], qkv[:, 2])
        k = jax.nn.softmax(k, axis=-1)
        context = jnp.einsum('bhdn,bhen->bhde', k, v)
        o = jnp.einsum('bhde,bhdn->bhen', context, q)
        o = o.reshape(b, HEADS * DIM, h, w)
        o = jnp.einsum('bchw,oc->bohw', o, w_out) + b_out[None, :, None, None]
        return o

    def _L0_ffn_ref(x, Wg, bg, W1, b1, W2, b2):
        import jax, jax.numpy as jnp
        import numpy as np
        TOP_K = 2
        B, L, D = x.shape
        E = W1.shape[0]
        xf = x.reshape(-1, D)
        gate_logits = xf @ Wg + bg
        top_w, top_i = jax.lax.top_k(gate_logits, TOP_K)
        top_w = jax.nn.softmax(top_w, axis=-1)
        w_dense = jnp.sum(jax.nn.one_hot(top_i, E, dtype=xf.dtype) * top_w[..., None], axis=1)
        out = jnp.zeros_like(xf)
        for e in range(E):
            h = jax.nn.gelu(xf @ W1[e] + b1[e], approximate=False)
            out = out + w_dense[:, e:e + 1] * (h @ W2[e] + b2[e])
        return out.reshape(B, L, D)

    def _L1_conv_ref(x, W, b):
        import jax, jax.numpy as jnp
        import numpy as np
        GAMMA = 2.0
        EPS = 1e-08
        B, C, H, W_ = x.shape
        N = H * W_
        xf = x.reshape(B, C, N)
        norm = jnp.maximum(jnp.sqrt(jnp.sum(xf * xf, axis=1)), EPS)
        xn = xf / norm[:, None, :]
        sim = jnp.einsum('bcn,bcm->bnm', xn, xn)
        sim = jax.nn.relu(sim) ** GAMMA
        t = jnp.einsum('oc,bchw->bohw', W, x) + b[None, :, None, None]
        tf = t.reshape(B, C, N)
        out = jnp.einsum('bnm,bcm->bcn', sim, tf)
        return out.reshape(B, C, H, W_)

    def _L1_ffn_ref(x, gate_w, gate_b, W1, b1, W2, b2):
        import jax, jax.numpy as jnp
        import numpy as np
        B, T, D, H, E = (16, 1024, 64, 128, 8)
        Bb, Tt, Dd = x.shape
        Ee = gate_w.shape[1]
        xf = x.reshape(-1, Dd)
        N = xf.shape[0]
        logits = xf @ gate_w + gate_b
        probs = jax.nn.softmax(logits, axis=-1)
        top2_vals, top2_idx = jax.lax.top_k(probs, 2)
        cw = jnp.zeros((N, Ee), dtype=xf.dtype).at[jnp.arange(N)[:, None], top2_idx].add(top2_vals)

        def step(acc, params):
            w1, bb1, w2, bb2, we = params
            h = jax.nn.gelu(xf @ w1 + bb1, approximate=False)
            y = h @ w2 + bb2
            return (acc + we[:, None] * y, None)
        out, _ = jax.lax.scan(step, jnp.zeros_like(xf), (W1, b1, W2, b2, cw.T))
        return out.reshape(Bb, Tt, Dd)

    def _L2_conv_ref(x, ln_w, ln_b, skip_scale, proj_w, proj_b, W_in, conv_w, conv_b, dt_bias, A_log, D, rms_w, W_out):
        import jax, jax.numpy as jnp
        import numpy as np
        B0, CIN, Hh, Ww = (8, 64, 24, 24)
        SPLIT = 8
        DM = CIN // SPLIT
        EXPAND = 2
        DIN = EXPAND * DM
        DSTATE = 16
        DCONV = 3
        HEADDIM = 8
        NH = DIN // HEADDIM
        DOUT = 64
        CHUNK = 32
        D_IN_PROJ = 2 * DIN + 2 * DSTATE + NH
        CONV_CH = DIN + 2 * DSTATE

        def _layernorm(x, w, b, eps=1e-05):
            mu = jnp.mean(x, -1, keepdims=True)
            xc = x - mu
            var = jnp.mean(xc * xc, -1, keepdims=True)
            return xc * jax.lax.rsqrt(var + eps) * w + b

        def _ssd(x, A, Bm, Cm, chunk):
            b, l, h, p = x.shape
            n = Bm.shape[-1]
            nc = l // chunk
            xc = x.reshape(b, nc, chunk, h, p)
            Ac = A.reshape(b, nc, chunk, h).transpose(0, 3, 1, 2)
            Bc = Bm.reshape(b, nc, chunk, n)
            Cc = Cm.reshape(b, nc, chunk, n)
            ac = jnp.cumsum(Ac, -1)
            seg = ac[..., :, None] - ac[..., None, :]
            mask = jnp.tril(jnp.ones((chunk, chunk), bool))
            L = jnp.where(mask, jnp.exp(jnp.where(mask, seg, 0.0)), 0.0)
            Yd = jnp.einsum('bcln,bcsn,bhcls,bcshp->bclhp', Cc, Bc, L, xc)
            decay_states = jnp.exp(ac[..., -1:] - ac)
            states = jnp.einsum('bcln,bhcl,bclhp->bchpn', Bc, decay_states, xc)
            chunk_decay = jnp.exp(ac[..., -1])

            def step(carry, inp):
                s, d = inp
                return (carry * d[..., None, None] + s, carry)
            states_t = jnp.moveaxis(states, 1, 0)
            dec_t = jnp.moveaxis(chunk_decay, 2, 0)
            _, prev = jax.lax.scan(step, jnp.zeros_like(states_t[0]), (states_t, dec_t))
            prev = jnp.moveaxis(prev, 0, 1)
            Yo = jnp.einsum('bcln,bchpn,bhcl->bclhp', Cc, prev, jnp.exp(ac))
            return (Yd + Yo).reshape(b, l, h, p)

        def _mamba2(u, W_in, conv_w, conv_b, dt_bias, A_log, D, rms_w, W_out):
            b, l, _ = u.shape
            zxbcdt = u @ W_in
            z = zxbcdt[..., :DIN]
            xBC = zxbcdt[..., DIN:DIN + CONV_CH]
            dt = jax.nn.softplus(zxbcdt[..., -NH:] + dt_bias)
            conv = jax.lax.conv_general_dilated(xBC.transpose(0, 2, 1), conv_w, (1,), [(DCONV - 1, 0)], dimension_numbers=('NCH', 'OIH', 'NCH'), feature_group_count=CONV_CH)
            xBC = jax.nn.silu(conv + conv_b[None, :, None]).transpose(0, 2, 1)
            xs = xBC[..., :DIN].reshape(b, l, NH, HEADDIM)
            Bm = xBC[..., DIN:DIN + DSTATE]
            Cm = xBC[..., DIN + DSTATE:]
            A = -jnp.exp(A_log)
            y = _ssd(xs * dt[..., None], dt * A, Bm, Cm, CHUNK)
            y = y + xs * D[None, None, :, None]
            y = y.reshape(b, l, DIN) * jax.nn.silu(z)
            y = y * jax.lax.rsqrt(jnp.mean(y * y, -1, keepdims=True) + 1e-05) * rms_w
            return y @ W_out
        Bn, C, h, w = x.shape
        L = h * w
        xf = x.reshape(Bn, C, L).transpose(0, 2, 1)
        xn = _layernorm(xf, ln_w, ln_b)
        d = C // SPLIT
        xs = jnp.moveaxis(xn.reshape(Bn, L, SPLIT, d), 2, 0)
        xs = xs.reshape(SPLIT * Bn, L, d)
        ym = _mamba2(xs, W_in, conv_w, conv_b, dt_bias, A_log, D, rms_w, W_out)
        ym = ym + skip_scale * xs
        ym = jnp.moveaxis(ym.reshape(SPLIT, Bn, L, d), 0, 2).reshape(Bn, L, C)
        ym = _layernorm(ym, ln_w, ln_b)
        out = ym @ proj_w + proj_b
        return out.transpose(0, 2, 1).reshape(Bn, DOUT, h, w)

    def _L2_ffn_ref(x, Wg, bg, W1, b1, W2, b2):
        import jax, jax.numpy as jnp
        import numpy as np
        TOP_K = 2
        B, L, D = x.shape
        E = W1.shape[0]
        xf = x.reshape(-1, D)
        gate_logits = xf @ Wg + bg
        top_w, top_i = jax.lax.top_k(gate_logits, TOP_K)
        top_w = jax.nn.softmax(top_w, axis=-1)
        w_dense = jnp.sum(jax.nn.one_hot(top_i, E, dtype=xf.dtype) * top_w[..., None], axis=1)
        out = jnp.zeros_like(xf)
        for e in range(E):
            h = jax.nn.gelu(xf @ W1[e] + b1[e], approximate=False)
            out = out + w_dense[:, e:e + 1] * (h @ W2[e] + b2[e])
        return out.reshape(B, L, D)

    def _L3_conv_ref(x, w_reduce, w_span, gamma, beta):
        import jax, jax.numpy as jnp
        import numpy as np
        C = 64
        K = 3
        BN_EPS = 1e-05

        def _involution(x, w_reduce, w_span, gamma, beta):
            B, Ch, H, W = x.shape
            r = jnp.einsum('bchw,oc->bohw', x, w_reduce)
            mean = jnp.mean(r, axis=(0, 2, 3), keepdims=True)
            var = jnp.var(r, axis=(0, 2, 3), keepdims=True)
            r = (r - mean) * jax.lax.rsqrt(var + BN_EPS)
            r = r * gamma[None, :, None, None] + beta[None, :, None, None]
            r = jax.nn.relu(r)
            kern = jnp.einsum('bchw,kc->bkhw', r, w_span)
            xp = jnp.pad(x, ((0, 0), (0, 0), (1, 1), (1, 1)))
            patches = jnp.stack([xp[:, :, i:i + H, j:j + W] for i in range(K) for j in range(K)], axis=2)
            return jnp.einsum('bckhw,bkhw->bchw', patches, kern)
        out = _involution(x, w_reduce, w_span, gamma, beta)
        return out + out

    def _L3_ffn_ref(x, Wr, br, ln_g, ln_b, W1, b1, W2, b2):
        import jax, jax.numpy as jnp
        import numpy as np
        TOP_K = 2
        LN_EPS = 1e-05
        B, S, D = x.shape
        N = B * S
        xt = x.reshape(N, D)
        logits = xt @ Wr + br
        probs = jax.nn.softmax(logits, axis=-1)
        top_p, top_idx = jax.lax.top_k(probs, TOP_K)
        weights = top_p / top_p.sum(axis=-1, keepdims=True)
        mu = xt.mean(axis=-1, keepdims=True)
        var = ((xt - mu) ** 2).mean(axis=-1, keepdims=True)
        xn = (xt - mu) * jax.lax.rsqrt(var + LN_EPS)
        xe = xn[None, :, :] * ln_g[:, None, :] + ln_b[:, None, :]
        h = jax.nn.gelu(jnp.einsum('end,edh->enh', xe, W1) + b1[:, None, :], approximate=False)
        y = jnp.einsum('enh,ehd->end', h, W2) + b2[:, None, :]
        y_tok = jnp.transpose(y, (1, 0, 2))
        sel = jnp.take_along_axis(y_tok, top_idx[:, :, None], axis=1)
        out = (weights[:, :, None] * sel).sum(axis=1)
        return out.reshape(B, S, D)

    def _gn(v, G=32, eps=1e-05):
        B_, C_, H_, W_ = v.shape
        g = v.reshape(B_, G, C_ // G, H_, W_)
        m = jnp.mean(g, axis=(2, 3, 4), keepdims=True)
        s = jnp.var(g, axis=(2, 3, 4), keepdims=True)
        return ((g - m) / jnp.sqrt(s + eps)).reshape(v.shape)

    def _ln_c(v, eps=1e-06):
        m = jnp.mean(v, axis=1, keepdims=True)
        s = jnp.var(v, axis=1, keepdims=True)
        return (v - m) / jnp.sqrt(s + eps)

    def _ln_t(v, eps=1e-05):
        m = jnp.mean(v, axis=-1, keepdims=True)
        s = jnp.var(v, axis=-1, keepdims=True)
        return (v - m) / jnp.sqrt(s + eps)

    def _to_tokens(v):
        B_, C_, H_, W_ = v.shape
        return v.reshape(B_, C_, H_ * W_).transpose(0, 2, 1)

    def _from_tokens(t, like):
        B_, C_, H_, W_ = like.shape
        return t.transpose(0, 2, 1).reshape(B_, C_, H_, W_)
    x = x + _L0_conv_ref(_ln_c(x), L0_conv_w_qkv, L0_conv_w_out, L0_conv_b_out)
    t = _to_tokens(x)
    t = t + _L0_ffn_ref(_ln_t(t), L0_ffn_Wg, L0_ffn_bg, L0_ffn_W1, L0_ffn_b1, L0_ffn_W2, L0_ffn_b2)
    x = _from_tokens(t, x)
    x = x + _L1_conv_ref(_ln_c(x), L1_conv_W, L1_conv_b)
    t = _to_tokens(x)
    t = t + _L1_ffn_ref(_ln_t(t), L1_ffn_gate_w, L1_ffn_gate_b, L1_ffn_W1, L1_ffn_b1, L1_ffn_W2, L1_ffn_b2)
    x = _from_tokens(t, x)
    x = x + _L2_conv_ref(_ln_c(x), L2_conv_ln_w, L2_conv_ln_b, L2_conv_skip_scale, L2_conv_proj_w, L2_conv_proj_b, L2_conv_W_in, L2_conv_conv_w, L2_conv_conv_b, L2_conv_dt_bias, L2_conv_A_log, L2_conv_D, L2_conv_rms_w, L2_conv_W_out)
    t = _to_tokens(x)
    t = t + _L2_ffn_ref(_ln_t(t), L2_ffn_Wg, L2_ffn_bg, L2_ffn_W1, L2_ffn_b1, L2_ffn_W2, L2_ffn_b2)
    x = _from_tokens(t, x)
    x = x + _L3_conv_ref(_ln_c(x), L3_conv_w_reduce, L3_conv_w_span, L3_conv_gamma, L3_conv_beta)
    t = _to_tokens(x)
    t = t + _L3_ffn_ref(_ln_t(t), L3_ffn_Wr, L3_ffn_br, L3_ffn_ln_g, L3_ffn_ln_b, L3_ffn_W1, L3_ffn_b1, L3_ffn_W2, L3_ffn_b2)
    x = _from_tokens(t, x)
    return x

_drawn_inputs = setup_inputs


def setup_inputs(seed=0):
    import zlib

    import numpy as np

    out = dict(_drawn_inputs(seed))
    spreads = {'L0_ffn_bg': (0.0, 0.1),
     'L0_ffn_b1': (0.0, 0.1),
     'L0_ffn_b2': (0.0, 0.1),
     'L1_ffn_gate_b': (0.0, 0.8),
     'L1_ffn_b1': (0.0, 0.8),
     'L1_ffn_b2': (0.0, 0.69),
     'L2_conv_ln_w': (1.0, 0.2),
     'L2_conv_ln_b': (0.0, 0.1),
     'L2_conv_proj_b': (0.0, 0.1),
     'L2_conv_conv_b': (0.0, 0.1),
     'L2_conv_rms_w': (1.0, 0.2),
     'L2_ffn_bg': (0.0, 0.36),
     'L2_ffn_b1': (0.0, 0.8),
     'L2_ffn_b2': (0.0, 0.307),
     'L3_conv_gamma': (1.0, 0.2),
     'L3_conv_beta': (0.0, 0.1),
     'L3_ffn_br': (0.0, 0.335),
     'L3_ffn_ln_g': (1.0, 0.6),
     'L3_ffn_ln_b': (0.0, 0.8),
     'L3_ffn_b1': (0.0, 0.8),
     'L3_ffn_b2': (0.0, 0.68)}
    factors = {'L1_ffn_gate_w': 5.454,
     'L1_ffn_W1': 8.0,
     'L1_ffn_W2': 8.0,
     'L2_ffn_W1': 7.363,
     'L2_ffn_W2': 6.369}
    for name, (base, spread) in spreads.items():
        noise = np.random.default_rng([zlib.crc32(name.encode()), seed]).standard_normal(out[name].shape)
        drawn = base * np.exp(spread * noise) if base else spread * noise
        out[name] = jnp.asarray(drawn.astype(out[name].dtype))
    for name, factor in factors.items():
        out[name] = (out[name] * factor).astype(out[name].dtype)
    return out
```

```python
from contextlib import ExitStack

import numpy as np
import concourse.bass as bass
from concourse import mybir

FP32 = mybir.dt.float32
BF16 = mybir.dt.bfloat16
ALU = mybir.AluOpType
ACT = mybir.ActivationFunctionType
AX = mybir.AxisListType

B, C, S = 8, 64, 1024
R = 2
P = R * C
Q = B // R
T = 512
NT = Q * S // T
E = 8
TOK = 128
NG = Q * S // TOK
JS = S // TOK
PARTS = 3
GW = PARTS * R * E
SPLIT, DM, DIN, DST, NH, HD = 8, 8, 16, 16, 2, 8
TAPS = 3
WIN3 = 9
IMG = 32
PAD = IMG + 2
LN_EXP = "natural_log_exp_and_others"
CREDIT = 2
HIDDEN = {"L0": 2, "L1": 1, "L2": 2, "L3": 2}


def columns():
    sizes = [("ident", P), ("center", P), ("mean64", P), ("ones64", P), ("mean16", P),
             ("pairs", P), ("heads", P), ("rank", E), ("eps5", 1), ("eps6", 1), ("ones", P),
             ("l0_wkT", 256), ("l0_wvT", 256), ("l0_wq", 128), ("l0_woT", 128), ("l0_bo", 1),
             ("l1_wT", C), ("l1_b", C)]
    for name, blocks in HIDDEN.items():
        sizes += [(name + "_wg", R * E), (name + "_bg", E), (name + "_w1", E * blocks * 128),
                  (name + "_w2", E * blocks * C), (name + "_b1", E * blocks), (name + "_b2", E)]
    sizes += [("m_lnw", 1), ("m_lnb", 1), ("m_win", 4 * P), ("m_cw", TAPS * 3),
              ("m_cb", 3), ("m_wdt", Q * P), ("m_dtb", 1), ("m_alog", 1), ("m_d", 1),
              ("m_rms", 1), ("m_wout", C), ("m_skip", 1), ("m_proj", P), ("m_projb", 1),
              ("i_wr", P), ("i_ws", WIN3 * P), ("i_gamma", 1), ("i_beta", 1),
              ("l3_g", E), ("l3_b", E)]
    at, out = 0, {}
    for name, n in sizes:
        out[name] = (at, n)
        at += n
    return out, at


COLS, NCOLS = columns()


class Count:

    def __init__(self, sem):
        self.sem, self.base = sem, 0

    def at(self, n):
        return n + self.base


class Chain:

    def __init__(self, eng, count, start=0):
        self.eng, self.count, self.start, self.n = eng, count, start, 0

    def step(self, ins):
        self.n += 1
        ins.then_inc(self.count.sem, 1)
        self.eng.wait_ge(self.count.sem, self.count.at(self.start + self.n))


def build(nc, x_dram, w_dram, sel_dram, out_dram, stages):
    ctx = ExitStack()
    with ctx:
        def sb(name, shape, dt=FP32):
            return ctx.enter_context(nc.sbuf_tensor(name, shape, dt))

        counts = []

        def count(name):
            counts.append(Count(ctx.enter_context(nc.semaphore(name))))
            return counts[-1]

        X = sb("X", [P, Q * S])
        XN = sb("XN", [P, Q * S])
        W = sb("W", [P, NCOLS])
        SEL = sb("SEL", [P, E, P], BF16)
        IDB = sb("IDB", [P, P], BF16)
        ARENA = sb("ARENA", [P, 23600])
        ROWS = sb("ROWS", [P, 2 * S + 2 * P])
        scratch = [nc.dram_tensor(f"scratch_{k}", (B, P, S), FP32, kind="Internal").ap() for k in "zxbc"]
        ys_dram = nc.dram_tensor("scratch_y", (B, P, S), FP32, kind="Internal").ap()
        PS = ctx.enter_context(nc.psum_tensor("PS", [P, 8, T], FP32))

        def w(name, lo=0, hi=None, rows=slice(None)):
            at, n = COLS[name]
            return W[rows, at + lo:at + (n if hi is None else hi)]

        def apart(eng):
            eng.wait_ge(loaded.sem, CREDIT + 64)

        def half(r):
            return slice(r * C, (r + 1) * C)

        class Arena:

            def __init__(self):
                self.used = 0

            def take(self, *shape):
                n = int(np.prod(shape))
                ap = ARENA[:, self.used:self.used + n]
                self.used += n
                assert self.used <= 23600, self.used
                if len(shape) == 2:
                    ap = ap.rearrange("p (a b) -> p a b", b=shape[1])
                if len(shape) == 3:
                    ap = ap.rearrange("p (a b c) -> p a b c", b=shape[1], c=shape[2])
                return ap

        loaded = count("loaded")
        stored = count("stored")
        ln_centered = count("ln_centered")
        ln_squared = count("ln_squared")
        ln_varied = count("ln_varied")
        ln_log = count("ln_log")
        ln_scaled = count("ln_scaled")
        ln_inverted = count("ln_inverted")
        ln_normed = count("ln_normed")
        g_logits = count("g_logits")
        g_exp = count("g_exp")
        g_cleared = count("g_cleared")
        g_chain = count("g_chain")
        g_split = count("g_split")
        g_turned = count("g_turned")
        g_rows = count("g_rows")
        e_input = count("e_input")
        e_hidden = count("e_hidden")
        e_gelu = count("e_gelu")
        e_weight = count("e_weight")
        e_wcopy = count("e_wcopy")
        e_out = count("e_out")
        e_scaled = count("e_scaled")
        e_added = count("e_added")
        e_fold = count("e_fold")
        a_b1 = count("a_b1")
        a_b1copy = count("a_b1copy")
        a_ctx = count("a_ctx")
        a_ctxcopy = count("a_ctxcopy")
        a_done = count("a_done")
        a_exp = count("a_exp")
        a_input = count("a_input")
        a_inv = count("a_inv")
        a_k = count("a_k")
        a_maxed = count("a_maxed")
        a_mt = count("a_mt")
        a_mtcopy = count("a_mtcopy")
        a_out = count("a_out")
        a_sums = count("a_sums")
        a_turned = count("a_turned")
        a_xt = count("a_xt")
        a_xturned = count("a_xturned")
        a_pt = count("a_pt")
        a_gt = count("a_gt")
        b_chain = count("b_chain")
        b_cleared = count("b_cleared")
        b_moment = count("b_moment")
        b_reduced = count("b_reduced")
        b_total = count("b_total")
        c_bc = count("c_bc")
        c_carry = count("c_carry")
        c_dtx = count("c_dtx")
        c_kept = count("c_kept")
        c_scan = count("c_scan")
        c_stored = [count(f"c_stored{k}") for k in range(2)]
        c_sum = count("c_sum")
        c_u = count("c_u")
        c_x = [count(f"c_x{k}") for k in range(2)]
        c_ycopy = count("c_ycopy")
        c_z = count("c_z")
        f_done = count("f_done")
        f_shift = count("f_shift")
        i_added = count("i_added")
        i_done = count("i_done")
        i_input = count("i_input")
        i_kern = count("i_kern")
        i_scaled = count("i_scaled")
        m_cleared = count("m_cleared")
        m_dt = count("m_dt")
        m_input = count("m_input")
        m_proj = count("m_proj")
        m_rate = count("m_rate")
        m_silu = count("m_silu")
        m_soft = count("m_soft")
        m_stored = [count(f"m_stored{k}") for k in range(2)]
        m_taps = count("m_taps")
        m_raw = count("m_raw")
        m_conv = count("m_conv")
        o_done = count("o_done")
        o_gated = count("o_gated")
        o_input = [count(f"o_input{k}") for k in range(2)]
        o_mean = count("o_mean")
        o_normed = count("o_normed")
        o_out = count("o_out")
        o_root = count("o_root")
        o_squared = count("o_squared")
        p_done = count("p_done")
        s_chain = count("s_chain")
        o_chain = count("o_chain")
        p_out = count("p_out")
        s_done = count("s_done")
        s_input = count("s_input")
        s_mixed = count("s_mixed")
        s_norm = count("s_norm")
        s_power = count("s_power")
        s_relu = count("s_relu")
        s_root = count("s_root")
        s_sim = count("s_sim")
        s_squared = count("s_squared")
        s_t = count("s_t")
        s_tcopy = count("s_tcopy")
        s_unit = count("s_unit")

        with nc.Block() as block:
            @block.sync
            def _(sp):
                xv = x_dram.rearrange("(q r) c s -> (r c) q s", r=R)
                for r in range(R):
                    src = x_dram.rearrange("(q r) c s -> r c q s", r=R)[r]
                    sp.dma_start(X[half(r), :].rearrange("c (q s) -> c q s", q=Q), src).then_inc(loaded.sem, 16)
                sp.dma_start(W[:, :], w_dram).then_inc(loaded.sem, 16)
                sp.dma_start(SEL[:, :, :], sel_dram).then_inc(loaded.sem, 16)
                sp.wait_ge(loaded.sem, CREDIT + 64)

            @block.gpsimd
            def _(pool):
                for c in counts:
                    pool.sem_inc(c.sem, CREDIT)
        for c in counts:
            c.base = CREDIT
        loaded.base += 64

        with nc.Block() as block:
            @block.vector
            def _(dve):
                nc.vector.tensor_copy(IDB[:, :], w("ident")).then_inc(stored.sem, 1)
                dve.wait_ge(stored.sem, stored.at(1))

        def tile(buf, t):
            return buf[:, bass.ds(t * T, T)]

        def layer_norm(dst, src, eps, affine=None):
            a = Arena()
            SQ, LOG, INV, NRM = a.take(2, T), a.take(2, T), a.take(2, T), a.take(2, T)
            with nc.Block() as block:
                @block.tensor
                def _(pe):
                    with pe.Fori(0, NT // 2) as i:
                        for k in range(2):
                            pe.wait_ge(ln_normed.sem, ln_normed.at(i * 2 + (k - 1)))
                            nc.tensor.matmul(PS[:, k, :], w("center"), tile(src, i * 2 + k),
                                             start=True, stop=True).then_inc(ln_centered.sem, 1)
                        for k in range(2):
                            pe.wait_ge(ln_squared.sem, ln_squared.at(i * 2 + (k + 1)))
                            nc.tensor.matmul(PS[:, 2 + k, :], w("mean64"), SQ[:, k, :],
                                             start=True, stop=True).then_inc(ln_varied.sem, 1)

                @block.scalar
                def _(act):
                    act.preload_act_table_set(LN_EXP)
                    with act.Fori(0, NT // 2) as i:
                        for k in range(2):
                            act.wait_ge(ln_centered.sem, ln_centered.at(i * 2 + (k + 1)))
                            nc.scalar.activation(SQ[:, k, :], PS[:, k, :], ACT.Square)\
                                .then_inc(ln_squared.sem, 1)
                        for k in range(2):
                            act.wait_ge(ln_varied.sem, ln_varied.at(i * 2 + (k + 1)))
                            nc.scalar.activation(LOG[:, k, :], PS[:, 2 + k, :], ACT.Ln, bias=w(eps))\
                                .then_inc(ln_log.sem, 1)
                        for k in range(2):
                            act.wait_ge(ln_log.sem, ln_log.at(i * 2 + (k + 1)))
                            nc.scalar.activation(INV[:, k, :], LOG[:, k, :], ACT.Exp, scale=-0.5)\
                                .then_inc(ln_inverted.sem, 1)

                @block.vector
                def _(dve):
                    with dve.Fori(0, NT // 2) as i:
                        for k in range(2):
                            dve.wait_ge(ln_inverted.sem, ln_inverted.at(i * 2 + (k + 1)))
                            if affine is None:
                                nc.vector.tensor_tensor(tile(dst, i * 2 + k), PS[:, k, :], INV[:, k, :],
                                                        ALU.mult).then_inc(ln_normed.sem, 1)
                            else:
                                nc.vector.tensor_tensor(NRM[:, k, :], PS[:, k, :], INV[:, k, :],
                                                        ALU.mult).then_inc(ln_scaled.sem, 1)
                                dve.wait_ge(ln_scaled.sem, ln_scaled.at(i * 2 + (k + 1)))
                                nc.vector.tensor_scalar(tile(dst, i * 2 + k), NRM[:, k, :], w(affine[0]),
                                                        w(affine[1]), ALU.mult, ALU.add)\
                                    .then_inc(ln_normed.sem, 1)
            for c in (ln_centered, ln_squared, ln_varied, ln_log, ln_inverted, ln_normed):
                c.base += NT
            if affine:
                ln_scaled.base += NT

        WT = ROWS[:, 0:2 * S].bitcast(BF16)

        def gate(layer, over_all):
            a = Arena()
            L, M, SC, S1, S2, EX = (a.take(NG * R, E) for _ in range(6))
            M1, M2, W1, W2, D = (a.take(NG * R) for _ in range(5))
            REST = a.take(NG * R, E)
            PT = a.take(NG, GW // 2).rearrange("p a b -> p (a b)").bitcast(BF16)\
                .rearrange("p (g k r e) -> p g k r e", k=PARTS, r=R, e=E)
            PTW = PT.rearrange("p g k r e -> p g (k r e)")

            def over(m):
                return m.unsqueeze(2).to_broadcast([P, NG * R, E])

            def gr(v):
                return v.rearrange("p (g r) e -> p g r e", r=R)

            with nc.Block() as block:
                @block.tensor
                def _(pe):
                    for g in range(NG):
                        last = nc.tensor.matmul(PS[:, 0, g * R * E:(g + 1) * R * E],
                                                XN[:, g * TOK:(g + 1) * TOK], w(layer + "_wg"),
                                                start=True, stop=True)
                    last.then_inc(g_logits.sem, 1)
                    pe.wait_ge(g_split.sem, g_split.at(1))
                    for t in range(NT):
                        if t >= 2:
                            pe.wait_ge(g_rows.sem, g_rows.at(t - 1))
                        bank = PS[0:GW, 2 + t % 2, 0:T // 2].bitcast(BF16)
                        for j in range(T // TOK):
                            last = nc.tensor.transpose(bank[:, j * TOK:(j + 1) * TOK],
                                                       PTW[:, t * (T // TOK) + j, :], IDB[:, :])
                        last.then_inc(g_turned.sem, 1)

                @block.scalar
                def _(act):
                    act.preload_act_table_set(LN_EXP)
                    act.wait_ge(g_exp.sem, g_exp.at(1))
                    if over_all:
                        nc.scalar.activation(EX, EX, ACT.Exp).then_inc(g_exp.sem, 1)
                    nc.scalar.activation(D, D, ACT.Exp).then_inc(g_exp.sem, 1)
                    act.wait_ge(g_cleared.sem, g_cleared.at(1))
                    for t in range(NT):
                        act.wait_ge(g_turned.sem, g_turned.at(t + 1))
                        nc.scalar.copy(WT[0:GW, t * T:(t + 1) * T],
                                       PS[0:GW, 2 + t % 2, 0:T // 2].bitcast(BF16)).then_inc(g_rows.sem, 1)

                @block.gpsimd
                def _(pool):
                    nc.gpsimd.memset(ROWS[:, 0:2 * S], 0.0).then_inc(g_cleared.sem, 1)

                @block.vector
                def _(dve):
                    v = nc.vector
                    step = Chain(dve, g_chain).step
                    rank = w("rank").unsqueeze(1).to_broadcast([P, NG * R, E])
                    dve.wait_ge(g_logits.sem, g_logits.at(1))
                    step(v.tensor_tensor(L, PS[:, 0, :].rearrange("p (a e) -> p a e", e=E),
                                         w(layer + "_bg").unsqueeze(1).to_broadcast([P, NG * R, E]), ALU.add))
                    for src, m, sel in ((L, M1, S1), (M, M2, S2)):
                        step(v.tensor_reduce(m, src, AX.X, ALU.max))
                        step(v.tensor_tensor(SC, src, over(m), ALU.is_equal))
                        step(v.tensor_tensor(SC, SC, rank, ALU.mult))
                        step(v.tensor_reduce(W1, SC, AX.X, ALU.max))
                        step(v.tensor_tensor(sel, SC, over(W1), ALU.is_equal))
                        if sel is S1:
                            step(v.scalar_tensor_tensor(M, S1, -3.0e38, L, ALU.mult, ALU.add))
                    step(v.tensor_tensor(D, M2, M1, ALU.subtract))
                    if over_all:
                        step(v.tensor_tensor(EX, L, over(M1), ALU.subtract))
                    v.tensor_copy(W2, M1).then_inc(g_exp.sem, 1)
                    dve.wait_ge(g_exp.sem, g_exp.at(3 if over_all else 2))
                    if over_all:
                        step(v.tensor_reduce(M1, EX, AX.X, ALU.add))
                    else:
                        step(v.tensor_scalar(M1, D, 1.0, None, ALU.add))
                    step(v.reciprocal(W1, M1))
                    step(v.tensor_tensor(W2, D, W1, ALU.mult))
                    step(v.tensor_tensor(S1, S1, over(W1), ALU.mult))
                    step(v.tensor_tensor(S2, S2, over(W2), ALU.mult))
                    step(v.tensor_tensor(L, S1, S2, ALU.add))
                    rest = L
                    for k in range(PARTS):
                        step(v.tensor_copy(PT[:, :, k, :, :], gr(rest)))
                        if k < PARTS - 1:
                            step(v.tensor_tensor(gr(REST), gr(rest), PT[:, :, k, :, :], ALU.subtract))
                            rest = REST
                    v.tensor_copy(M2, M1).then_inc(g_split.sem, 1)
                    gate.steps = 1 + 5 + 1 + 5 + 1 + (2 if over_all else 1) + 5 + 5
            g_logits.base += 1
            g_exp.base += 3 if over_all else 2
            g_chain.base += gate.steps
            g_split.base += 1
            g_cleared.base += 1
            g_turned.base += NT
            g_rows.base += NT

        def experts(layer):
            blocks = HIDDEN[layer]
            NB = E * blocks
            a = Arena()
            XS, H = a.take(2, T), a.take(2, R * T)
            WB, TMP, SUM = a.take(2, T), a.take(2, T), a.take(2, T)
            with nc.Block() as block:
                @block.sync
                def _(sp):
                    with sp.Fori(0, NT // 2) as i:
                        for k in range(2):
                            sp.wait_ge(e_hidden.sem, e_hidden.at((i * 2 + k) * NB))
                            sp.dma_start(XS[:, k, :], tile(XN, i * 2 + k)).then_inc(e_input.sem, 16)

                @block.tensor
                def _(pe):
                    with pe.Fori(0, NT // 2) as i:
                        for k in range(2):
                            t = i * 2 + k
                            pe.wait_ge(e_input.sem, e_input.at((t + 1) * 16))

                            def up(b):
                                pe.wait_ge(e_gelu.sem, e_gelu.at(t * NB + (b - 1)))
                                for r in range(R):
                                    last = nc.tensor.matmul(
                                        PS[:, (b % 2) * R + r, :], w(layer + "_w1", b * 128, (b + 1) * 128, half(r)),
                                        XS[half(r), k, :], start=True, stop=True)
                                last.then_inc(e_hidden.sem, 1)

                            def down(b):
                                e, part = divmod(b, blocks)
                                if part == 0:
                                    pe.wait_ge(e_wcopy.sem, e_wcopy.at(t * E + e))
                                    nc.tensor.matmul(PS[:, 6, :], SEL[:, e, :], WT[:, bass.ds(t * T, T)],
                                                     start=True, stop=True).then_inc(e_weight.sem, 1)
                                    pe.wait_ge(e_scaled.sem, e_scaled.at(t * E + (e - 1)))
                                pe.wait_ge(e_gelu.sem, e_gelu.at(t * NB + (b + 1)))
                                for r in range(R):
                                    last = nc.tensor.matmul(
                                        PS[half(r), 4 + e % 2, :], w(layer + "_w2", b * C, (b + 1) * C),
                                        H[:, b % 2, r * T:(r + 1) * T], start=part == 0, stop=part == blocks - 1)
                                if part == blocks - 1:
                                    last.then_inc(e_out.sem, 1)

                            up(0)
                            for b in range(1, NB):
                                up(b)
                                down(b - 1)
                            down(NB - 1)

                @block.scalar
                def _(act):
                    with act.Fori(0, NT // 2) as i:
                        for k in range(2):
                            t = i * 2 + k
                            for b in range(NB):
                                act.wait_ge(e_hidden.sem, e_hidden.at(t * NB + (b + 1)))
                                nc.scalar.activation(
                                    H[:, b % 2, :], PS[:, (b % 2) * R:(b % 2) * R + R, :].rearrange("p a b -> p (a b)"),
                                    ACT.Gelu, bias=w(layer + "_b1", b, b + 1)).then_inc(e_gelu.sem, 1)

                @block.vector
                def _(dve):
                    with dve.Fori(0, NT // 2) as i:
                        for k in range(2):
                            t = i * 2 + k
                            for e in range(E):
                                dve.wait_ge(e_weight.sem, e_weight.at(t * E + (e + 1)))
                                nc.vector.tensor_copy(WB[:, e % 2, :], PS[:, 6, :]).then_inc(e_wcopy.sem, 1)
                                dve.wait_ge(e_wcopy.sem, e_wcopy.at(t * E + (e + 1)))
                                dve.wait_ge(e_out.sem, e_out.at(t * E + (e + 1)))
                                if e:
                                    dve.wait_ge(e_added.sem, e_added.at(t * (E - 1) + max(e - 2, 0)))
                                nc.vector.scalar_tensor_tensor(
                                    TMP[:, e % 2, :] if e else SUM[:, k, :], PS[:, 4 + e % 2, :],
                                    w(layer + "_b2", e, e + 1), WB[:, e % 2, :],
                                    ALU.add, ALU.mult).then_inc(e_scaled.sem, 1)
                            dve.wait_ge(e_added.sem, e_added.at((t + 1) * (E - 1)))
                            nc.vector.tensor_tensor(tile(X, t), tile(X, t), SUM[:, k, :], ALU.add)\
                                .then_inc(e_fold.sem, 1)

                @block.gpsimd
                def _(pool):
                    with pool.Fori(0, NT // 2) as i:
                        for k in range(2):
                            t = i * 2 + k
                            for e in range(1, E):
                                pool.wait_ge(e_scaled.sem, e_scaled.at(t * E + (e + 1)))
                                if e > 1:
                                    pool.wait_ge(e_added.sem, e_added.at(t * (E - 1) + (e - 1)))
                                nc.gpsimd.tensor_tensor(SUM[:, k, :], SUM[:, k, :], TMP[:, e % 2, :], ALU.add)\
                                    .then_inc(e_added.sem, 1)
            e_input.base += NT * 16
            e_hidden.base += NT * NB
            e_gelu.base += NT * NB
            for c in (e_weight, e_wcopy, e_out, e_scaled):
                c.base += NT * E
            e_added.base += NT * (E - 1)
            e_fold.base += NT

        def linear_attention():
            a = Arena()
            XS, PC, PT, XT = a.take(S), a.take(2, S), a.take(R, JS, 2 * P), a.take(JS, R, C)
            NM, SUM, GT, CT = a.take(2 * R), a.take(2 * R), a.take(2 * P), a.take(2 * R, P)
            B1S, MT = a.take(2 * R, C), a.take(C)
            NU = 2 * R

            def wide(bank, n=2):
                return PS[:, bank:bank + n, :].rearrange("p a b -> p (a b)")

            with nc.Block() as block:
                @block.sync
                def _(sp):
                    with sp.Fori(0, Q) as q:
                        sp.wait_ge(a_out.sem, a_out.at(q * 2))
                        sp.dma_start(XS, XN[:, bass.ds(q * S, S)]).then_inc(a_input.sem, 16)

                @block.tensor
                def _(pe):
                    mm = nc.tensor.matmul
                    with pe.Fori(0, Q) as q:
                        def k_of(u):
                            r, b = divmod(u, 2)
                            pe.wait_ge(a_exp.sem, a_exp.at(q * NU + max(u - 1, 0)))
                            for h in range(2):
                                last = mm(PS[:, 2 * (u % 2) + h, :], w("l0_wkT", b * P, (b + 1) * P, half(r)),
                                          XS[half(r), h * T:(h + 1) * T], start=True, stop=True)
                            last.then_inc(a_k.sem, 1)

                        def turn(u):
                            pe.wait_ge(a_exp.sem, a_exp.at(q * NU + (u + 1)))
                            pe.wait_ge(a_pt.sem, a_pt.at(q * NU + u))
                            for j in range(JS):
                                last = nc.tensor.transpose(PS[:, 4 + j // 4, (j % 4) * TOK:(j % 4 + 1) * TOK],
                                                           PC[:, u % 2, j * TOK:(j + 1) * TOK], w("ident"))
                            last.then_inc(a_turned.sem, 1)

                        pe.wait_ge(a_input.sem, a_input.at((q + 1) * 16))
                        pe.wait_ge(a_done.sem, a_done.at(q * 2))
                        k_of(0)
                        k_of(1)
                        for j in range(JS):
                            last = nc.tensor.transpose(PS[:, 6 + j // 4, (j % 4) * TOK:(j % 4 + 1) * TOK],
                                                       XS[:, j * TOK:(j + 1) * TOK], w("ident"))
                        last.then_inc(a_xturned.sem, 1)
                        turn(0)
                        k_of(2)
                        turn(1)
                        k_of(3)
                        turn(2)
                        turn(3)
                        pe.wait_ge(a_xt.sem, a_xt.at(q + 1))
                        pe.wait_ge(a_pt.sem, a_pt.at((q + 1) * NU))
                        for j in range(JS):
                            for r in range(R):
                                last = mm(PS[half(r), 6, 0:2 * P], XT[:, j, r, :], PT[:, r, j, :],
                                          start=j == 0, stop=j == JS - 1)
                        last.then_inc(a_sums.sem, 1)
                        pe.wait_ge(a_gt.sem, a_gt.at(q + 1))
                        for r in range(R):
                            for b in range(2):
                                u = r * 2 + b
                                last = mm(PS[:, 7 - 2 * r, b * P:(b + 1) * P], w("l0_wvT", b * P, (b + 1) * P, half(r)),
                                          GT[half(r), b * P:(b + 1) * P], start=True, stop=True)
                        last.then_inc(a_ctx.sem, 1)
                        pe.wait_ge(a_ctxcopy.sem, a_ctxcopy.at((q + 1) * R))
                        for u in range(NU):
                            last = mm(PS[:, 6, u * C:(u + 1) * C], CT[:, u, :],
                                      w("l0_woT", (u % 2) * C, (u % 2 + 1) * C), start=True, stop=True)
                        last.then_inc(a_b1.sem, 1)
                        pe.wait_ge(a_b1copy.sem, a_b1copy.at(q + 1))
                        for b in range(2):
                            for r in range(R):
                                last = mm(PS[half(r), 7, 0:C], w("l0_wq", b * C, (b + 1) * C), B1S[:, r * 2 + b, :],
                                          start=b == 0, stop=b == 1)
                        last.then_inc(a_mt.sem, 1)
                        apart(pe)
                        pe.wait_ge(a_mtcopy.sem, a_mtcopy.at(q + 1))
                        for h in range(2):
                            for r in range(R):
                                last = mm(PS[half(r), 4 + h, :], MT[half(r), :], XS[half(r), h * T:(h + 1) * T],
                                          start=True, stop=True)
                            last.then_inc(a_out.sem, 1)

                @block.scalar
                def _(act):
                    act.preload_act_table_set(LN_EXP)
                    with act.Fori(0, Q) as q:
                        for u in range(NU):
                            act.wait_ge(a_maxed.sem, a_maxed.at(q * NU + (u + 1)))
                            act.wait_ge(a_turned.sem, a_turned.at(q * NU + max(u - 1, 0)))
                            if u == 0:
                                act.wait_ge(a_b1copy.sem, a_b1copy.at(q))
                            nc.scalar.activation(PC[:, u % 2, :], wide(2 * (u % 2)), ACT.Exp,
                                                 bias=NM[:, u:u + 1], accum_out=SUM[:, u:u + 1])\
                                .then_inc(a_exp.sem, 1)
                            if u == 1:
                                act.wait_ge(a_xturned.sem, a_xturned.at(q + 1))
                                nc.scalar.copy(XT, wide(6).rearrange("p (j r c) -> p j r c", r=R, c=C))\
                                    .then_inc(a_xt.sem, 1)

                @block.vector
                def _(dve):
                    v = nc.vector
                    with dve.Fori(0, Q) as q:
                        def maximum(u):
                            dve.wait_ge(a_k.sem, a_k.at(q * NU + (u + 1)))
                            v.tensor_reduce(NM[:, u:u + 1], wide(2 * (u % 2)), AX.X, ALU.max, negate=True)\
                                .then_inc(a_maxed.sem, 1)

                        def keep(u):
                            r, b = divmod(u, 2)
                            dve.wait_ge(a_turned.sem, a_turned.at(q * NU + (u + 1)))
                            v.tensor_copy(PT[:, r, :, b * P:(b + 1) * P],
                                          wide(4).rearrange("p (j d) -> p j d", d=P)).then_inc(a_pt.sem, 1)

                        maximum(0)
                        maximum(1)
                        for u in range(NU):
                            keep(u)
                            if u + 2 < NU:
                                maximum(u + 2)
                        dve.wait_ge(a_exp.sem, a_exp.at((q + 1) * NU))
                        v.reciprocal(SUM, SUM).then_inc(a_inv.sem, 1)
                        dve.wait_ge(a_sums.sem, a_sums.at(q + 1))
                        v.tensor_copy(GT, PS[:, 6, 0:2 * P]).then_inc(a_gt.sem, 1)
                        dve.wait_ge(a_ctx.sem, a_ctx.at(q + 1))
                        for r in range(R):
                            v.tensor_tensor(CT[:, 2 * r:2 * r + 2, :],
                                            PS[:, 7 - 2 * r, 0:2 * P].rearrange("p (b d) -> p b d", b=2),
                                            w("heads").unsqueeze(1).to_broadcast([P, 2, P]), ALU.mult)\
                                .then_inc(a_ctxcopy.sem, 1)
                        dve.wait_ge(a_b1.sem, a_b1.at(q + 1))
                        dve.wait_ge(a_inv.sem, a_inv.at(q + 1))
                        v.tensor_tensor(B1S, PS[:, 6, 0:NU * C].rearrange("p (b c) -> p b c", b=NU),
                                        SUM.unsqueeze(2).to_broadcast([P, NU, C]), ALU.mult)\
                            .then_inc(a_b1copy.sem, 1)
                        dve.wait_ge(a_mt.sem, a_mt.at(q + 1))
                        v.tensor_copy(MT, PS[:, 7, 0:C]).then_inc(a_mtcopy.sem, 1)
                        for h in range(2):
                            dve.wait_ge(a_out.sem, a_out.at(q * 2 + (h + 1)))
                            xt = X[:, bass.ds(q * S + h * T, T)]
                            v.scalar_tensor_tensor(xt, PS[:, 4 + h, :], w("l0_bo"), xt, ALU.add, ALU.add)\
                                .then_inc(a_done.sem, 1)

        def similarity():
            a = Arena()
            XS, SQ, RN, XH = a.take(S), a.take(S), a.take(S), a.take(S)
            TT, RL, R2 = a.take(R, JS, C), a.take(R, S), a.take(R, S)
            with nc.Block() as block:
                @block.sync
                def _(sp):
                    with sp.Fori(0, Q) as q:
                        sp.wait_ge(s_mixed.sem, s_mixed.at(q * (JS * R)))
                        sp.dma_start(XS, XN[:, bass.ds(q * S, S)]).then_inc(s_input.sem, 16)

                @block.tensor
                def _(pe):
                    mm = nc.tensor.matmul
                    with pe.Fori(0, Q) as q:
                        pe.wait_ge(s_input.sem, s_input.at((q + 1) * 16))
                        pe.wait_ge(s_done.sem, s_done.at(q * 2))
                        for r in range(R):
                            for m in range(JS):
                                last = mm(PS[:, 4 + r, m * C:(m + 1) * C], XS[half(r), m * TOK:(m + 1) * TOK],
                                          w("l1_wT", rows=half(r)), start=True, stop=True)
                        last.then_inc(s_t.sem, 1)
                        pe.wait_ge(s_squared.sem, s_squared.at(q + 1))
                        for h in range(2):
                            last = mm(PS[:, 6 + h, :], w("ones64"), SQ[:, h * T:(h + 1) * T], start=True, stop=True)
                        last.then_inc(s_norm.sem, 1)
                        pe.wait_ge(s_unit.sem, s_unit.at(q + 1))

                        def similar(m):
                            for r in range(R):
                                pe.wait_ge(s_relu.sem, s_relu.at(q * (JS * R) + max(m * R + r - 1, 0)))
                                for h in range(2):
                                    last = mm(PS[:, 2 * r + h, :], XH[half(r), m * TOK:(m + 1) * TOK],
                                              XH[half(r), h * T:(h + 1) * T], start=True, stop=True)
                                last.then_inc(s_sim.sem, 1)

                        def mix(m):
                            if m == 0:
                                pe.wait_ge(s_tcopy.sem, s_tcopy.at((q + 1) * R))
                            for r in range(R):
                                pe.wait_ge(s_power.sem, s_power.at(q * (JS * R) + (m * R + r + 1)))
                                for h in range(2):
                                    last = mm(PS[half(r), 6 + h, :], TT[:, r, m, :], R2[:, r, h * T:(h + 1) * T],
                                              start=m == 0, stop=m == JS - 1)
                                last.then_inc(s_mixed.sem, 1)

                        similar(0)
                        for m in range(1, JS):
                            similar(m)
                            mix(m - 1)
                        mix(JS - 1)

                @block.scalar
                def _(act):
                    act.preload_act_table_set(LN_EXP)
                    with act.Fori(0, Q) as q:
                        act.wait_ge(s_input.sem, s_input.at((q + 1) * 16))
                        nc.scalar.activation(SQ, XS, ACT.Square).then_inc(s_squared.sem, 1)
                        step = Chain(act, s_root, q * 2).step
                        act.wait_ge(s_chain.sem, s_chain.at(q + 1))
                        step(nc.scalar.activation(SQ, RN, ACT.Ln, scale=1.0 / C))
                        step(nc.scalar.activation(SQ, SQ, ACT.Exp, scale=-0.5))
                        for m in range(JS):
                            for r in range(R):
                                act.wait_ge(s_sim.sem, s_sim.at(q * (JS * R) + (m * R + r + 1)))
                                act.wait_ge(s_power.sem, s_power.at(q * (JS * R) + max(m * R + r - 1, 0)))
                                nc.scalar.activation(RL[:, r, :],
                                                     PS[:, 2 * r:2 * r + 2, :].rearrange("p a b -> p (a b)"),
                                                     ACT.Relu).then_inc(s_relu.sem, 1)

                @block.vector
                def _(dve):
                    v = nc.vector
                    with dve.Fori(0, Q) as q:
                        dve.wait_ge(s_t.sem, s_t.at(q + 1))
                        for r in range(R):
                            v.tensor_tensor(TT[:, r, :, :], PS[:, 4 + r, :].rearrange("p (m c) -> p m c", c=C),
                                            w("l1_b").unsqueeze(1).to_broadcast([P, JS, C]), ALU.add)\
                                .then_inc(s_tcopy.sem, 1)
                        dve.wait_ge(s_norm.sem, s_norm.at(q + 1))
                        v.tensor_scalar(RN, PS[:, 6:8, :].rearrange("p a b -> p (a b)"), 1e-16, None, ALU.max)\
                            .then_inc(s_chain.sem, 1)
                        dve.wait_ge(s_root.sem, s_root.at((q + 1) * 2))
                        v.scalar_tensor_tensor(XH, XS, C ** -0.5, SQ, ALU.mult, ALU.mult).then_inc(s_unit.sem, 1)
                        for m in range(JS):
                            for r in range(R):
                                dve.wait_ge(s_relu.sem, s_relu.at(q * (JS * R) + (m * R + r + 1)))
                                if m:
                                    dve.wait_ge(s_mixed.sem, s_mixed.at(q * (JS * R) + (m * R + r - 1)))
                                v.tensor_tensor(R2[:, r, :], RL[:, r, :], RL[:, r, :], ALU.mult)\
                                    .then_inc(s_power.sem, 1)
                        dve.wait_ge(s_mixed.sem, s_mixed.at((q + 1) * (JS * R)))
                        for h in range(2):
                            xt = X[:, bass.ds(q * S + h * T, T)]
                            v.tensor_tensor(xt, PS[:, 6 + h, :], xt, ALU.add).then_inc(s_done.sem, 1)

        TM = T

        def mamba_project():
            a = Arena()
            XS, RAW, ACC, OUT = a.take(S), a.take(2, S + TAPS - 1), a.take(2, S), a.take(2, S)
            ABS, EXPA, LN1, POS, A = a.take(S), a.take(S), a.take(S), a.take(S), a.take(1)
            DT, DEC = ROWS[:, 0:S], ROWS[:, S:2 * S]
            UNITS = [(r, k) for r in range(R) for k in (1, 2, 3, 0)]
            NU, NC = len(UNITS), R * 3
            with nc.Block() as block:
                @block.sync
                def _(sp):
                    with sp.Fori(0, Q) as q:
                        sp.wait_ge(m_proj.sem, m_proj.at(q * NU))
                        sp.dma_start(XS, XN[:, bass.ds(q * S, S)]).then_inc(m_input.sem, 16)
                        for u, (r, k) in enumerate(UNITS):
                            sp.wait_ge(m_silu.sem, m_silu.at(q * NU + (u + 1)))
                            sp.dma_start(scratch[k][bass.ds(q * R + r, 1), :, :].rearrange("a p s -> (a p) s"),
                                         OUT[:, u % 2, :]).then_inc(m_stored[u % 2].sem, 16)
                    for k in range(2):
                        sp.wait_ge(m_stored[k].sem, m_stored[k].at(Q * NU // 2 * 16))

                @block.gpsimd
                def _(pool):
                    nc.gpsimd.memset(RAW[:, :, 0:TAPS - 1], 0.0).then_inc(m_cleared.sem, 1)

                @block.tensor
                def _(pe):
                    mm = nc.tensor.matmul
                    for q in range(Q):
                        for h in range(2):
                            last = mm(PS[:, 4 + h, :], w("m_wdt", q * P, (q + 1) * P),
                                      XN[:, q * S + h * T:q * S + (h + 1) * T], start=q == 0, stop=q == Q - 1)
                    last.then_inc(m_dt.sem, 1)
                    with pe.Fori(0, Q) as q:
                        pe.wait_ge(m_input.sem, m_input.at((q + 1) * 16))
                        for u, (r, k) in enumerate(UNITS):
                            pe.wait_ge(m_raw.sem, m_raw.at(q * NU + (u - 1)))
                            for h in range(2):
                                last = mm(PS[:, 2 * (u % 2) + h, :], w("m_win", k * P, (k + 1) * P, half(r)),
                                          XS[half(r), h * T:(h + 1) * T], start=True, stop=True)
                            last.then_inc(m_proj.sem, 1)

                @block.scalar
                def _(act):
                    f = nc.scalar.activation
                    dt_psum = PS[:, 4:6, :].rearrange("p a b -> p (a b)")
                    act.preload_act_table_set(LN_EXP)
                    act.wait_ge(m_dt.sem, m_dt.at(1))
                    step = Chain(act, m_soft).step
                    step(f(ABS, dt_psum, ACT.Abs, bias=w("m_dtb")))
                    step(f(EXPA, ABS, ACT.Exp, scale=-1.0))
                    step(f(LN1, EXPA, ACT.Ln, bias=1.0))
                    step(f(A, w("m_alog"), ACT.Exp))
                    act.wait_ge(m_rate.sem, m_rate.at(3))
                    f(DEC, DT, ACT.Exp, scale=A).then_inc(m_soft.sem, 1)
                    act.wait_ge(m_cleared.sem, m_cleared.at(1))

                    def silu(q, u):
                        r, k = UNITS[u]
                        act.wait_ge(m_stored[u % 2].sem, m_stored[u % 2].at((q * (NU // 2) + u // 2) * 16))
                        if k:
                            act.wait_ge(m_conv.sem, m_conv.at(q * NC + (r * 3 + k)))
                            f(OUT[:, u % 2, :], ACC[:, (r * 3 + k - 1) % 2, :], ACT.Silu,
                              bias=w("m_cb", k - 1, k)).then_inc(m_silu.sem, 1)
                        else:
                            act.wait_ge(m_proj.sem, m_proj.at(q * NU + (u + 1)))
                            f(OUT[:, u % 2, :], PS[:, 2 * (u % 2):2 * (u % 2) + 2, :].rearrange("p a b -> p (a b)"),
                              ACT.Silu).then_inc(m_silu.sem, 1)

                    act.preload_act_table(ACT.Silu)
                    with act.Fori(0, Q) as q:
                        for u, (r, k) in enumerate(UNITS):
                            if k:
                                n = r * 3 + k - 1
                                act.wait_ge(m_proj.sem, m_proj.at(q * NU + (u + 1)))
                                act.wait_ge(m_conv.sem, m_conv.at(q * NC + max(n - 1, 0)))
                                f(RAW[:, n % 2, TAPS - 1:], PS[:, 2 * (u % 2):2 * (u % 2) + 2, :]
                                  .rearrange("p a b -> p (a b)"), ACT.Copy).then_inc(m_raw.sem, 1)
                                if k > 1:
                                    silu(q, u - 1)
                            else:
                                silu(q, u - 1)
                                silu(q, u)
                                act.wait_ge(m_silu.sem, m_silu.at(q * NU + (u + 1)))
                                act.sem_inc(m_raw.sem, 1)

                @block.vector
                def _(dve):
                    v = nc.vector
                    dve.wait_ge(m_soft.sem, m_soft.at(1))
                    step = Chain(dve, m_rate).step
                    step(v.tensor_scalar(POS, PS[:, 4:6, :].rearrange("p a b -> p (a b)"), w("m_dtb"), 0.0,
                                         ALU.add, ALU.max))
                    dve.wait_ge(m_soft.sem, m_soft.at(4))
                    step(v.tensor_tensor(DT, POS, LN1, ALU.add))
                    step(v.tensor_scalar(A, A, -1.0, None, ALU.mult))
                    with dve.Fori(0, Q) as q:
                        for u, (r, k) in enumerate(UNITS):
                            if k == 0:
                                continue
                            n = r * 3 + k - 1
                            raw, acc = RAW[:, n % 2, :], ACC[:, n % 2, :]
                            dve.wait_ge(m_raw.sem, m_raw.at(q * NU + (u + 1)))
                            dve.wait_ge(m_silu.sem, m_silu.at(q * NU + max(u - 1, 0)))
                            step = Chain(dve, m_taps, (q * NC + n) * (TAPS - 1)).step
                            for tap in range(TAPS):
                                cw = w("m_cw", (k - 1) * TAPS + tap, (k - 1) * TAPS + tap + 1)
                                if tap == 0:
                                    step(v.tensor_scalar(acc, raw[:, 0:S], cw, None, ALU.mult))
                                else:
                                    ins = v.scalar_tensor_tensor(acc, raw[:, tap:tap + S], cw, acc,
                                                                 ALU.mult, ALU.add)
                                    if tap < TAPS - 1:
                                        step(ins)
                                    else:
                                        ins.then_inc(m_conv.sem, 1)

        def mamba_scan():
            a = Arena()
            BT, CT = a.take(DST, TM), a.take(DST, TM)
            XP, U, ST, Z, YS, LAST = (a.take(2, TM), a.take(3, TM), a.take(3, TM), a.take(2, TM),
                                      a.take(2, TM), a.take(2, DST))
            DXP = a.take(2, TM)
            DT, DEC, CARRY = ROWS[:, 0:S], ROWS[:, S:2 * S], ROWS[:, 2 * S:2 * S + P]
            x_rows = scratch[1].rearrange("b (g p) s -> (b g) p s", p=HD)
            y_rows = ys_dram.rearrange("b (g p) s -> (b g) p s", p=HD)
            for th in range(S // TM):
                now = slice(th * TM, (th + 1) * TM)
                with nc.Block() as block:
                    @block.sync
                    def _(sp):
                        for k, dst in ((2, BT), (3, CT)):
                            rows = scratch[k].rearrange("b (g n) s -> (b g) n s", n=DST)
                            for head in range(NH):
                                sp.dma_start(dst[head:P - 1 + head:NH], rows[:, :, now]).then_inc(c_bc.sem, 16)
                        with sp.Fori(0, HD // 2) as i:
                            for k in range(2):
                                p = i * 2 + k
                                sp.wait_ge(c_dtx.sem, c_dtx.at(p))
                                sp.dma_start(XP[:, k, :], x_rows[:, bass.ds(p, 1), now].rearrange("g a s -> g (a s)"))\
                                    .then_inc(c_x[k].sem, 16)
                            for k in range(2):
                                p = i * 2 + k
                                sp.wait_ge(c_ycopy.sem, c_ycopy.at(p + 1))
                                sp.dma_start(y_rows[:, bass.ds(p, 1), now].rearrange("g a s -> g (a s)"), YS[:, k, :])\
                                    .then_inc(c_stored[k].sem, 16)
                        for k in range(2):
                            sp.wait_ge(c_stored[k].sem, c_stored[k].at(HD // 2 * 16))

                    @block.gpsimd
                    def _(pool):
                        pool.wait_ge(c_bc.sem, c_bc.at(4 * 16))
                        with pool.Fori(0, HD // 2) as i:
                            for k in range(2):
                                p = i * 2 + k
                                pool.wait_ge(c_dtx.sem, c_dtx.at(p + 1))
                                for n in range(DST):
                                    j = k * DST + n
                                    if j < 3:
                                        pool.wait_ge(c_scan.sem, c_scan.at(i * (2 * DST)))
                                    else:
                                        pool.wait_ge(c_scan.sem, c_scan.at(i * (2 * DST) + (j - 2)))
                                    nc.gpsimd.tensor_tensor(U[:, j % 3, :], DXP[:, k, :], BT[:, n, :], ALU.mult)\
                                        .then_inc(c_u.sem, 1)

                    @block.vector
                    def _(dve):
                        v = nc.vector
                        dve.wait_ge(c_bc.sem, c_bc.at(4 * 16))
                        with dve.Fori(0, HD // 2) as i:
                            for k in range(2):
                                p = i * 2 + k
                                dve.wait_ge(c_x[k].sem, c_x[k].at((i + 1) * 16))
                                dve.wait_ge(c_u.sem, c_u.at(p * DST))
                                v.tensor_tensor(DXP[:, k, :], XP[:, k, :], DT[:, now], ALU.mult)\
                                    .then_inc(c_dtx.sem, 1)

                                def scan(n):
                                    j = k * DST + n
                                    at = i * (2 * DST) + j
                                    dve.wait_ge(c_u.sem, c_u.at(at + 1))
                                    before = i * (2 * DST) + max(j - 2, 0)
                                    dve.wait_ge(c_z.sem, c_z.at(before))
                                    if th == 0:
                                        dve.wait_ge(c_kept.sem, c_kept.at(before))
                                    first = 0.0 if th == 0 else CARRY[:, bass.ds(p * DST + n, 1)]
                                    v.tensor_tensor_scan(ST[:, j % 3, :], DEC[:, now], U[:, j % 3, :], first,
                                                         ALU.mult, ALU.add).then_inc(c_scan.sem, 1)

                                def weigh(n):
                                    j = k * DST + n
                                    dve.wait_ge(c_scan.sem, c_scan.at(i * (2 * DST) + (j + 1)))
                                    dve.wait_ge(c_sum.sem, c_sum.at(i * (2 * DST) + max(j - 1, 0)))
                                    v.tensor_tensor(Z[:, j % 2, :], ST[:, j % 3, :], CT[:, n, :], ALU.mult)\
                                        .then_inc(c_z.sem, 1)

                                scan(0)
                                for n in range(1, DST):
                                    scan(n)
                                    weigh(n - 1)
                                weigh(DST - 1)
                                if th == 0:
                                    dve.wait_ge(c_kept.sem, c_kept.at((p + 1) * DST))
                                    v.tensor_scalar(CARRY[:, bass.ds(p * DST, DST)], LAST[:, k, :], 1.0, None,
                                                    ALU.mult).then_inc(c_carry.sem, 1)
                                    dve.wait_ge(c_carry.sem, c_carry.at(p + 1))

                    @block.tensor
                    def _(pe):
                        with pe.Fori(0, HD // 2) as i:
                            for k in range(2):
                                p = i * 2 + k
                                pe.wait_ge(c_ycopy.sem, c_ycopy.at(p))
                                for n in range(DST):
                                    j = k * DST + n
                                    pe.wait_ge(c_z.sem, c_z.at(i * (2 * DST) + (j + 1)))
                                    nc.tensor.matmul(PS[:, k, :], w("ident"), Z[:, j % 2, :], start=n == 0,
                                                     stop=n == DST - 1).then_inc(c_sum.sem, 1)

                    @block.scalar
                    def _(act):
                        with act.Fori(0, HD // 2) as i:
                            for k in range(2):
                                p = i * 2 + k
                                if th == 0:
                                    for n in range(DST):
                                        j = k * DST + n
                                        act.wait_ge(c_scan.sem, c_scan.at(i * (2 * DST) + (j + 1)))
                                        nc.scalar.copy(LAST[:, k, n:n + 1], ST[:, j % 3, TM - 1:TM])\
                                            .then_inc(c_kept.sem, 1)
                                act.wait_ge(c_sum.sem, c_sum.at((p + 1) * DST))
                                act.wait_ge(c_stored[k].sem, c_stored[k].at(i * 16))
                                nc.scalar.copy(YS[:, k, :], PS[:, k, :]).then_inc(c_ycopy.sem, 1)
                c_bc.base += 4 * 16
                c_dtx.base += HD
                for c in c_x + c_stored:
                    c.base += HD // 2 * 16
                c_ycopy.base += HD
                for c in (c_u, c_scan, c_z, c_sum):
                    c.base += HD * DST
                if th == 0:
                    c_kept.base += HD * DST
                    c_carry.base += HD

        def mamba_gate():
            a = Arena()
            YL, XL, ZL, G, SQ, ROOT, YN = (a.take(R, S) for _ in range(7))
            WO = a.take(C)
            with nc.Block() as block:
                @block.sync
                def _(sp):
                    with sp.Fori(0, Q) as q:
                        for r in range(R):
                            sp.wait_ge(o_gated.sem, o_gated.at(q * R + r))
                            for src, dst in ((ys_dram, YL), (scratch[1], XL), (scratch[0], ZL)):
                                sp.dma_start(dst[:, r, :], src[bass.ds(q * R + r, 1), :, :]
                                             .rearrange("a p s -> (a p) s")).then_inc(o_input[r].sem, 16)

                @block.tensor
                def _(pe):
                    mm = nc.tensor.matmul
                    with pe.Fori(0, Q) as q:
                        for r in range(R):
                            n = q * R + r
                            pe.wait_ge(o_squared.sem, o_squared.at(n + 1))
                            for h in range(2):
                                last = mm(PS[:, 2 * r + h, :], w("mean16"), SQ[:, r, h * T:(h + 1) * T],
                                          start=True, stop=True)
                            last.then_inc(o_mean.sem, 1)
                        pe.wait_ge(o_done.sem, o_done.at(q * 2 + 1))
                        for r in range(R):
                            n = q * R + r
                            pe.wait_ge(o_normed.sem, o_normed.at(n + 1))
                            for h in range(2):
                                last = mm(PS[half(r), 4 + h, :], WO, YN[:, r, h * T:(h + 1) * T],
                                          start=True, stop=True)
                            last.then_inc(o_out.sem, 1)

                @block.scalar
                def _(act):
                    act.preload_act_table_set(LN_EXP)
                    with act.Fori(0, Q) as q:
                        for r in range(R):
                            n = q * R + r
                            act.wait_ge(o_gated.sem, o_gated.at(n + 1))
                            nc.scalar.activation(SQ[:, r, :], G[:, r, :], ACT.Square).then_inc(o_squared.sem, 1)
                            act.wait_ge(o_mean.sem, o_mean.at(n + 1))
                            step = Chain(act, o_root, n * 2).step
                            step(nc.scalar.activation(ROOT[:, r, :],
                                                      PS[:, 2 * r:2 * r + 2, :].rearrange("p a b -> p (a b)"),
                                                      ACT.Ln, bias=w("eps5")))
                            step(nc.scalar.activation(ROOT[:, r, :], ROOT[:, r, :], ACT.Exp, scale=-0.5))

                @block.vector
                def _(dve):
                    v = nc.vector
                    v.tensor_scalar(WO, w("m_wout"), w("m_rms"), None, ALU.mult).then_inc(o_done.sem, 1)
                    with dve.Fori(0, Q) as q:
                        for r in range(R):
                            n = q * R + r
                            dve.wait_ge(o_input[r].sem, o_input[r].at((q + 1) * 48))
                            step = Chain(dve, o_chain, n).step
                            step(v.scalar_tensor_tensor(G[:, r, :], XL[:, r, :], w("m_d"), YL[:, r, :],
                                                        ALU.mult, ALU.add))
                            v.tensor_tensor(G[:, r, :], G[:, r, :], ZL[:, r, :], ALU.mult).then_inc(o_gated.sem, 1)
                            dve.wait_ge(o_gated.sem, o_gated.at(n + 1))
                            dve.wait_ge(o_root.sem, o_root.at((n + 1) * 2))
                            dve.wait_ge(o_out.sem, o_out.at(q * R))
                            v.tensor_tensor(YN[:, r, :], G[:, r, :], ROOT[:, r, :], ALU.mult)\
                                .then_inc(o_normed.sem, 1)
                        dve.wait_ge(o_out.sem, o_out.at((q + 1) * R))
                        for h in range(2):
                            xt = XN[:, bass.ds(q * S + h * T, T)]
                            v.scalar_tensor_tensor(xt, xt, w("m_skip"), PS[:, 4 + h, :], ALU.mult, ALU.add)\
                                .then_inc(o_done.sem, 1)

        def mamba_output():
            with nc.Block() as block:
                @block.tensor
                def _(pe):
                    with pe.Fori(0, NT // 2) as i:
                        for k in range(2):
                            t = i * 2 + k
                            pe.wait_ge(p_done.sem, p_done.at(t))
                            nc.tensor.matmul(PS[:, k, :], w("m_proj"), tile(XN, t), start=True, stop=True)\
                                .then_inc(p_out.sem, 1)

                @block.vector
                def _(dve):
                    with dve.Fori(0, NT // 2) as i:
                        for k in range(2):
                            t = i * 2 + k
                            dve.wait_ge(p_out.sem, p_out.at(t + 1))
                            nc.vector.scalar_tensor_tensor(tile(X, t), PS[:, k, :], w("m_projb"), tile(X, t),
                                                           ALU.add, ALU.add).then_inc(p_done.sem, 1)

        def involution():
            a = Arena()
            RR, RN = a.take(Q * S), a.take(Q * S)
            XP = a.take(PAD, PAD)
            TMP, SUM = a.take(2, T), a.take(2, T)
            TOTAL, NEGM, SS, SD, SCALE, SHIFT = (a.take(1) for _ in range(6))
            ROWS_T = T // IMG
            with nc.Block() as block:
                @block.tensor
                def _(pe):
                    mm = nc.tensor.matmul
                    for t in range(NT):
                        last = mm(PS[:, t, :], w("i_wr"), XN[:, t * T:(t + 1) * T], start=True, stop=True)
                    last.then_inc(b_reduced.sem, 1)
                    for src, done in ((TOTAL, 1), (SS, 2)):
                        pe.wait_ge(b_total.sem, b_total.at(done))
                        mm(PS[:, 0, 0:1], w("pairs"), src, start=True, stop=True).then_inc(b_moment.sem, 1)

                @block.scalar
                def _(act):
                    f = nc.scalar.activation
                    act.wait_ge(b_reduced.sem, b_reduced.at(1))
                    f(RR, PS[:, :, :].rearrange("p a b -> p (a b)"), ACT.Identity, accum_out=TOTAL)\
                        .then_inc(b_total.sem, 1)
                    act.wait_ge(b_chain.sem, b_chain.at(1))
                    f(RN, RR, ACT.Square, bias=NEGM, accum_out=SS).then_inc(b_total.sem, 1)
                    act.wait_ge(b_moment.sem, b_moment.at(2))
                    f(SD, PS[:, 0, 0:1], ACT.Sqrt, bias=w("eps5")).then_inc(b_total.sem, 1)
                    act.wait_ge(b_chain.sem, b_chain.at(5))
                    f(RN, RR, ACT.Relu, bias=SHIFT, scale=SCALE).then_inc(b_total.sem, 1)

                @block.vector
                def _(dve):
                    v = nc.vector
                    step = Chain(dve, b_chain).step
                    dve.wait_ge(b_moment.sem, b_moment.at(1))
                    step(v.tensor_scalar(NEGM, PS[:, 0, 0:1], -1.0, None, ALU.mult))
                    dve.wait_ge(b_total.sem, b_total.at(3))
                    step(v.reciprocal(SD, SD))
                    step(v.tensor_tensor(SCALE, SD, w("i_gamma"), ALU.mult))
                    step(v.tensor_tensor(SHIFT, NEGM, SCALE, ALU.mult))
                    step(v.tensor_tensor(SHIFT, SHIFT, w("i_beta"), ALU.add))

                @block.gpsimd
                def _(pool):
                    nc.gpsimd.memset(XP, 0.0).then_inc(b_cleared.sem, 1)

            with nc.Block() as block:
                @block.sync
                def _(sp):
                    with sp.Fori(0, Q) as q:
                        sp.wait_ge(i_scaled.sem, i_scaled.at(q * (2 * WIN3)))
                        sp.dma_start(XP[:, 1:1 + IMG, 1:1 + IMG],
                                     XN[:, bass.ds(q * S, S)].rearrange("p (a b) -> p a b", b=IMG))\
                            .then_inc(i_input.sem, 16)

                @block.tensor
                def _(pe):
                    with pe.Fori(0, Q) as q:
                        for h in range(2):
                            for k in range(WIN3):
                                n = h * WIN3 + k
                                pe.wait_ge(i_scaled.sem, i_scaled.at(q * (2 * WIN3) + max(n - 1, 0)))
                                nc.tensor.matmul(PS[:, n % 2, :], w("i_ws", k * P, (k + 1) * P),
                                                 RN[:, bass.ds(q * S + h * T, T)], start=True, stop=True)\
                                    .then_inc(i_kern.sem, 1)

                @block.vector
                def _(dve):
                    v = nc.vector
                    with dve.Fori(0, Q) as q:
                        dve.wait_ge(i_input.sem, i_input.at((q + 1) * 16))
                        for h in range(2):
                            for k in range(WIN3):
                                n = h * WIN3 + k
                                dve.wait_ge(i_kern.sem, i_kern.at(q * (2 * WIN3) + (n + 1)))
                                dve.wait_ge(i_added.sem, i_added.at(q * (2 * (WIN3 - 1)) + h * (WIN3 - 1) + max(k - 2, 0)))
                                dy, dx = divmod(k, 3)
                                dst = TMP[:, k % 2, :] if k else SUM[:, h, :]
                                v.tensor_tensor(dst.rearrange("p (a b) -> p a b", b=IMG),
                                                XP[:, h * ROWS_T + dy:h * ROWS_T + dy + ROWS_T, dx:dx + IMG],
                                                PS[:, n % 2, :].rearrange("p (a b) -> p a b", b=IMG), ALU.mult)\
                                    .then_inc(i_scaled.sem, 1)
                            dve.wait_ge(i_added.sem, i_added.at(q * (2 * (WIN3 - 1)) + (h + 1) * (WIN3 - 1)))
                            xt = X[:, bass.ds(q * S + h * T, T)]
                            v.scalar_tensor_tensor(xt, SUM[:, h, :], 2.0, xt, ALU.mult, ALU.add)\
                                .then_inc(i_done.sem, 1)

                @block.gpsimd
                def _(pool):
                    with pool.Fori(0, Q) as q:
                        for h in range(2):
                            for k in range(1, WIN3):
                                pool.wait_ge(i_scaled.sem, i_scaled.at(q * (2 * WIN3) + h * WIN3 + (k + 1)))
                                if k > 1:
                                    pool.wait_ge(i_added.sem, i_added.at(q * (2 * (WIN3 - 1)) + h * (WIN3 - 1) + (k - 1)))
                                nc.gpsimd.tensor_tensor(SUM[:, h, :], SUM[:, h, :], TMP[:, k % 2, :], ALU.add)\
                                    .then_inc(i_added.sem, 1)

        def fold_gains():
            a = Arena()
            SHIFTED = a.take(E * 2)
            with nc.Block() as block:
                @block.tensor
                def _(pe):
                    for b in range(E * 2):
                        last = nc.tensor.matmul(PS[:, 0, b:b + 1], w("L3_w1", b * 128, (b + 1) * 128, slice(0, C)),
                                                w("l3_b", b // 2, b // 2 + 1, slice(0, C)), start=True, stop=True)
                    last.then_inc(f_shift.sem, 1)

                @block.vector
                def _(dve):
                    v = nc.vector
                    dve.wait_ge(f_shift.sem, f_shift.at(1))
                    v.tensor_tensor(w("L3_b1"), w("L3_b1"), PS[:, 0, 0:E * 2], ALU.add).then_inc(f_done.sem, 1)
                    for e in range(E):
                        v.tensor_scalar(w("L3_w1", e * 256, (e + 1) * 256), w("L3_w1", e * 256, (e + 1) * 256),
                                        w("l3_g", e, e + 1), None, ALU.mult).then_inc(f_done.sem, 1)

        for s in stages:
            if s == "ln6":
                layer_norm(XN, X, "eps6")
            elif s == "ln5":
                layer_norm(XN, X, "eps5")
            elif s.startswith("gate"):
                gate(s[4:6], over_all=s[4:6] == "L1")
            elif s.startswith("exp"):
                experts(s[3:5])
            elif s == "ln5affine":
                layer_norm(XN, XN, "eps5", ("m_lnw", "m_lnb"))
            else:
                {"L0": linear_attention, "L1": similarity, "project": mamba_project, "scan": mamba_scan,
                 "mgate": mamba_gate, "mout": mamba_output, "L3": involution, "fold": fold_gains}[s]()

        with nc.Block() as block:
            @block.sync
            def _(sp):
                src = stages and stages[-1].startswith("ln") and XN or X
                for r in range(R):
                    dst = out_dram.rearrange("(q r) c s -> r c q s", r=R)[r]
                    sp.dma_start(dst, src[half(r), :].rearrange("c (q s) -> c q s", q=Q))\
                        .then_inc(loaded.sem, 16)
                sp.wait_ge(loaded.sem, loaded.at(32))


STAGES = ["ln6","L0","ln5","gateL0","expL0","ln6","L1","ln5","gateL1","expL1","ln6","ln5affine","project","scan","mgate","ln5affine","mout","ln5","gateL2","expL2","ln6","L3","fold","ln5","gateL3","expL3"]


def packed(inputs):
    import numpy as _np
    f = {k: _np.asarray(v) for k, v in inputs.items()}
    W = _np.zeros((P, NCOLS), _np.float32)

    def put(name, a, rows=slice(None)):
        at, n = COLS[name]
        W[rows, at:at + n] = a.reshape(a.shape[0], n)

    p = _np.arange(P)
    eye = _np.eye(P, dtype=_np.float32)
    same = (p[:, None] // C == p[None, :] // C).astype(_np.float32)
    put("ident", eye)
    put("center", eye - same / C)
    put("mean64", same / C)
    put("ones64", same)
    put("mean16", (p[:, None] // DIN == p[None, :] // DIN).astype(_np.float32) / DIN)
    put("pairs", (p[:, None] % C == p[None, :] % C).astype(_np.float32) / (B * S))
    put("heads", (p[:, None] // 32 == p[None, :] // 32).astype(_np.float32))
    put("rank", _np.tile(_np.arange(E, 0, -1, dtype=_np.float32), (P, 1)))
    put("eps5", _np.full((P, 1), 1e-5, _np.float32))
    put("eps6", _np.full((P, 1), 1e-6, _np.float32))
    put("ones", _np.ones((P, P), _np.float32))

    def both(a):
        return _np.concatenate([a] * R)

    def diagonal(a, n):
        out = _np.zeros((n, a.shape[0], n, a.shape[1]), _np.float32)
        for i in range(n):
            out[i, :, i] = a
        return out.reshape(n * a.shape[0], n * a.shape[1])

    qkv = f["L0_conv_w_qkv"]
    put("l0_wkT", both(qkv[256:512].T))
    put("l0_wvT", both(qkv[512:768].T))
    put("l0_wq", qkv[0:256].reshape(2, P, C).transpose(1, 0, 2))
    put("l0_woT", f["L0_conv_w_out"].T.reshape(2, P, C).transpose(1, 0, 2))
    put("l0_bo", both(f["L0_conv_b_out"][:, None]))
    put("l1_wT", both(f["L1_conv_W"].T))
    put("l1_b", _np.tile(f["L1_conv_b"], (P, 1)))
    gates = {"L0": ("Wg", "bg"), "L1": ("gate_w", "gate_b"), "L2": ("Wg", "bg"), "L3": ("Wr", "br")}
    for name, blocks in HIDDEN.items():
        g = {k: f[f"{name}_ffn_{k}"] for k in gates[name] + ("W1", "b1", "W2", "b2")}
        put(name + "_wg", diagonal(g[gates[name][0]], R))
        put(name + "_bg", _np.tile(g[gates[name][1]], (P, 1)))
        put(name + "_w1", both(g["W1"].transpose(1, 0, 2)))
        put(name + "_b1", g["b1"].reshape(E * blocks, 128).T)
        put(name + "_w2", g["W2"].reshape(E * blocks, 128, C).transpose(1, 0, 2))
        put(name + "_b2", both(g["b2"].T))
    m = {k[8:]: v for k, v in f.items() if k.startswith("L2_conv_")}
    put("m_lnw", both(m["ln_w"][:, None]))
    put("m_lnb", both(m["ln_b"][:, None]))
    win = _np.stack([diagonal(m["W_in"][:, k * DIN:(k + 1) * DIN], SPLIT) for k in range(4)], 1)
    put("m_win", both(win))
    put("m_cw", _np.tile(m["conv_w"].reshape(3, DIN, TAPS).transpose(1, 0, 2).reshape(DIN, -1), (SPLIT, 1)))
    put("m_cb", _np.tile(m["conv_b"].reshape(3, DIN).T, (SPLIT, 1)))
    wdt = _np.zeros((R, SPLIT, DM, Q, B, SPLIT, NH), _np.float32)
    for q in range(Q):
        for r in range(R):
            for s in range(SPLIT):
                wdt[r, s, :, q, q * R + r, s] = m["W_in"][:, 4 * DIN:]
    put("m_wdt", wdt.reshape(P, Q * P))
    put("m_dtb", _np.tile(m["dt_bias"][:, None], (P // NH, 1)))
    put("m_alog", _np.tile(m["A_log"][:, None], (P // NH, 1)))
    put("m_d", _np.tile(_np.repeat(m["D"], HD)[:, None], (SPLIT, 1)))
    put("m_rms", _np.tile(m["rms_w"][:, None], (SPLIT, 1)))
    put("m_wout", diagonal(m["W_out"], SPLIT))
    put("m_skip", _np.tile(m["skip_scale"][:, None], (P, 1)))
    put("m_proj", diagonal(m["proj_w"], R))
    put("m_projb", both(m["proj_b"][:, None]))
    put("i_wr", diagonal(f["L3_conv_w_reduce"].T, R))
    put("i_ws", _np.stack([diagonal(_np.repeat(f["L3_conv_w_span"][k][:, None], C, 1), R)
                           for k in range(WIN3)], 1))
    put("i_gamma", both(f["L3_conv_gamma"][:, None]))
    put("i_beta", both(f["L3_conv_beta"][:, None]))
    put("l3_g", both(f["L3_ffn_ln_g"].T))
    put("l3_b", both(f["L3_ffn_ln_b"].T))
    return W


def selectors():
    import numpy as _np
    sel = _np.zeros((PARTS, R, E, E, R, C), _np.float32)
    for r in range(R):
        for e in range(E):
            sel[:, r, e, e, r] = 1
    return _np.concatenate([sel.reshape(GW, E, P), _np.zeros((P - GW, E, P), _np.float32)])


def kernel(**inputs):
    import numpy as _np
    import ml_dtypes as _ml
    import concourse.bacc as _bacc
    from concourse import mybir as _mybir
    from concourse.bass_utils import run_bass_kernel_spmd as _run

    nc = _bacc.Bacc("TRN2", target_bir_lowering=False, num_devices=1)
    arrays = {
        "x_dram": _np.ascontiguousarray(_np.asarray(inputs["x"]).reshape(B, C, S)),
        "w_dram": packed(inputs),
        "sel_dram": selectors().astype(_ml.bfloat16),
    }
    args = [nc.dram_tensor(n, a.shape, _mybir.dt.from_np(a.dtype), kind="ExternalInput").ap()
            for n, a in arrays.items()]
    out = nc.dram_tensor("out_dram", (B, C, S), _mybir.dt.float32, kind="ExternalOutput").ap()
    build(nc, *args, out, STAGES)
    r = _run(nc, [arrays], core_ids=[0])
    return r.results[0]["out_dram"].reshape(B, C, IMG, IMG)
```

```python
from contextlib import ExitStack

import numpy as np
import concourse.bass as bass
from concourse import mybir

FP32 = mybir.dt.float32
BF16 = mybir.dt.bfloat16
I32 = mybir.dt.int32
ALU = mybir.AluOpType
ACT = mybir.ActivationFunctionType
AX = mybir.AxisListType

B, C, S = 8, 64, 1024
R = 2
P = R * C
Q = B // R
T = 512
NT = Q * S // T
E = 8
TOK = 128
NG = Q * S // TOK
JS = S // TOK
PARTS = 3
GW = PARTS * R * E
SPLIT, DM, DIN, DST, NH, HD = 8, 8, 16, 16, 2, 8
TAPS = 3
WIN3 = 9
IMG = 32
PAD = IMG + 2
LN_EXP = "natural_log_exp_and_others"
RSQRT_MAGIC = 0x5F3759DF
ARENA_N = 23600
CREDIT = 4
HIDDEN = {"L0": 2, "L1": 1, "L2": 2, "L3": 2}


def columns():
    sizes = [("ident", P), ("center", P), ("mean64", P), ("ones64", P), ("mean16", P),
             ("pairs", P), ("heads", P), ("rank", E), ("eps5", 1), ("eps6", 1), ("ones", P),
             ("l0_wkT", 256), ("l0_wvT", 256), ("l0_wq", 128), ("l0_woT", 128), ("l0_bo", 1),
             ("l1_wT", C), ("l1_b", C)]
    for name, blocks in HIDDEN.items():
        sizes += [(name + "_wg", R * E), (name + "_bg", E), (name + "_w1", E * blocks * 128),
                  (name + "_w2", E * blocks * C), (name + "_b1", E * blocks), (name + "_b2", E)]
    sizes += [("m_lnw", 1), ("m_lnb", 1), ("m_win", 4 * P), ("m_cw", TAPS * 3),
              ("m_cb", 3), ("m_wdt", Q * P), ("m_dtb", 1), ("m_alog", 1), ("m_dh", 1),
              ("m_rms", 1), ("m_wout", C), ("m_skip", 1), ("m_proj", P), ("m_projb", 1),
              ("i_wr", P), ("i_ws", WIN3 * P), ("i_gamma", 1), ("i_beta", 1),
              ("l3_g", E), ("l3_b", E)]
    at, out = 0, {}
    for name, n in sizes:
        out[name] = (at, n)
        at += n
    return out, at


COLS, NCOLS = columns()


class Count:

    def __init__(self, sem):
        self.sem, self.base = sem, 0

    def at(self, n):
        return n + self.base


class Chain:

    def __init__(self, eng, count, start=0):
        self.eng, self.count, self.start, self.n = eng, count, start, 0

    def step(self, ins):
        self.n += 1
        ins.then_inc(self.count.sem, 1)
        self.eng.wait_ge(self.count.sem, self.count.at(self.start + self.n))


def build(nc, x_dram, w_dram, sel_dram, out_dram, stages):
    ctx = ExitStack()
    with ctx:
        def sb(name, shape, dt=FP32):
            return ctx.enter_context(nc.sbuf_tensor(name, shape, dt))

        counts = []

        def count(name):
            counts.append(Count(ctx.enter_context(nc.semaphore(name))))
            return counts[-1]

        X = sb("X", [P, Q * S])
        XN = sb("XN", [P, Q * S])
        W = sb("W", [P, NCOLS])
        SEL = sb("SEL", [P, E, P], BF16)
        IDB = sb("IDB", [P, P], BF16)
        ARENA = sb("ARENA", [P, ARENA_N])
        ROWS = sb("ROWS", [P, 2 * S + 2 * P])
        scratch = [nc.dram_tensor(f"scratch_{k}", (B, P, S), FP32, kind="Internal").ap() for k in "zxbc"]
        ys_dram = nc.dram_tensor("scratch_y", (B, P, S), FP32, kind="Internal").ap()
        PS = ctx.enter_context(nc.psum_tensor("PS", [P, 8, T], FP32))

        def w(name, lo=0, hi=None, rows=slice(None)):
            at, n = COLS[name]
            return W[rows, at + lo:at + (n if hi is None else hi)]

        def apart(eng):
            eng.wait_ge(loaded.sem, CREDIT + 64)

        def half(r):
            return slice(r * C, (r + 1) * C)

        class Arena:

            def __init__(self):
                self.used = 0

            def take(self, *shape):
                n = int(np.prod(shape))
                ap = ARENA[:, self.used:self.used + n]
                self.used += n
                assert self.used <= ARENA_N, self.used
                if len(shape) == 2:
                    ap = ap.rearrange("p (a b) -> p a b", b=shape[1])
                if len(shape) == 3:
                    ap = ap.rearrange("p (a b c) -> p a b c", b=shape[1], c=shape[2])
                return ap

        loaded = count("loaded")
        stored = count("stored")
        ln_centered = count("ln_centered")
        ln_squared = count("ln_squared")
        ln_varied = count("ln_varied")
        ln_log = count("ln_log")
        ln_scaled = count("ln_scaled")
        ln_inverted = count("ln_inverted")
        ln_normed = count("ln_normed")
        ln_taken = count("ln_taken")
        ln_newton = count("ln_newton")
        g_logits = count("g_logits")
        g_ranked = count("g_ranked")
        g_taken = count("g_taken")
        g_bent = count("g_bent")
        g_cleared = count("g_cleared")
        g_chain = count("g_chain")
        g_split = count("g_split")
        g_turned = count("g_turned")
        g_rows = count("g_rows")
        e_input = [count(f"e_input{k}") for k in range(2)]
        e_hidden = count("e_hidden")
        e_gelu = count("e_gelu")
        e_weight = count("e_weight")
        e_wcopy = count("e_wcopy")
        e_out = count("e_out")
        e_scaled = count("e_scaled")
        e_added = count("e_added")
        e_fold = count("e_fold")
        a_b1 = count("a_b1")
        a_b1copy = count("a_b1copy")
        a_ctx = count("a_ctx")
        a_ctxcopy = count("a_ctxcopy")
        a_done = count("a_done")
        a_exp = count("a_exp")
        a_input = count("a_input")
        a_inv = count("a_inv")
        a_k = count("a_k")
        a_maxed = count("a_maxed")
        a_mt = count("a_mt")
        a_mtcopy = count("a_mtcopy")
        a_out = count("a_out")
        a_sums = count("a_sums")
        a_turned = count("a_turned")
        a_xt = count("a_xt")
        a_xturned = count("a_xturned")
        a_pt = count("a_pt")
        a_gt = count("a_gt")
        b_chain = count("b_chain")
        b_cleared = count("b_cleared")
        b_moment = count("b_moment")
        b_reduced = count("b_reduced")
        b_total = count("b_total")
        c_bc = [count(f"c_bc{k}") for k in range(2)]
        c_carry = count("c_carry")
        c_dtx = count("c_dtx")
        c_kept = count("c_kept")
        c_scan = count("c_scan")
        c_stored = count("c_stored")
        c_skip = count("c_skip")
        c_sum = count("c_sum")
        c_u = count("c_u")
        c_x = [count(f"c_x{k}") for k in range(2)]
        c_ycopy = count("c_ycopy")
        c_z = count("c_z")
        f_done = count("f_done")
        f_shift = count("f_shift")
        i_added = count("i_added")
        i_done = count("i_done")
        i_input = count("i_input")
        i_kern = count("i_kern")
        i_scaled = count("i_scaled")
        m_cleared = count("m_cleared")
        m_dt = count("m_dt")
        m_input = count("m_input")
        m_proj = count("m_proj")
        m_rate = count("m_rate")
        m_silu = count("m_silu")
        m_soft = count("m_soft")
        m_stored = [count(f"m_stored{k}") for k in range(2)]
        m_taps = count("m_taps")
        m_raw = count("m_raw")
        m_conv = count("m_conv")
        o_done = count("o_done")
        o_gated = count("o_gated")
        o_input = [count(f"o_input{k}") for k in range(2)]
        o_mean = count("o_mean")
        o_normed = count("o_normed")
        o_out = count("o_out")
        o_root = count("o_root")
        o_squared = count("o_squared")
        p_done = count("p_done")
        s_chain = count("s_chain")
        p_out = count("p_out")
        s_done = count("s_done")
        s_input = [count(f"s_input{k}") for k in range(2)]
        s_mixed = count("s_mixed")
        s_norm = count("s_norm")
        s_power = count("s_power")
        s_relu = count("s_relu")
        s_root = count("s_root")
        s_sim = count("s_sim")
        s_squared = count("s_squared")
        s_t = count("s_t")
        s_tcopy = count("s_tcopy")
        s_unit = count("s_unit")

        with nc.Block() as block:
            @block.sync
            def _(sp):
                xv = x_dram.rearrange("(q r) c s -> (r c) q s", r=R)
                for r in range(R):
                    src = x_dram.rearrange("(q r) c s -> r c q s", r=R)[r]
                    sp.dma_start(X[half(r), :].rearrange("c (q s) -> c q s", q=Q), src).then_inc(loaded.sem, 16)
                sp.dma_start(W[:, :], w_dram).then_inc(loaded.sem, 16)
                sp.dma_start(SEL[:, :, :], sel_dram).then_inc(loaded.sem, 16)
                sp.wait_ge(loaded.sem, CREDIT + 64)

            @block.gpsimd
            def _(pool):
                for c in counts:
                    pool.sem_inc(c.sem, CREDIT)
        for c in counts:
            c.base = CREDIT
        loaded.base += 64

        with nc.Block() as block:
            @block.vector
            def _(dve):
                nc.vector.tensor_copy(IDB[:, :], w("ident")).then_inc(stored.sem, 1)
                dve.wait_ge(stored.sem, stored.at(1))

        def tile(buf, t):
            return buf[:, bass.ds(t * T, T)]

        def layer_norm(dst, src, eps, affine=None):
            a = Arena()
            FLY = 4
            SQ, LOG, INV, NRM = (a.take(FLY, T) for _ in range(4))
            with nc.Block() as block:
                @block.tensor
                def _(pe):
                    with pe.Fori(0, NT // FLY) as i:
                        for k in range(FLY):
                            pe.wait_ge(ln_normed.sem, ln_normed.at(i * FLY + (k + 1 - FLY)))
                            nc.tensor.matmul(PS[:, k, :], w("center"), tile(src, i * FLY + k),
                                             start=True, stop=True).then_inc(ln_centered.sem, 1)
                        for k in range(FLY):
                            pe.wait_ge(ln_squared.sem, ln_squared.at(i * FLY + (k + 1)))
                            nc.tensor.matmul(PS[:, FLY + k, :], w("mean64"), SQ[:, k, :],
                                             start=True, stop=True).then_inc(ln_varied.sem, 1)

                @block.scalar
                def _(act):
                    act.preload_act_table_set(LN_EXP)
                    with act.Fori(0, NT // FLY) as i:
                        for k in range(FLY):
                            act.wait_ge(ln_centered.sem, ln_centered.at(i * FLY + (k + 1)))
                            nc.scalar.activation(SQ[:, k, :], PS[:, k, :], ACT.Square)\
                                .then_inc(ln_squared.sem, 1)
                        for k in range(FLY):
                            act.wait_ge(ln_varied.sem, ln_varied.at(i * FLY + (k + 1)))
                            nc.scalar.activation(LOG[:, k, :], PS[:, FLY + k, :], ACT.Ln, bias=w(eps))\
                                .then_inc(ln_log.sem, 1)
                        for k in range(FLY):
                            act.wait_ge(ln_log.sem, ln_log.at(i * FLY + (k + 1)))
                            nc.scalar.activation(INV[:, k, :], LOG[:, k, :], ACT.Exp, scale=-0.5)\
                                .then_inc(ln_inverted.sem, 1)

                @block.vector
                def _(dve):
                    with dve.Fori(0, NT // FLY) as i:
                        for k in range(FLY):
                            dve.wait_ge(ln_inverted.sem, ln_inverted.at(i * FLY + (k + 1)))
                            if affine is None:
                                nc.vector.tensor_tensor(tile(dst, i * FLY + k), PS[:, k, :], INV[:, k, :],
                                                        ALU.mult).then_inc(ln_normed.sem, 1)
                            else:
                                nc.vector.tensor_tensor(NRM[:, k, :], PS[:, k, :], INV[:, k, :],
                                                        ALU.mult).then_inc(ln_scaled.sem, 1)
                                dve.wait_ge(ln_scaled.sem, ln_scaled.at(i * FLY + (k + 1)))
                                nc.vector.tensor_scalar(tile(dst, i * FLY + k), NRM[:, k, :], w(affine[0]),
                                                        w(affine[1]), ALU.mult, ALU.add)\
                                    .then_inc(ln_normed.sem, 1)
            for c in (ln_centered, ln_squared, ln_varied, ln_log, ln_inverted, ln_normed):
                c.base += NT
            if affine:
                ln_scaled.base += NT

        WT = ROWS[:, 0:T].bitcast(BF16).rearrange("p (a b) -> p a b", b=T)

        def experts(layer, over_all=False, norms=1):
            blocks = HIDDEN[layer]
            NB = E * blocks
            NORMS = norms
            renorm = norms == 2
            G = T // TOK
            GR = G * R
            a = Arena()
            XS, H = a.take(2, T), a.take(2, R * T)
            XE = a.take(2, T) if renorm else XS
            WB, TMP, SUM = a.take(2, T), a.take(2, T), a.take(2, T)
            SQ, CEN, VAR, INV, NEWT = (a.take(T) for _ in range(5))
            L, M, SC, S1, S2, REST = (a.take(GR, E) for _ in range(6))
            EX, EY = a.take(GR, E + 1), a.take(GR, E + 1)
            M1, M2, W1, W2 = (a.take(GR) for _ in range(4))
            D = EX[:, :, E:E + 1].rearrange("p a b -> p (a b)")
            PT = a.take(G, GW // 2).rearrange("p a b -> p (a b)").bitcast(BF16)\
                .rearrange("p (g k r e) -> p g k r e", k=PARTS, r=R, e=E)
            PTW = PT.rearrange("p g k r e -> p g (k r e)")
            NEWTON = 2 + 3 * 3
            RANK, WEIGH = 11 + (2 if over_all else 1), 8 + (6 if over_all else 2)
            SIDE = 7

            if renorm:
                pe_at = {0: "center", 2: "vary", 7: "logits", 8: "center2", 10: "vary2", 13: "turn"}
                act_at = {1: "square", 9: "bend square2", 13: "rows"}
                dve_at = {-1: "keep", 1: "start 3 3", 2: "3 norm", 3: "rank", 4: "keep2 weigh start2 3",
                          5: "3 3 norm2"}
            elif norms == 1:
                pe_at = {0: "center", 3: "vary", 8: "logits", 13: "turn"}
                act_at = {1: "square", 11: "bend", 13: "rows"}
                dve_at = {-1: "keep", 1: "start 3 3", 2: "3 norm", 4: "rank", 5: "weigh"}
            else:
                pe_at = {1: "logits", 5: "turn"}
                act_at = {3: "bend", 5: "rows"}
                dve_at = {1: "rank", 3: "weigh"}

            def over(m):
                return m.unsqueeze(2).to_broadcast([P, GR, E])

            def gr(v):
                return v.rearrange("p (g r) e -> p g r e", r=R)

            with nc.Block() as block:
                if not norms:
                    @block.sync
                    def _(sp):
                        for k in range(2):
                            sp.dma_start(XS[:, k, :], tile(XN, k)).then_inc(e_input[k].sem, 16)
                        with sp.Fori(0, NT // 2 - 1) as i:
                            for k in range(2):
                                sp.wait_ge(e_hidden.sem, e_hidden.at((i * 2 + k + 1) * NB))
                                sp.dma_start(XS[:, k, :], tile(XN, i * 2 + k + 2))\
                                    .then_inc(e_input[k].sem, 16)

                @block.gpsimd
                def _(pool):
                    nc.gpsimd.memset(ROWS[:, 0:T], 0.0).then_inc(g_cleared.sem, 1)

                    def tile_of(t, k):
                        for e in range(1, E):
                            pool.wait_ge(e_scaled.sem, e_scaled.at(t * E + (e + 1)))
                            if e > 1:
                                pool.wait_ge(e_added.sem, e_added.at(t * (E - 1) + (e - 1)))
                            nc.gpsimd.tensor_tensor(SUM[:, k, :], SUM[:, k, :], TMP[:, e % 2, :], ALU.add)\
                                .then_inc(e_added.sem, 1)

                    with pool.Fori(0, NT // 2) as i:
                        for k in range(2):
                            tile_of(i * 2 + k, k)

                @block.tensor
                def _(pe):
                    mm = nc.tensor.matmul

                    def center(p, k, n):
                        if n:
                            pe.wait_ge(g_taken.sem, g_taken.at(p + 1))
                        else:
                            pe.wait_ge(g_rows.sem, g_rows.at(p))
                        mm(PS[:, SIDE, :], w("center"), XS[:, k, :] if n else tile(X, p),
                           start=True, stop=True).then_inc(ln_centered.sem, 1)

                    def vary(p, k, n):
                        pe.wait_ge(ln_squared.sem, ln_squared.at(p * NORMS + (n + 1)))
                        mm(PS[:, SIDE, :], w("mean64"), SQ, start=True, stop=True).then_inc(ln_varied.sem, 1)

                    def logits(p, k, turn=None):
                        if norms:
                            pe.wait_ge(ln_normed.sem, ln_normed.at(p * NORMS + 1))
                        else:
                            pe.wait_ge(e_input[k].sem, e_input[k].at((turn + 1) * 16))
                            pe.wait_ge(g_rows.sem, g_rows.at(p))
                        for g in range(G):
                            last = mm(PS[:, SIDE, g * R * E:(g + 1) * R * E], XS[:, k, g * TOK:(g + 1) * TOK],
                                      w(layer + "_wg"), start=True, stop=True)
                        last.then_inc(g_logits.sem, 1)

                    def transpose(p, k):
                        if renorm:
                            pe.wait_ge(ln_taken.sem, ln_taken.at((p + 1) * (2 * NORMS)))
                        pe.wait_ge(g_split.sem, g_split.at(p + 1))
                        for g in range(G):
                            last = mm(PS[0:GW, SIDE, g * TOK:(g + 1) * TOK], PTW[:, g, :], IDB[:, :],
                                      start=True, stop=True)
                        last.then_inc(g_turned.sem, 1)

                    def prepare(what, p, k, turn):
                        if what == "center":
                            center(p, k, 0)
                        elif what == "vary":
                            vary(p, k, 0)
                        elif what == "logits":
                            logits(p, k, turn)
                        elif what == "center2":
                            center(p, k, 1)
                        elif what == "vary2":
                            vary(p, k, 1)
                        elif what == "turn":
                            transpose(p, k)

                    def up(t, k, b):
                        if norms and b == 0:
                            pe.wait_ge(ln_normed.sem, ln_normed.at((t + 1) * NORMS))
                        pe.wait_ge(e_gelu.sem, e_gelu.at(t * NB + (b - 1)))
                        for r in range(R):
                            last = mm(PS[:, (b % 2) * R + r, :], w(layer + "_w1", b * 128, (b + 1) * 128, half(r)),
                                      XE[half(r), k, :], start=True, stop=True)
                        last.then_inc(e_hidden.sem, 1)

                    def tile_of(t, k, i, more=True):
                        def down(b):
                            e, part = divmod(b, blocks)
                            if part == 0:
                                pe.wait_ge(e_wcopy.sem, e_wcopy.at(t * E + e))
                                if e == 0:
                                    pe.wait_ge(g_rows.sem, g_rows.at(t + 1))
                                mm(PS[:, 6, :], SEL[:, e, :], WT[:, k, :], start=True, stop=True)\
                                    .then_inc(e_weight.sem, 1)
                                pe.wait_ge(e_scaled.sem, e_scaled.at(t * E + (e - 1)))
                            pe.wait_ge(e_gelu.sem, e_gelu.at(t * NB + (b + 1)))
                            for r in range(R):
                                last = mm(PS[half(r), 4 + e % 2, :], w(layer + "_w2", b * C, (b + 1) * C),
                                          H[:, b % 2, r * T:(r + 1) * T], start=part == 0, stop=part == blocks - 1)
                            if part == blocks - 1:
                                last.then_inc(e_out.sem, 1)

                        for b in range(NB):
                            if b + 1 < NB:
                                up(t, k, b + 1)
                            elif more:
                                up(t + 1, 1 - k, 0)
                            down(b)
                            if more:
                                prepare(pe_at.get(b), t + 1, 1 - k, i + k)

                    for b in sorted(pe_at):
                        prepare(pe_at[b], 0, 0, 0)
                    up(0, 0, 0)
                    with pe.Fori(0, NT // 2 - 1) as i:
                        for k in range(2):
                            tile_of(i * 2 + k, k, i)
                    tile_of(NT - 2, 0, NT // 2 - 1)
                    tile_of(NT - 1, 1, NT // 2 - 1, more=False)

                @block.scalar
                def _(act):
                    f = nc.scalar.activation
                    act.preload_act_table(ACT.Gelu)

                    def square(p, n):
                        act.wait_ge(ln_taken.sem, ln_taken.at(p * (2 * NORMS) + (2 * n + 1)))
                        f(SQ, CEN, ACT.Square).then_inc(ln_squared.sem, 1)

                    def bend(p):
                        act.wait_ge(g_ranked.sem, g_ranked.at(p + 1))
                        if over_all:
                            f(EX, EX, ACT.Tanh, scale=0.5).then_inc(g_bent.sem, 1)
                        else:
                            f(D, D, ACT.Tanh, scale=0.5).then_inc(g_bent.sem, 1)

                    def rows(p, k):
                        act.wait_ge(g_cleared.sem, g_cleared.at(1))
                        act.wait_ge(g_turned.sem, g_turned.at(p + 1))
                        nc.scalar.copy(WT[0:GW, k, :], PS[0:GW, SIDE, :])\
                            .then_inc(g_rows.sem, 1)

                    def prepare(steps, p, k):
                        for what in steps.split():
                            if what == "square":
                                square(p, 0)
                            elif what == "bend":
                                bend(p)
                            elif what == "square2":
                                square(p, 1)
                            elif what == "rows":
                                rows(p, k)

                    def tile_of(t, k, more=True):
                        def weight(e):
                            act.wait_ge(e_weight.sem, e_weight.at(t * E + (e + 1)))
                            act.wait_ge(e_scaled.sem, e_scaled.at(t * E + (e - 1)))
                            nc.scalar.copy(WB[:, e % 2, :], PS[:, 6, :]).then_inc(e_wcopy.sem, 1)

                        for b in range(NB + 1):
                            if b < NB:
                                act.wait_ge(e_hidden.sem, e_hidden.at(t * NB + (b + 1)))
                                f(H[:, b % 2, :], PS[:, (b % 2) * R:(b % 2) * R + R, :].rearrange("p a b -> p (a b)"),
                                  ACT.Gelu, bias=w(layer + "_b1", b, b + 1)).then_inc(e_gelu.sem, 1)
                            if b and (b - 1) % blocks == 0:
                                weight((b - 1) // blocks)
                            if b and more:
                                prepare(act_at.get(b - 1, ""), t + 1, 1 - k)

                    for b in sorted(act_at):
                        prepare(act_at[b], 0, 0)
                    with act.Fori(0, NT // 2 - 1) as i:
                        for k in range(2):
                            tile_of(i * 2 + k, k)
                    tile_of(NT - 2, 0)
                    tile_of(NT - 1, 1, more=False)

                @block.vector
                def _(dve):
                    v = nc.vector
                    rank_of = w("rank").unsqueeze(1).to_broadcast([P, GR, E])

                    def keep(p, n):
                        dve.wait_ge(ln_centered.sem, ln_centered.at(p * NORMS + (n + 1)))
                        v.tensor_copy(CEN, PS[:, SIDE, :]).then_inc(ln_taken.sem, 1)

                    def invert(p, k, n, chain, what):
                        step = chain.step
                        if what.startswith("start"):
                            dve.wait_ge(ln_varied.sem, ln_varied.at(p * NORMS + (n + 1)))
                            v.tensor_scalar(VAR, PS[:, SIDE, :], w("eps5"), None, ALU.add).then_inc(ln_taken.sem, 1)
                            dve.wait_ge(ln_taken.sem, ln_taken.at(p * (2 * NORMS) + 2 * (n + 1)))
                            step(v.tensor_scalar(INV.bitcast(I32), VAR.bitcast(I32), 1, None,
                                                 ALU.arith_shift_right))
                            step(v.tensor_scalar(INV.bitcast(I32), INV.bitcast(I32), -1, RSQRT_MAGIC,
                                                 ALU.mult, ALU.add))
                        elif what == "3":
                            step(v.tensor_tensor(NEWT, INV, INV, ALU.mult))
                            step(v.scalar_tensor_tensor(NEWT, NEWT, -0.5, VAR, ALU.mult, ALU.mult))
                            step(v.scalar_tensor_tensor(INV, NEWT, 1.5, INV, ALU.add, ALU.mult))
                        else:
                            assert chain.n == NEWTON
                            v.tensor_tensor((XE if n else XS)[:, k, :], CEN, INV, ALU.mult)\
                                .then_inc(ln_normed.sem, 1)

                    def rank(p):
                        chain = Chain(dve, g_chain, p * (RANK + WEIGH))
                        step = chain.step
                        dve.wait_ge(g_logits.sem, g_logits.at(p + 1))
                        v.tensor_tensor(L, PS[:, SIDE, 0:GR * E].rearrange("p (a e) -> p a e", e=E),
                                        w(layer + "_bg").unsqueeze(1).to_broadcast([P, GR, E]), ALU.add)\
                            .then_inc(g_taken.sem, 1)
                        dve.wait_ge(g_taken.sem, g_taken.at(p + 1))
                        for src, m, sel in ((L, M1, S1), (M, M2, S2)):
                            step(v.tensor_reduce(m, src, AX.X, ALU.max))
                            step(v.tensor_tensor(SC, src, over(m), ALU.is_equal))
                            step(v.tensor_tensor(SC, SC, rank_of, ALU.mult))
                            step(v.tensor_reduce(W1, SC, AX.X, ALU.max))
                            step(v.tensor_tensor(sel, SC, over(W1), ALU.is_equal))
                            if sel is S1:
                                step(v.scalar_tensor_tensor(M, S1, -3.0e38, L, ALU.mult, ALU.add))
                        if over_all:
                            step(v.tensor_tensor(EX[:, :, 0:E], L, over(M1), ALU.subtract))
                        step(v.tensor_tensor(D, M2, M1, ALU.subtract))
                        assert chain.n == RANK
                        dve.sem_inc(g_ranked.sem, 1)

                    def weigh(p):
                        chain = Chain(dve, g_chain, p * (RANK + WEIGH) + RANK)
                        step = chain.step
                        dve.wait_ge(g_bent.sem, g_bent.at(p + 1))
                        if over_all:
                            step(v.tensor_scalar(EY, EX, -1.0, 1.0, ALU.mult, ALU.add))
                            step(v.reciprocal(EY, EY))
                            step(v.scalar_tensor_tensor(EX, EX, 1.0, EY, ALU.add, ALU.mult))
                            step(v.tensor_reduce(M1, EX[:, :, 0:E], AX.X, ALU.add))
                            step(v.reciprocal(W1, M1))
                            step(v.tensor_tensor(W2, D, W1, ALU.mult))
                        else:
                            step(v.tensor_scalar(W1, D, -0.5, 0.5, ALU.mult, ALU.add))
                            step(v.tensor_scalar(W2, D, 0.5, 0.5, ALU.mult, ALU.add))
                        step(v.tensor_tensor(S1, S1, over(W1), ALU.mult))
                        step(v.tensor_tensor(S2, S2, over(W2), ALU.mult))
                        step(v.tensor_tensor(L, S1, S2, ALU.add))
                        rest = L
                        for part in range(PARTS):
                            step(v.tensor_copy(PT[:, :, part, :, :], gr(rest)))
                            if part < PARTS - 1:
                                step(v.tensor_tensor(gr(REST), gr(rest), PT[:, :, part, :, :], ALU.subtract))
                                rest = REST
                        assert chain.n == WEIGH
                        dve.sem_inc(g_split.sem, 1)

                    def prepare_all(p, k):
                        chains = [Chain(dve, ln_newton, p * (NORMS * NEWTON) + n * NEWTON) for n in range(NORMS)]
                        norm = [0]

                        def run(steps):
                            for what in steps.split():
                                if what in ("keep", "keep2"):
                                    keep(p, int(what == "keep2"))
                                elif what == "rank":
                                    rank(p)
                                elif what == "weigh":
                                    weigh(p)
                                else:
                                    invert(p, k, norm[0], chains[norm[0]], what)
                                    if what == "norm":
                                        norm[0] = NORMS - 1
                        return run

                    def tile_of(t, k, more=True):
                        prepare = prepare_all(t + 1, 1 - k)
                        if more:
                            prepare(dve_at.get(-1, ""))
                        for e in range(E):
                            dve.wait_ge(e_wcopy.sem, e_wcopy.at(t * E + (e + 1)))
                            dve.wait_ge(e_out.sem, e_out.at(t * E + (e + 1)))
                            if e:
                                dve.wait_ge(e_added.sem, e_added.at(t * (E - 1) + max(e - 2, 0)))
                            v.scalar_tensor_tensor(
                                TMP[:, e % 2, :] if e else SUM[:, k, :], PS[:, 4 + e % 2, :],
                                w(layer + "_b2", e, e + 1), WB[:, e % 2, :],
                                ALU.add, ALU.mult).then_inc(e_scaled.sem, 1)
                            if more:
                                prepare(dve_at.get(e, ""))
                        dve.wait_ge(e_added.sem, e_added.at((t + 1) * (E - 1)))
                        v.tensor_tensor(tile(X, t), tile(X, t), SUM[:, k, :], ALU.add).then_inc(e_fold.sem, 1)

                    prepare = prepare_all(0, 0)
                    for e in sorted(dve_at):
                        prepare(dve_at[e])
                    with dve.Fori(0, NT // 2 - 1) as i:
                        for k in range(2):
                            tile_of(i * 2 + k, k)
                    tile_of(NT - 2, 0)
                    tile_of(NT - 1, 1, more=False)
            if not norms:
                for c in e_input:
                    c.base += NT // 2 * 16
            e_hidden.base += NT * NB
            e_gelu.base += NT * NB
            for c in (e_weight, e_wcopy, e_out, e_scaled):
                c.base += NT * E
            e_added.base += NT * (E - 1)
            e_fold.base += NT
            for c in (ln_centered, ln_squared, ln_varied, ln_normed):
                c.base += NT * NORMS
            ln_taken.base += NT * NORMS * 2
            ln_newton.base += NT * NORMS * NEWTON
            for c in (g_logits, g_taken, g_ranked, g_bent, g_split, g_turned, g_rows):
                c.base += NT
            g_chain.base += NT * (RANK + WEIGH)
            g_cleared.base += 1

        def linear_attention():
            a = Arena()
            XS, PC, PT, XT = a.take(S), a.take(2, S), a.take(R, JS, 2 * P), a.take(JS, R, C)
            NM, SUM, GT, CT = a.take(2 * R), a.take(2 * R), a.take(2 * P), a.take(2 * R, P)
            B1S, MT = a.take(2 * R, C), a.take(C)
            NU = 2 * R

            def wide(bank, n=2):
                return PS[:, bank:bank + n, :].rearrange("p a b -> p (a b)")

            with nc.Block() as block:
                @block.sync
                def _(sp):
                    with sp.Fori(0, Q) as q:
                        sp.wait_ge(a_out.sem, a_out.at(q * 2))
                        sp.dma_start(XS, XN[:, bass.ds(q * S, S)]).then_inc(a_input.sem, 16)

                @block.tensor
                def _(pe):
                    mm = nc.tensor.matmul
                    with pe.Fori(0, Q) as q:
                        def k_of(u):
                            r, b = divmod(u, 2)
                            pe.wait_ge(a_exp.sem, a_exp.at(q * NU + max(u - 1, 0)))
                            for h in range(2):
                                last = mm(PS[:, 2 * (u % 2) + h, :], w("l0_wkT", b * P, (b + 1) * P, half(r)),
                                          XS[half(r), h * T:(h + 1) * T], start=True, stop=True)
                            last.then_inc(a_k.sem, 1)

                        def turn(u):
                            pe.wait_ge(a_exp.sem, a_exp.at(q * NU + (u + 1)))
                            pe.wait_ge(a_pt.sem, a_pt.at(q * NU + u))
                            for j in range(JS):
                                last = nc.tensor.transpose(PS[:, 4 + j // 4, (j % 4) * TOK:(j % 4 + 1) * TOK],
                                                           PC[:, u % 2, j * TOK:(j + 1) * TOK], w("ident"))
                            last.then_inc(a_turned.sem, 1)

                        pe.wait_ge(a_input.sem, a_input.at((q + 1) * 16))
                        pe.wait_ge(a_done.sem, a_done.at(q * 2))
                        k_of(0)
                        k_of(1)
                        for j in range(JS):
                            last = nc.tensor.transpose(PS[:, 6 + j // 4, (j % 4) * TOK:(j % 4 + 1) * TOK],
                                                       XS[:, j * TOK:(j + 1) * TOK], w("ident"))
                        last.then_inc(a_xturned.sem, 1)
                        turn(0)
                        k_of(2)
                        turn(1)
                        k_of(3)
                        turn(2)
                        turn(3)
                        pe.wait_ge(a_xt.sem, a_xt.at(q + 1))
                        pe.wait_ge(a_pt.sem, a_pt.at((q + 1) * NU))
                        for j in range(JS):
                            for r in range(R):
                                last = mm(PS[half(r), 6, 0:2 * P], XT[:, j, r, :], PT[:, r, j, :],
                                          start=j == 0, stop=j == JS - 1)
                        last.then_inc(a_sums.sem, 1)
                        pe.wait_ge(a_gt.sem, a_gt.at(q + 1))
                        for r in range(R):
                            for b in range(2):
                                u = r * 2 + b
                                last = mm(PS[:, 7 - 2 * r, b * P:(b + 1) * P], w("l0_wvT", b * P, (b + 1) * P, half(r)),
                                          GT[half(r), b * P:(b + 1) * P], start=True, stop=True)
                        last.then_inc(a_ctx.sem, 1)
                        pe.wait_ge(a_ctxcopy.sem, a_ctxcopy.at((q + 1) * R))
                        for u in range(NU):
                            last = mm(PS[:, 6, u * C:(u + 1) * C], CT[:, u, :],
                                      w("l0_woT", (u % 2) * C, (u % 2 + 1) * C), start=True, stop=True)
                        last.then_inc(a_b1.sem, 1)
                        pe.wait_ge(a_b1copy.sem, a_b1copy.at(q + 1))
                        for b in range(2):
                            for r in range(R):
                                last = mm(PS[half(r), 7, 0:C], w("l0_wq", b * C, (b + 1) * C), B1S[:, r * 2 + b, :],
                                          start=b == 0, stop=b == 1)
                        last.then_inc(a_mt.sem, 1)
                        apart(pe)
                        pe.wait_ge(a_mtcopy.sem, a_mtcopy.at(q + 1))
                        for h in range(2):
                            for r in range(R):
                                last = mm(PS[half(r), 4 + h, :], MT[half(r), :], XS[half(r), h * T:(h + 1) * T],
                                          start=True, stop=True)
                            last.then_inc(a_out.sem, 1)

                @block.scalar
                def _(act):
                    act.preload_act_table_set(LN_EXP)
                    with act.Fori(0, Q) as q:
                        for u in range(NU):
                            act.wait_ge(a_maxed.sem, a_maxed.at(q * NU + (u + 1)))
                            act.wait_ge(a_turned.sem, a_turned.at(q * NU + max(u - 1, 0)))
                            if u == 0:
                                act.wait_ge(a_b1copy.sem, a_b1copy.at(q))
                            nc.scalar.activation(PC[:, u % 2, :], wide(2 * (u % 2)), ACT.Exp,
                                                 bias=NM[:, u:u + 1], accum_out=SUM[:, u:u + 1])\
                                .then_inc(a_exp.sem, 1)
                            if u == 1:
                                act.wait_ge(a_xturned.sem, a_xturned.at(q + 1))
                                nc.scalar.copy(XT, wide(6).rearrange("p (j r c) -> p j r c", r=R, c=C))\
                                    .then_inc(a_xt.sem, 1)

                @block.vector
                def _(dve):
                    v = nc.vector
                    with dve.Fori(0, Q) as q:
                        def maximum(u):
                            dve.wait_ge(a_k.sem, a_k.at(q * NU + (u + 1)))
                            v.tensor_reduce(NM[:, u:u + 1], wide(2 * (u % 2)), AX.X, ALU.max, negate=True)\
                                .then_inc(a_maxed.sem, 1)

                        def keep(u):
                            r, b = divmod(u, 2)
                            dve.wait_ge(a_turned.sem, a_turned.at(q * NU + (u + 1)))
                            v.tensor_copy(PT[:, r, :, b * P:(b + 1) * P],
                                          wide(4).rearrange("p (j d) -> p j d", d=P)).then_inc(a_pt.sem, 1)

                        maximum(0)
                        maximum(1)
                        for u in range(NU):
                            keep(u)
                            if u + 2 < NU:
                                maximum(u + 2)
                        dve.wait_ge(a_exp.sem, a_exp.at((q + 1) * NU))
                        v.reciprocal(SUM, SUM).then_inc(a_inv.sem, 1)
                        dve.wait_ge(a_sums.sem, a_sums.at(q + 1))
                        v.tensor_copy(GT, PS[:, 6, 0:2 * P]).then_inc(a_gt.sem, 1)
                        dve.wait_ge(a_ctx.sem, a_ctx.at(q + 1))
                        for r in range(R):
                            v.tensor_tensor(CT[:, 2 * r:2 * r + 2, :],
                                            PS[:, 7 - 2 * r, 0:2 * P].rearrange("p (b d) -> p b d", b=2),
                                            w("heads").unsqueeze(1).to_broadcast([P, 2, P]), ALU.mult)\
                                .then_inc(a_ctxcopy.sem, 1)
                        dve.wait_ge(a_b1.sem, a_b1.at(q + 1))
                        dve.wait_ge(a_inv.sem, a_inv.at(q + 1))
                        v.tensor_tensor(B1S, PS[:, 6, 0:NU * C].rearrange("p (b c) -> p b c", b=NU),
                                        SUM.unsqueeze(2).to_broadcast([P, NU, C]), ALU.mult)\
                            .then_inc(a_b1copy.sem, 1)
                        dve.wait_ge(a_mt.sem, a_mt.at(q + 1))
                        v.tensor_copy(MT, PS[:, 7, 0:C]).then_inc(a_mtcopy.sem, 1)
                        for h in range(2):
                            dve.wait_ge(a_out.sem, a_out.at(q * 2 + (h + 1)))
                            xt = X[:, bass.ds(q * S + h * T, T)]
                            v.scalar_tensor_tensor(xt, PS[:, 4 + h, :], w("l0_bo"), xt, ALU.add, ALU.add)\
                                .then_inc(a_done.sem, 1)

        def similarity():
            a = Arena()
            XS, XH = a.take(2, S), a.take(2, S)
            SQ, RN = a.take(S), a.take(S)
            TT = [a.take(R, JS, C) for _ in range(2)]
            RL, R2 = a.take(R, S), a.take(R, S)
            NB = JS * R

            def both(bank):
                return PS[:, bank:bank + 2, :].rearrange("p a b -> p (a b)")

            pe_at = {1: "mapped", 3: "norm"}
            act_at = {1: "square", 5: "root"}
            dve_at = {2: "shift", 4: "guard", 6: "unit"}

            def pairs(eng, body, prepare, steps):
                for at in sorted(steps):
                    prepare(steps[at], 0, 0, 0)
                with eng.Fori(0, Q // 2 - 1) as i:
                    for k in range(2):
                        body(i * 2 + k, k, lambda at, i=i, k=k:
                             at in steps and prepare(steps[at], i * 2 + (k + 1), 1 - k, i + k))
                body(Q - 2, 0, lambda at: at in steps and prepare(steps[at], Q - 1, 1, Q // 2 - 1))
                body(Q - 1, 1, lambda at: None)

            with nc.Block() as block:
                @block.sync
                def _(sp):
                    for k in range(2):
                        sp.dma_start(XS[:, k, :], XN[:, k * S:(k + 1) * S]).then_inc(s_input[k].sem, 16)
                    with sp.Fori(0, Q // 2 - 1) as i:
                        for k in range(2):
                            sp.wait_ge(s_unit.sem, s_unit.at(i * 2 + (k + 1)))
                            sp.dma_start(XS[:, k, :], XN[:, bass.ds(i * (2 * S) + (k + 2) * S, S)])\
                                .then_inc(s_input[k].sem, 16)

                @block.tensor
                def _(pe):
                    mm = nc.tensor.matmul

                    def prepare(what, q, k, turn):
                        if what == "mapped":
                            pe.wait_ge(s_input[k].sem, s_input[k].at((turn + 1) * 16))
                            pe.wait_ge(s_chain.sem, s_chain.at(q))
                            for r in range(R):
                                for m in range(JS):
                                    last = mm(PS[:, 4 + r, m * C:(m + 1) * C],
                                              XS[half(r), k, m * TOK:(m + 1) * TOK],
                                              w("l1_wT", rows=half(r)), start=True, stop=True)
                            last.then_inc(s_t.sem, 1)
                        else:
                            pe.wait_ge(s_squared.sem, s_squared.at(q + 1))
                            pe.wait_ge(s_tcopy.sem, s_tcopy.at((q + 1) * R))
                            for h in range(2):
                                last = mm(PS[:, 4 + h, :], w("ones64"), SQ[:, h * T:(h + 1) * T],
                                          start=True, stop=True)
                            last.then_inc(s_norm.sem, 1)

                    def body(q, k, beside):
                        pe.wait_ge(s_unit.sem, s_unit.at(q + 1))

                        def similar(m):
                            for r in range(R):
                                pe.wait_ge(s_relu.sem, s_relu.at(q * NB + (m * R + r - 1)))
                                for h in range(2):
                                    last = mm(PS[:, 2 * r + h, :], XH[half(r), k, m * TOK:(m + 1) * TOK],
                                              XH[half(r), k, h * T:(h + 1) * T], start=True, stop=True)
                                last.then_inc(s_sim.sem, 1)

                        def mix(m):
                            if m == 0:
                                pe.wait_ge(s_done.sem, s_done.at(q * 2))
                            for r in range(R):
                                pe.wait_ge(s_power.sem, s_power.at(q * NB + (m * R + r + 1)))
                                for h in range(2):
                                    last = mm(PS[half(r), 6 + h, :], TT[k][:, r, m, :],
                                              R2[:, r, h * T:(h + 1) * T], start=m == 0, stop=m == JS - 1)
                                last.then_inc(s_mixed.sem, 1)

                        similar(0)
                        for m in range(1, JS):
                            similar(m)
                            mix(m - 1)
                            beside(m)
                        mix(JS - 1)

                    pairs(pe, body, prepare, pe_at)

                @block.scalar
                def _(act):
                    act.preload_act_table_set(LN_EXP)

                    def prepare(what, q, k, turn):
                        if what == "square":
                            act.wait_ge(s_input[k].sem, s_input[k].at((turn + 1) * 16))
                            act.wait_ge(s_unit.sem, s_unit.at(q))
                            nc.scalar.activation(SQ, XS[:, k, :], ACT.Square).then_inc(s_squared.sem, 1)
                        else:
                            step = Chain(act, s_root, q * 2).step
                            act.wait_ge(s_chain.sem, s_chain.at(q + 1))
                            step(nc.scalar.activation(SQ, RN, ACT.Ln, scale=1.0 / C))
                            step(nc.scalar.activation(SQ, SQ, ACT.Exp, scale=-0.5))

                    def body(q, k, beside):
                        for m in range(JS):
                            for r in range(R):
                                act.wait_ge(s_sim.sem, s_sim.at(q * NB + (m * R + r + 1)))
                                act.wait_ge(s_power.sem, s_power.at(q * NB + (m * R + r - 1)))
                                nc.scalar.activation(RL[:, r, :], both(2 * r), ACT.Relu).then_inc(s_relu.sem, 1)
                            beside(m)

                    pairs(act, body, prepare, act_at)

                @block.vector
                def _(dve):
                    v = nc.vector

                    def prepare(what, q, k, turn):
                        if what == "shift":
                            dve.wait_ge(s_t.sem, s_t.at(q + 1))
                            for r in range(R):
                                v.tensor_tensor(TT[k][:, r, :, :], PS[:, 4 + r, :].rearrange("p (m c) -> p m c", c=C),
                                                w("l1_b").unsqueeze(1).to_broadcast([P, JS, C]), ALU.add)\
                                    .then_inc(s_tcopy.sem, 1)
                        elif what == "guard":
                            dve.wait_ge(s_norm.sem, s_norm.at(q + 1))
                            v.tensor_scalar(RN, both(4), 1e-16, None, ALU.max).then_inc(s_chain.sem, 1)
                        else:
                            dve.wait_ge(s_root.sem, s_root.at((q + 1) * 2))
                            v.scalar_tensor_tensor(XH[:, k, :], XS[:, k, :], C ** -0.5, SQ, ALU.mult, ALU.mult)\
                                .then_inc(s_unit.sem, 1)

                    def body(q, k, beside):
                        for m in range(JS):
                            for r in range(R):
                                dve.wait_ge(s_relu.sem, s_relu.at(q * NB + (m * R + r + 1)))
                                dve.wait_ge(s_mixed.sem, s_mixed.at(q * NB + (m * R + r - 1)))
                                v.tensor_tensor(R2[:, r, :], RL[:, r, :], RL[:, r, :], ALU.mult)\
                                    .then_inc(s_power.sem, 1)
                            beside(m)
                        dve.wait_ge(s_mixed.sem, s_mixed.at(q * NB + NB))
                        for h in range(2):
                            xt = X[:, bass.ds(q * S + h * T, T)]
                            v.tensor_tensor(xt, PS[:, 6 + h, :], xt, ALU.add).then_inc(s_done.sem, 1)

                    pairs(dve, body, prepare, dve_at)

        TM = T

        def mamba_project():
            a = Arena()
            XS, RAW, ACC, OUT = a.take(S), a.take(2, S + TAPS - 1), a.take(2, S), a.take(2, S)
            ABS, EXPA, LN1, POS, A = a.take(S), a.take(S), a.take(S), a.take(S), a.take(1)
            DT, DEC = ROWS[:, 0:S], ROWS[:, S:2 * S]
            UNITS = [(r, k) for r in range(R) for k in (1, 2, 3, 0)]
            NU, NC = len(UNITS), R * 3
            with nc.Block() as block:
                @block.sync
                def _(sp):
                    with sp.Fori(0, Q) as q:
                        sp.wait_ge(m_proj.sem, m_proj.at(q * NU))
                        sp.dma_start(XS, XN[:, bass.ds(q * S, S)]).then_inc(m_input.sem, 16)
                        for u, (r, k) in enumerate(UNITS):
                            sp.wait_ge(m_silu.sem, m_silu.at(q * NU + (u + 1)))
                            sp.dma_start(scratch[k][bass.ds(q * R + r, 1), :, :].rearrange("a p s -> (a p) s"),
                                         OUT[:, u % 2, :]).then_inc(m_stored[u % 2].sem, 16)
                    for k in range(2):
                        sp.wait_ge(m_stored[k].sem, m_stored[k].at(Q * NU // 2 * 16))

                @block.gpsimd
                def _(pool):
                    nc.gpsimd.memset(RAW[:, :, 0:TAPS - 1], 0.0).then_inc(m_cleared.sem, 1)

                @block.tensor
                def _(pe):
                    mm = nc.tensor.matmul
                    for q in range(Q):
                        for h in range(2):
                            last = mm(PS[:, 4 + h, :], w("m_wdt", q * P, (q + 1) * P),
                                      XN[:, q * S + h * T:q * S + (h + 1) * T], start=q == 0, stop=q == Q - 1)
                    last.then_inc(m_dt.sem, 1)
                    pe.wait_ge(m_rate.sem, m_rate.at(1))
                    with pe.Fori(0, Q) as q:
                        pe.wait_ge(m_input.sem, m_input.at((q + 1) * 16))
                        for u, (r, k) in enumerate(UNITS):
                            pe.wait_ge(m_raw.sem, m_raw.at(q * NU + (u - 3)))
                            for h in range(2):
                                last = mm(PS[:, 2 * (u % 4) + h, :], w("m_win", k * P, (k + 1) * P, half(r)),
                                          XS[half(r), h * T:(h + 1) * T], start=True, stop=True)
                            last.then_inc(m_proj.sem, 1)

                @block.scalar
                def _(act):
                    f = nc.scalar.activation
                    dt_psum = PS[:, 4:6, :].rearrange("p a b -> p (a b)")
                    act.preload_act_table_set(LN_EXP)
                    act.wait_ge(m_dt.sem, m_dt.at(1))
                    step = Chain(act, m_soft).step
                    step(f(ABS, dt_psum, ACT.Abs, bias=w("m_dtb")))
                    step(f(EXPA, ABS, ACT.Exp, scale=-1.0))
                    step(f(LN1, EXPA, ACT.Ln, bias=1.0))
                    step(f(A, w("m_alog"), ACT.Exp))
                    act.wait_ge(m_rate.sem, m_rate.at(3))
                    f(DEC, DT, ACT.Exp, scale=A).then_inc(m_soft.sem, 1)
                    act.wait_ge(m_cleared.sem, m_cleared.at(1))

                    def silu(q, u):
                        r, k = UNITS[u]
                        act.wait_ge(m_stored[u % 2].sem, m_stored[u % 2].at((q * (NU // 2) + u // 2) * 16))
                        if k:
                            act.wait_ge(m_conv.sem, m_conv.at(q * NC + (r * 3 + k)))
                            f(OUT[:, u % 2, :], ACC[:, (r * 3 + k - 1) % 2, :], ACT.Silu,
                              bias=w("m_cb", k - 1, k)).then_inc(m_silu.sem, 1)
                        else:
                            act.wait_ge(m_proj.sem, m_proj.at(q * NU + (u + 1)))
                            f(OUT[:, u % 2, :], PS[:, 2 * (u % 4):2 * (u % 4) + 2, :].rearrange("p a b -> p (a b)"),
                              ACT.Silu).then_inc(m_silu.sem, 1)

                    act.preload_act_table(ACT.Silu)
                    with act.Fori(0, Q) as q:
                        for u, (r, k) in enumerate(UNITS):
                            if k:
                                n = r * 3 + k - 1
                                act.wait_ge(m_proj.sem, m_proj.at(q * NU + (u + 1)))
                                act.wait_ge(m_conv.sem, m_conv.at(q * NC + max(n - 1, 0)))
                                f(RAW[:, n % 2, TAPS - 1:], PS[:, 2 * (u % 4):2 * (u % 4) + 2, :]
                                  .rearrange("p a b -> p (a b)"), ACT.Copy).then_inc(m_raw.sem, 1)
                                if k > 1:
                                    silu(q, u - 1)
                            else:
                                silu(q, u - 1)
                                silu(q, u)
                                act.wait_ge(m_silu.sem, m_silu.at(q * NU + (u + 1)))
                                act.sem_inc(m_raw.sem, 1)

                @block.vector
                def _(dve):
                    v = nc.vector
                    dve.wait_ge(m_soft.sem, m_soft.at(1))
                    step = Chain(dve, m_rate).step
                    step(v.tensor_scalar(POS, PS[:, 4:6, :].rearrange("p a b -> p (a b)"), w("m_dtb"), 0.0,
                                         ALU.add, ALU.max))
                    dve.wait_ge(m_soft.sem, m_soft.at(4))
                    step(v.tensor_tensor(DT, POS, LN1, ALU.add))
                    step(v.tensor_scalar(A, A, -1.0, None, ALU.mult))
                    with dve.Fori(0, Q) as q:
                        for u, (r, k) in enumerate(UNITS):
                            if k == 0:
                                continue
                            n = r * 3 + k - 1
                            raw, acc = RAW[:, n % 2, :], ACC[:, n % 2, :]
                            dve.wait_ge(m_raw.sem, m_raw.at(q * NU + (u + 1)))
                            dve.wait_ge(m_silu.sem, m_silu.at(q * NU + max(u - 1, 0)))
                            step = Chain(dve, m_taps, (q * NC + n) * (TAPS - 1)).step
                            for tap in range(TAPS):
                                cw = w("m_cw", (k - 1) * TAPS + tap, (k - 1) * TAPS + tap + 1)
                                if tap == 0:
                                    step(v.tensor_scalar(acc, raw[:, 0:S], cw, None, ALU.mult))
                                else:
                                    ins = v.scalar_tensor_tensor(acc, raw[:, tap:tap + S], cw, acc,
                                                                 ALU.mult, ALU.add)
                                    if tap < TAPS - 1:
                                        step(ins)
                                    else:
                                        ins.then_inc(m_conv.sem, 1)

        def mamba_scan():
            a = Arena()
            XP, DXP = a.take(2 * HD, TM), a.take(2 * HD, TM)
            U, ST, Z, BT, CT = (a.take(4, TM), a.take(4, TM), a.take(2, TM), a.take(2, TM), a.take(2, TM))
            LAST = a.take(2, HD)
            DT, DEC, CARRY = ROWS[:, 0:S], ROWS[:, S:2 * S], ROWS[:, 2 * S:2 * S + P]
            SKIP = w("m_wdt", 0, P)
            x_rows = scratch[1].rearrange("b (g p) s -> (b g) p s", p=HD)
            y_rows = ys_dram.rearrange("b (g p) s -> (b g) p s", p=HD)
            bc_rows = [scratch[k].rearrange("b (g n) s -> (b g) n s", n=DST) for k in (2, 3)]
            HALVES, STEPS, TURN = S // TM, HD * DST, 2 * HD

            with nc.Block() as block:
                @block.sync
                def _(sp):
                    def load_bc(th, n, k):
                        now = slice(th * TM, (th + 1) * TM)
                        for rows, dst in zip(bc_rows, (BT, CT)):
                            for head in range(NH):
                                sp.dma_start(dst[head:P - 1 + head:NH, k, :],
                                             rows[:, bass.ds(n, 1), now].rearrange("g a s -> g (a s)"))\
                                    .then_inc(c_bc[k].sem, 16)

                    def load_x(th):
                        sp.dma_start(XP[:, th * HD:(th + 1) * HD, :], x_rows[:, :, th * TM:(th + 1) * TM])\
                            .then_inc(c_x[th].sem, 16)

                    def store_y(th):
                        sp.wait_ge(c_ycopy.sem, c_ycopy.at((th + 1) * HD))
                        sp.dma_start(y_rows[:, :, th * TM:(th + 1) * TM], XP[:, th * HD:(th + 1) * HD, :])\
                            .then_inc(c_stored.sem, 16)

                    load_x(0)
                    for k in range(2):
                        load_bc(0, k, k)
                    load_x(1)
                    for th in range(HALVES):
                        if th:
                            for k in range(2):
                                sp.wait_ge(c_u.sem, c_u.at(th * STEPS - (1 - k) * HD))
                                sp.wait_ge(c_z.sem, c_z.at(th * STEPS - (1 - k) * HD))
                                load_bc(th, k, k)
                            store_y(th - 1)
                        with sp.Fori(0, DST // 2 - 1) as i:
                            for k in range(2):
                                sp.wait_ge(c_u.sem, c_u.at(i * TURN + (th * STEPS + (k + 1) * HD)))
                                sp.wait_ge(c_z.sem, c_z.at(i * TURN + (th * STEPS + (k + 1) * HD)))
                                load_bc(th, i * 2 + (k + 2), k)
                    store_y(HALVES - 1)
                    sp.wait_ge(c_stored.sem, c_stored.at(HALVES * 16))

                @block.gpsimd
                def _(pool):
                    for th in range(HALVES):
                        pool.wait_ge(c_dtx.sem, c_dtx.at(th + 1))
                        with pool.Fori(0, DST // 2) as i:
                            for k in range(2):
                                pool.wait_ge(c_bc[k].sem, c_bc[k].at(i * 64 + (th * (DST // 2) + 1) * 64))
                                for p in range(HD):
                                    j = k * HD + p
                                    pool.wait_ge(c_scan.sem, c_scan.at(i * TURN + (th * STEPS + j - 3)))
                                    nc.gpsimd.tensor_tensor(U[:, j % 4, :], DXP[:, th * HD + p, :], BT[:, k, :],
                                                            ALU.mult).then_inc(c_u.sem, 1)

                @block.vector
                def _(dve):
                    v = nc.vector
                    v.tensor_scalar(SKIP, w("ident"), w("m_dh"), None, ALU.mult).then_inc(c_skip.sem, 1)
                    for th in range(HALVES):
                        now = slice(th * TM, (th + 1) * TM)
                        dve.wait_ge(c_x[th].sem, c_x[th].at(16))
                        v.tensor_tensor(DXP[:, th * HD:(th + 1) * HD, :], XP[:, th * HD:(th + 1) * HD, :],
                                        DT[:, now].unsqueeze(1).to_broadcast([P, HD, TM]), ALU.mult)\
                            .then_inc(c_dtx.sem, 1)
                        with dve.Fori(0, DST // 2) as i:
                            def scan(j):
                                at = i * TURN + (th * STEPS + j)
                                dve.wait_ge(c_u.sem, c_u.at(at + 1))
                                dve.wait_ge(c_z.sem, c_z.at(at - 3))
                                if th + 1 < HALVES:
                                    dve.wait_ge(c_kept.sem, c_kept.at(at - 3))
                                first = CARRY[:, bass.ds(i * TURN + j, 1)] if th else 0.0
                                v.tensor_tensor_scan(ST[:, j % 4, :], DEC[:, now], U[:, j % 4, :], first,
                                                     ALU.mult, ALU.add).then_inc(c_scan.sem, 1)

                            def weigh(j):
                                at = i * TURN + (th * STEPS + j)
                                dve.wait_ge(c_scan.sem, c_scan.at(at + 1))
                                dve.wait_ge(c_sum.sem, c_sum.at(at - 1))
                                v.tensor_tensor(Z[:, j % 2, :], ST[:, j % 4, :], CT[:, j // HD, :], ALU.mult)\
                                    .then_inc(c_z.sem, 1)

                            def carry(k):
                                dve.wait_ge(c_kept.sem, c_kept.at(i * TURN + (k + 1) * HD))
                                v.tensor_scalar(CARRY[:, bass.ds(i * TURN + k * HD, HD)], LAST[:, k, :], 1.0, None,
                                                ALU.mult).then_inc(c_carry.sem, 1)

                            for j in range(TURN):
                                scan(j)
                                if j % HD == 1:
                                    dve.wait_ge(c_bc[j // HD].sem,
                                                c_bc[j // HD].at(i * 64 + (th * (DST // 2) + 1) * 64))
                                if j:
                                    weigh(j - 1)
                                if j == HD + 1 and th + 1 < HALVES:
                                    carry(0)
                            weigh(TURN - 1)
                            if th + 1 < HALVES:
                                carry(1)
                        if th + 1 < HALVES:
                            dve.wait_ge(c_carry.sem, c_carry.at(DST))

                @block.tensor
                def _(pe):
                    mm = nc.tensor.matmul
                    pe.wait_ge(c_skip.sem, c_skip.at(1))
                    for th in range(HALVES):
                        pe.wait_ge(c_x[th].sem, c_x[th].at(16))
                        for p in range(HD):
                            if th:
                                pe.wait_ge(c_ycopy.sem, c_ycopy.at(p + 1))
                            mm(PS[:, p, :], SKIP, XP[:, th * HD + p, :], start=True, stop=False)

                        def turn(i, last=False):
                            for j in range(TURN):
                                pe.wait_ge(c_z.sem, c_z.at(i * TURN + (th * STEPS + j + 1)))
                                mm(PS[:, j % HD, :], w("ident"), Z[:, j % 2, :], start=False,
                                   stop=last and j >= HD).then_inc(c_sum.sem, 1)

                        with pe.Fori(0, DST // 2 - 1) as i:
                            turn(i)
                        turn(DST // 2 - 1, last=True)

                @block.scalar
                def _(act):
                    for th in range(HALVES):
                        if th + 1 < HALVES:
                            with act.Fori(0, DST // 2) as i:
                                for j in range(TURN):
                                    act.wait_ge(c_scan.sem, c_scan.at(i * TURN + (j + 1)))
                                    if j % HD == 0:
                                        act.wait_ge(c_carry.sem, c_carry.at(i * 2 + (j // HD - 1)))
                                    nc.scalar.copy(LAST[:, j // HD, j % HD:j % HD + 1], ST[:, j % 4, TM - 1:TM])\
                                        .then_inc(c_kept.sem, 1)
                        for p in range(HD):
                            act.wait_ge(c_sum.sem, c_sum.at((th + 1) * STEPS - (HD - 1 - p)))
                            if p == 0:
                                act.wait_ge(c_dtx.sem, c_dtx.at(th + 1))
                            nc.scalar.copy(XP[:, th * HD + p, :], PS[:, p, :]).then_inc(c_ycopy.sem, 1)

        def mamba_gate():
            a = Arena()
            YL, ZL, G, SQ, ROOT, YN = (a.take(R, S) for _ in range(6))
            WO = a.take(C)
            with nc.Block() as block:
                @block.sync
                def _(sp):
                    with sp.Fori(0, Q) as q:
                        for r in range(R):
                            sp.wait_ge(o_gated.sem, o_gated.at(q * R + r))
                            for src, dst in ((ys_dram, YL), (scratch[0], ZL)):
                                sp.dma_start(dst[:, r, :], src[bass.ds(q * R + r, 1), :, :]
                                             .rearrange("a p s -> (a p) s")).then_inc(o_input[r].sem, 16)

                @block.tensor
                def _(pe):
                    mm = nc.tensor.matmul
                    with pe.Fori(0, Q) as q:
                        for r in range(R):
                            n = q * R + r
                            pe.wait_ge(o_squared.sem, o_squared.at(n + 1))
                            for h in range(2):
                                last = mm(PS[:, 2 * r + h, :], w("mean16"), SQ[:, r, h * T:(h + 1) * T],
                                          start=True, stop=True)
                            last.then_inc(o_mean.sem, 1)
                        pe.wait_ge(o_done.sem, o_done.at(q * 2 + 1))
                        for r in range(R):
                            n = q * R + r
                            pe.wait_ge(o_normed.sem, o_normed.at(n + 1))
                            for h in range(2):
                                last = mm(PS[half(r), 4 + h, :], WO, YN[:, r, h * T:(h + 1) * T],
                                          start=True, stop=True)
                            last.then_inc(o_out.sem, 1)

                @block.scalar
                def _(act):
                    act.preload_act_table_set(LN_EXP)
                    with act.Fori(0, Q) as q:
                        for r in range(R):
                            n = q * R + r
                            act.wait_ge(o_gated.sem, o_gated.at(n + 1))
                            nc.scalar.activation(SQ[:, r, :], G[:, r, :], ACT.Square).then_inc(o_squared.sem, 1)
                            act.wait_ge(o_mean.sem, o_mean.at(n + 1))
                            step = Chain(act, o_root, n * 2).step
                            step(nc.scalar.activation(ROOT[:, r, :],
                                                      PS[:, 2 * r:2 * r + 2, :].rearrange("p a b -> p (a b)"),
                                                      ACT.Ln, bias=w("eps5")))
                            step(nc.scalar.activation(ROOT[:, r, :], ROOT[:, r, :], ACT.Exp, scale=-0.5))

                @block.vector
                def _(dve):
                    v = nc.vector
                    v.tensor_scalar(WO, w("m_wout"), w("m_rms"), None, ALU.mult).then_inc(o_done.sem, 1)
                    with dve.Fori(0, Q) as q:
                        for r in range(R):
                            n = q * R + r
                            dve.wait_ge(o_input[r].sem, o_input[r].at((q + 1) * 32))
                            v.tensor_tensor(G[:, r, :], YL[:, r, :], ZL[:, r, :], ALU.mult).then_inc(o_gated.sem, 1)
                            dve.wait_ge(o_gated.sem, o_gated.at(n + 1))
                            dve.wait_ge(o_root.sem, o_root.at((n + 1) * 2))
                            dve.wait_ge(o_out.sem, o_out.at(q * R))
                            v.tensor_tensor(YN[:, r, :], G[:, r, :], ROOT[:, r, :], ALU.mult)\
                                .then_inc(o_normed.sem, 1)
                        dve.wait_ge(o_out.sem, o_out.at((q + 1) * R))
                        for h in range(2):
                            xt = XN[:, bass.ds(q * S + h * T, T)]
                            v.scalar_tensor_tensor(xt, xt, w("m_skip"), PS[:, 4 + h, :], ALU.mult, ALU.add)\
                                .then_inc(o_done.sem, 1)

        def mamba_output():
            with nc.Block() as block:
                @block.tensor
                def _(pe):
                    with pe.Fori(0, NT // 2) as i:
                        for k in range(2):
                            t = i * 2 + k
                            pe.wait_ge(p_done.sem, p_done.at(t))
                            nc.tensor.matmul(PS[:, k, :], w("m_proj"), tile(XN, t), start=True, stop=True)\
                                .then_inc(p_out.sem, 1)

                @block.vector
                def _(dve):
                    with dve.Fori(0, NT // 2) as i:
                        for k in range(2):
                            t = i * 2 + k
                            dve.wait_ge(p_out.sem, p_out.at(t + 1))
                            nc.vector.scalar_tensor_tensor(tile(X, t), PS[:, k, :], w("m_projb"), tile(X, t),
                                                           ALU.add, ALU.add).then_inc(p_done.sem, 1)

        def involution():
            a = Arena()
            RR, RN = a.take(Q * S), a.take(Q * S)
            XP = a.take(PAD, PAD)
            TMP, SUM = a.take(2, T), a.take(2, T)
            TOTAL, NEGM, SS, SD, SCALE, SHIFT = (a.take(1) for _ in range(6))
            ROWS_T = T // IMG
            with nc.Block() as block:
                @block.tensor
                def _(pe):
                    mm = nc.tensor.matmul
                    for t in range(NT):
                        last = mm(PS[:, t, :], w("i_wr"), XN[:, t * T:(t + 1) * T], start=True, stop=True)
                    last.then_inc(b_reduced.sem, 1)
                    for src, done in ((TOTAL, 1), (SS, 2)):
                        pe.wait_ge(b_total.sem, b_total.at(done))
                        mm(PS[:, 0, 0:1], w("pairs"), src, start=True, stop=True).then_inc(b_moment.sem, 1)

                @block.scalar
                def _(act):
                    f = nc.scalar.activation
                    act.wait_ge(b_reduced.sem, b_reduced.at(1))
                    f(RR, PS[:, :, :].rearrange("p a b -> p (a b)"), ACT.Identity, accum_out=TOTAL)\
                        .then_inc(b_total.sem, 1)
                    act.wait_ge(b_chain.sem, b_chain.at(1))
                    f(RN, RR, ACT.Square, bias=NEGM, accum_out=SS).then_inc(b_total.sem, 1)
                    act.wait_ge(b_moment.sem, b_moment.at(2))
                    f(SD, PS[:, 0, 0:1], ACT.Sqrt, bias=w("eps5")).then_inc(b_total.sem, 1)
                    act.wait_ge(b_chain.sem, b_chain.at(5))
                    f(RN, RR, ACT.Relu, bias=SHIFT, scale=SCALE).then_inc(b_total.sem, 1)

                @block.vector
                def _(dve):
                    v = nc.vector
                    step = Chain(dve, b_chain).step
                    dve.wait_ge(b_moment.sem, b_moment.at(1))
                    step(v.tensor_scalar(NEGM, PS[:, 0, 0:1], -1.0, None, ALU.mult))
                    dve.wait_ge(b_total.sem, b_total.at(3))
                    step(v.reciprocal(SD, SD))
                    step(v.tensor_tensor(SCALE, SD, w("i_gamma"), ALU.mult))
                    step(v.tensor_tensor(SHIFT, NEGM, SCALE, ALU.mult))
                    step(v.tensor_tensor(SHIFT, SHIFT, w("i_beta"), ALU.add))

                @block.gpsimd
                def _(pool):
                    nc.gpsimd.memset(XP, 0.0).then_inc(b_cleared.sem, 1)

            with nc.Block() as block:
                @block.sync
                def _(sp):
                    with sp.Fori(0, Q) as q:
                        sp.wait_ge(i_scaled.sem, i_scaled.at(q * (2 * WIN3)))
                        sp.dma_start(XP[:, 1:1 + IMG, 1:1 + IMG],
                                     XN[:, bass.ds(q * S, S)].rearrange("p (a b) -> p a b", b=IMG))\
                            .then_inc(i_input.sem, 16)

                @block.tensor
                def _(pe):
                    with pe.Fori(0, Q) as q:
                        for h in range(2):
                            for k in range(WIN3):
                                n = h * WIN3 + k
                                pe.wait_ge(i_scaled.sem, i_scaled.at(q * (2 * WIN3) + max(n - 1, 0)))
                                nc.tensor.matmul(PS[:, n % 2, :], w("i_ws", k * P, (k + 1) * P),
                                                 RN[:, bass.ds(q * S + h * T, T)], start=True, stop=True)\
                                    .then_inc(i_kern.sem, 1)

                @block.vector
                def _(dve):
                    v = nc.vector
                    with dve.Fori(0, Q) as q:
                        dve.wait_ge(i_input.sem, i_input.at((q + 1) * 16))
                        for h in range(2):
                            for k in range(WIN3):
                                n = h * WIN3 + k
                                dve.wait_ge(i_kern.sem, i_kern.at(q * (2 * WIN3) + (n + 1)))
                                dve.wait_ge(i_added.sem, i_added.at(q * (2 * (WIN3 - 1)) + h * (WIN3 - 1) + max(k - 2, 0)))
                                dy, dx = divmod(k, 3)
                                dst = TMP[:, k % 2, :] if k else SUM[:, h, :]
                                v.tensor_tensor(dst.rearrange("p (a b) -> p a b", b=IMG),
                                                XP[:, h * ROWS_T + dy:h * ROWS_T + dy + ROWS_T, dx:dx + IMG],
                                                PS[:, n % 2, :].rearrange("p (a b) -> p a b", b=IMG), ALU.mult)\
                                    .then_inc(i_scaled.sem, 1)
                            dve.wait_ge(i_added.sem, i_added.at(q * (2 * (WIN3 - 1)) + (h + 1) * (WIN3 - 1)))
                            xt = X[:, bass.ds(q * S + h * T, T)]
                            v.scalar_tensor_tensor(xt, SUM[:, h, :], 2.0, xt, ALU.mult, ALU.add)\
                                .then_inc(i_done.sem, 1)

                @block.gpsimd
                def _(pool):
                    with pool.Fori(0, Q) as q:
                        for h in range(2):
                            for k in range(1, WIN3):
                                pool.wait_ge(i_scaled.sem, i_scaled.at(q * (2 * WIN3) + h * WIN3 + (k + 1)))
                                if k > 1:
                                    pool.wait_ge(i_added.sem, i_added.at(q * (2 * (WIN3 - 1)) + h * (WIN3 - 1) + (k - 1)))
                                nc.gpsimd.tensor_tensor(SUM[:, h, :], SUM[:, h, :], TMP[:, k % 2, :], ALU.add)\
                                    .then_inc(i_added.sem, 1)

        def fold_gains():
            a = Arena()
            SHIFTED = a.take(E * 2)
            with nc.Block() as block:
                @block.tensor
                def _(pe):
                    for b in range(E * 2):
                        last = nc.tensor.matmul(PS[:, 0, b:b + 1], w("L3_w1", b * 128, (b + 1) * 128, slice(0, C)),
                                                w("l3_b", b // 2, b // 2 + 1, slice(0, C)), start=True, stop=True)
                    last.then_inc(f_shift.sem, 1)

                @block.vector
                def _(dve):
                    v = nc.vector
                    dve.wait_ge(f_shift.sem, f_shift.at(1))
                    v.tensor_tensor(w("L3_b1"), w("L3_b1"), PS[:, 0, 0:E * 2], ALU.add).then_inc(f_done.sem, 1)
                    for e in range(E):
                        v.tensor_scalar(w("L3_w1", e * 256, (e + 1) * 256), w("L3_w1", e * 256, (e + 1) * 256),
                                        w("l3_g", e, e + 1), None, ALU.mult).then_inc(f_done.sem, 1)

        for s in stages:
            if s == "ln6":
                layer_norm(XN, X, "eps6")
            elif s == "ln5":
                layer_norm(XN, X, "eps5")
            elif s.startswith("exp"):
                experts(s[3:5], over_all=s[3:5] == "L1", norms={"L1": 0, "L3": 2}.get(s[3:5], 1))
            elif s == "ln5affine":
                layer_norm(XN, XN, "eps5", ("m_lnw", "m_lnb"))
            else:
                {"L0": linear_attention, "L1": similarity, "project": mamba_project, "scan": mamba_scan,
                 "mgate": mamba_gate, "mout": mamba_output, "L3": involution, "fold": fold_gains}[s]()

        with nc.Block() as block:
            @block.sync
            def _(sp):
                src = stages and stages[-1].startswith("ln") and XN or X
                for r in range(R):
                    dst = out_dram.rearrange("(q r) c s -> r c q s", r=R)[r]
                    sp.dma_start(dst, src[half(r), :].rearrange("c (q s) -> c q s", q=Q))\
                        .then_inc(loaded.sem, 16)
                sp.wait_ge(loaded.sem, loaded.at(32))


STAGES = ["ln6","L0","expL0","ln6","L1","ln5","expL1","ln6","ln5affine","project","scan","mgate","ln5affine","mout","expL2","ln6","L3","fold","expL3"]


def packed(inputs):
    import numpy as _np
    f = {k: _np.asarray(v) for k, v in inputs.items()}
    W = _np.zeros((P, NCOLS), _np.float32)

    def put(name, a, rows=slice(None)):
        at, n = COLS[name]
        W[rows, at:at + n] = a.reshape(a.shape[0], n)

    p = _np.arange(P)
    eye = _np.eye(P, dtype=_np.float32)
    same = (p[:, None] // C == p[None, :] // C).astype(_np.float32)
    put("ident", eye)
    put("center", eye - same / C)
    put("mean64", same / C)
    put("ones64", same)
    put("mean16", (p[:, None] // DIN == p[None, :] // DIN).astype(_np.float32) / DIN)
    put("pairs", (p[:, None] % C == p[None, :] % C).astype(_np.float32) / (B * S))
    put("heads", (p[:, None] // 32 == p[None, :] // 32).astype(_np.float32))
    put("rank", _np.tile(_np.arange(E, 0, -1, dtype=_np.float32), (P, 1)))
    put("eps5", _np.full((P, 1), 1e-5, _np.float32))
    put("eps6", _np.full((P, 1), 1e-6, _np.float32))
    put("ones", _np.ones((P, P), _np.float32))

    def both(a):
        return _np.concatenate([a] * R)

    def diagonal(a, n):
        out = _np.zeros((n, a.shape[0], n, a.shape[1]), _np.float32)
        for i in range(n):
            out[i, :, i] = a
        return out.reshape(n * a.shape[0], n * a.shape[1])

    qkv = f["L0_conv_w_qkv"]
    put("l0_wkT", both(qkv[256:512].T))
    put("l0_wvT", both(qkv[512:768].T))
    put("l0_wq", qkv[0:256].reshape(2, P, C).transpose(1, 0, 2))
    put("l0_woT", f["L0_conv_w_out"].T.reshape(2, P, C).transpose(1, 0, 2))
    put("l0_bo", both(f["L0_conv_b_out"][:, None]))
    put("l1_wT", both(f["L1_conv_W"].T))
    put("l1_b", _np.tile(f["L1_conv_b"], (P, 1)))
    gates = {"L0": ("Wg", "bg"), "L1": ("gate_w", "gate_b"), "L2": ("Wg", "bg"), "L3": ("Wr", "br")}
    for name, blocks in HIDDEN.items():
        g = {k: f[f"{name}_ffn_{k}"] for k in gates[name] + ("W1", "b1", "W2", "b2")}
        put(name + "_wg", diagonal(g[gates[name][0]], R))
        put(name + "_bg", _np.tile(g[gates[name][1]], (P, 1)))
        put(name + "_w1", both(g["W1"].transpose(1, 0, 2)))
        put(name + "_b1", g["b1"].reshape(E * blocks, 128).T)
        put(name + "_w2", g["W2"].reshape(E * blocks, 128, C).transpose(1, 0, 2))
        put(name + "_b2", both(g["b2"].T))
    m = {k[8:]: v for k, v in f.items() if k.startswith("L2_conv_")}
    put("m_lnw", both(m["ln_w"][:, None]))
    put("m_lnb", both(m["ln_b"][:, None]))
    win = _np.stack([diagonal(m["W_in"][:, k * DIN:(k + 1) * DIN], SPLIT) for k in range(4)], 1)
    put("m_win", both(win))
    put("m_cw", _np.tile(m["conv_w"].reshape(3, DIN, TAPS).transpose(1, 0, 2).reshape(DIN, -1), (SPLIT, 1)))
    put("m_cb", _np.tile(m["conv_b"].reshape(3, DIN).T, (SPLIT, 1)))
    wdt = _np.zeros((R, SPLIT, DM, Q, B, SPLIT, NH), _np.float32)
    for q in range(Q):
        for r in range(R):
            for s in range(SPLIT):
                wdt[r, s, :, q, q * R + r, s] = m["W_in"][:, 4 * DIN:]
    put("m_wdt", wdt.reshape(P, Q * P))
    put("m_dtb", _np.tile(m["dt_bias"][:, None], (P // NH, 1)))
    put("m_alog", _np.tile(m["A_log"][:, None], (P // NH, 1)))
    put("m_dh", _np.tile(m["D"][:, None], (P // NH, 1)))
    put("m_rms", _np.tile(m["rms_w"][:, None], (SPLIT, 1)))
    put("m_wout", diagonal(m["W_out"], SPLIT))
    put("m_skip", _np.tile(m["skip_scale"][:, None], (P, 1)))
    put("m_proj", diagonal(m["proj_w"], R))
    put("m_projb", both(m["proj_b"][:, None]))
    put("i_wr", diagonal(f["L3_conv_w_reduce"].T, R))
    put("i_ws", _np.stack([diagonal(_np.repeat(f["L3_conv_w_span"][k][:, None], C, 1), R)
                           for k in range(WIN3)], 1))
    put("i_gamma", both(f["L3_conv_gamma"][:, None]))
    put("i_beta", both(f["L3_conv_beta"][:, None]))
    put("l3_g", both(f["L3_ffn_ln_g"].T))
    put("l3_b", both(f["L3_ffn_ln_b"].T))
    return W


def selectors():
    import numpy as _np
    sel = _np.zeros((PARTS, R, E, E, R, C), _np.float32)
    for r in range(R):
        for e in range(E):
            sel[:, r, e, e, r] = 1
    return _np.concatenate([sel.reshape(GW, E, P), _np.zeros((P - GW, E, P), _np.float32)])


def kernel(**inputs):
    import numpy as _np
    import ml_dtypes as _ml
    import concourse.bacc as _bacc
    from concourse import mybir as _mybir
    from concourse.bass_utils import run_bass_kernel_spmd as _run

    nc = _bacc.Bacc("TRN2", target_bir_lowering=False, num_devices=1)
    arrays = {
        "x_dram": _np.ascontiguousarray(_np.asarray(inputs["x"]).reshape(B, C, S)),
        "w_dram": packed(inputs),
        "sel_dram": selectors().astype(_ml.bfloat16),
    }
    args = [nc.dram_tensor(n, a.shape, _mybir.dt.from_np(a.dtype), kind="ExternalInput").ap()
            for n, a in arrays.items()]
    out = nc.dram_tensor("out_dram", (B, C, S), _mybir.dt.float32, kind="ExternalOutput").ap()
    build(nc, *args, out, STAGES)
    r = _run(nc, [arrays], core_ids=[0])
    return r.results[0]["out_dram"].reshape(B, C, IMG, IMG)
```

```python
from contextlib import ExitStack

import numpy as np
import concourse.bass as bass
from concourse import mybir

FP32 = mybir.dt.float32
BF16 = mybir.dt.bfloat16
I32 = mybir.dt.int32
ALU = mybir.AluOpType
ACT = mybir.ActivationFunctionType
AX = mybir.AxisListType

B, C, S = 8, 64, 1024
R = 2
P = R * C
Q = B // R
T = 512
NT = Q * S // T
E = 8
TOK = 128
JS = S // TOK
PARTS = 3
GW = PARTS * R * E
SPLIT, DM, DIN, DST, NH, HD = 8, 8, 16, 16, 2, 8
TAPS = 3
WIN3 = 9
IMG = 32
PAD = IMG + 2
LN_EXP = "natural_log_exp_and_others"
RSQRT_MAGIC = 0x5F3759DF
ARENA_N = 23600
CREDIT = 4
HIDDEN = {"L0": 2, "L1": 1, "L2": 2, "L3": 2}


def columns():
    sizes = [("ident", P), ("center", P), ("mean64", P), ("ones64", P), ("mean16", P),
             ("pairs", P), ("heads", P), ("rank", E), ("eps5", 1), ("eps6", 1),
             ("l0_wkT", 256), ("l0_wvT", 256), ("l0_wq", 128), ("l0_woT", 128), ("l0_bo", 1),
             ("l1_wT", C), ("l1_b", C)]
    for name, blocks in HIDDEN.items():
        sizes += [(name + "_wg", R * E), (name + "_bg", E), (name + "_w1", E * blocks * 128),
                  (name + "_w2", E * blocks * C), (name + "_b1", E * blocks), (name + "_b2", E)]
    sizes += [("m_lnw", 1), ("m_lnb", 1), ("m_win", 4 * P), ("m_cw", TAPS * 3),
              ("m_cb", 3), ("m_wdt", Q * P), ("m_dtb", 1), ("m_alog", 1), ("m_dh", 1),
              ("m_rms", 1), ("m_wout", C), ("m_skip", 1), ("m_proj", P), ("m_projb", 1),
              ("i_wr", P), ("i_ws", WIN3 * P), ("i_gamma", 1), ("i_beta", 1),
              ("l3_g", E), ("l3_b", E)]
    at, out = 0, {}
    for name, n in sizes:
        out[name] = (at, n)
        at += n
    return out, at


COLS, NCOLS = columns()


class Count:

    def __init__(self, sem):
        self.sem, self.base = sem, 0

    def at(self, n):
        return n + self.base


class Chain:

    def __init__(self, eng, count, start=0):
        self.eng, self.count, self.start, self.n = eng, count, start, 0

    def step(self, ins):
        self.n += 1
        ins.then_inc(self.count.sem, 1)
        self.eng.wait_ge(self.count.sem, self.count.at(self.start + self.n))


def build(nc, x_dram, w_dram, sel_dram, out_dram):
    ctx = ExitStack()
    with ctx:
        def sb(name, shape, dt=FP32):
            return ctx.enter_context(nc.sbuf_tensor(name, shape, dt))

        counts = []

        def count(name):
            counts.append(Count(ctx.enter_context(nc.semaphore(name))))
            return counts[-1]

        X = sb("X", [P, Q * S])
        XN = sb("XN", [P, Q * S])
        W = sb("W", [P, NCOLS])
        SEL = sb("SEL", [P, E, P], BF16)
        IDB = sb("IDB", [P, P], BF16)
        ARENA = sb("ARENA", [P, ARENA_N])
        ROWS = sb("ROWS", [P, 2 * S + 2 * P])
        scratch = [nc.dram_tensor(f"scratch_{k}", (B, P, S), FP32, kind="Internal").ap() for k in "zxbc"]
        ys_dram = nc.dram_tensor("scratch_y", (B, P, S), FP32, kind="Internal").ap()
        PS = ctx.enter_context(nc.psum_tensor("PS", [P, 8, T], FP32))

        def w(name, lo=0, hi=None, rows=slice(None)):
            at, n = COLS[name]
            return W[rows, at + lo:at + (n if hi is None else hi)]

        def apart(eng):
            eng.wait_ge(loaded.sem, CREDIT + 48)

        def half(r):
            return slice(r * C, (r + 1) * C)

        class Arena:

            def __init__(self):
                self.used = 0

            def take(self, *shape):
                n = int(np.prod(shape))
                ap = ARENA[:, self.used:self.used + n]
                self.used += n
                assert self.used <= ARENA_N, self.used
                if len(shape) == 2:
                    ap = ap.rearrange("p (a b) -> p a b", b=shape[1])
                if len(shape) == 3:
                    ap = ap.rearrange("p (a b c) -> p a b c", b=shape[1], c=shape[2])
                return ap

        loaded = count("loaded")
        loaded_rest = count("loaded_rest")
        FIRST = COLS["L0_wg"][0]
        stored = count("stored")
        ln_centered = count("ln_centered")
        ln_squared = count("ln_squared")
        ln_varied = count("ln_varied")
        ln_log = count("ln_log")
        ln_scaled = count("ln_scaled")
        ln_inverted = count("ln_inverted")
        ln_normed = count("ln_normed")
        ln_taken = count("ln_taken")
        ln_newton = count("ln_newton")
        g_logits = count("g_logits")
        g_ranked = count("g_ranked")
        g_taken = count("g_taken")
        g_bent = count("g_bent")
        g_cleared = count("g_cleared")
        g_chain = count("g_chain")
        g_split = count("g_split")
        g_turned = count("g_turned")
        g_rows = count("g_rows")
        e_input = [count(f"e_input{k}") for k in range(2)]
        e_hidden = count("e_hidden")
        e_gelu = count("e_gelu")
        e_weight = count("e_weight")
        e_wcopy = count("e_wcopy")
        e_out = count("e_out")
        e_scaled = count("e_scaled")
        e_added = count("e_added")
        e_fold = count("e_fold")
        a_b1 = count("a_b1")
        a_b1copy = count("a_b1copy")
        a_ctx = count("a_ctx")
        a_ctxcopy = count("a_ctxcopy")
        a_done = count("a_done")
        a_exp = count("a_exp")
        a_input = [count(f"a_input{k}") for k in range(2)]
        a_inv = count("a_inv")
        a_k = count("a_k")
        a_maxed = count("a_maxed")
        a_mt = count("a_mt")
        a_mtcopy = count("a_mtcopy")
        a_out = count("a_out")
        a_sums = count("a_sums")
        a_turned = count("a_turned")
        a_xt = count("a_xt")
        a_xturned = count("a_xturned")
        a_pt = count("a_pt")
        a_gt = count("a_gt")
        b_chain = count("b_chain")
        b_cleared = count("b_cleared")
        b_moment = count("b_moment")
        b_reduced = count("b_reduced")
        b_total = count("b_total")
        c_bc = [count(f"c_bc{k}") for k in range(2)]
        c_carry = count("c_carry")
        c_dtx = count("c_dtx")
        c_kept = count("c_kept")
        c_scan = count("c_scan")
        c_stored = count("c_stored")
        c_skip = count("c_skip")
        c_sum = count("c_sum")
        c_u = count("c_u")
        c_x = [count(f"c_x{k}") for k in range(2)]
        c_ycopy = count("c_ycopy")
        c_z = count("c_z")
        f_done = count("f_done")
        f_shift = count("f_shift")
        i_added = count("i_added")
        i_done = count("i_done")
        i_input = [count(f"i_input{k}") for k in range(2)]
        i_own = count("i_own")
        i_kern = count("i_kern")
        i_scaled = count("i_scaled")
        m_cleared = count("m_cleared")
        m_dt = count("m_dt")
        m_padded = count("m_padded")
        m_proj = count("m_proj")
        m_rate = count("m_rate")
        m_silu = count("m_silu")
        m_soft = count("m_soft")
        m_stored = [count(f"m_stored{k}") for k in range(2)]
        m_taps = count("m_taps")
        m_raw = count("m_raw")
        m_conv = count("m_conv")
        o_done = count("o_done")
        o_gated = count("o_gated")
        o_input = [count(f"o_input{k}") for k in range(2)]
        o_mean = count("o_mean")
        o_normed = count("o_normed")
        o_out = count("o_out")
        o_root = count("o_root")
        o_squared = count("o_squared")
        p_done = count("p_done")
        s_chain = count("s_chain")
        p_out = count("p_out")
        s_done = count("s_done")
        s_input = [count(f"s_input{k}") for k in range(2)]
        s_mixed = count("s_mixed")
        s_norm = count("s_norm")
        s_power = count("s_power")
        s_relu = count("s_relu")
        s_root = count("s_root")
        s_sim = count("s_sim")
        s_squared = count("s_squared")
        s_t = count("s_t")
        s_tcopy = count("s_tcopy")
        s_unit = count("s_unit")

        with nc.Block() as block:
            @block.sync
            def _(sp):
                xv = x_dram.rearrange("(q r) c s -> (r c) q s", r=R)
                for r in range(R):
                    src = x_dram.rearrange("(q r) c s -> r c q s", r=R)[r]
                    sp.dma_start(X[half(r), :].rearrange("c (q s) -> c q s", q=Q), src).then_inc(loaded.sem, 16)
                sp.dma_start(W[:, 0:FIRST], w_dram[:, 0:FIRST]).then_inc(loaded.sem, 16)
                sp.dma_start(W[:, FIRST:], w_dram[:, FIRST:]).then_inc(loaded_rest.sem, 16)
                sp.dma_start(SEL[:, :, :], sel_dram).then_inc(loaded_rest.sem, 16)
                sp.wait_ge(loaded.sem, CREDIT + 48)

            @block.gpsimd
            def _(pool):
                for c in counts:
                    pool.sem_inc(c.sem, CREDIT)
        for c in counts:
            c.base = CREDIT
        loaded.base += 48

        with nc.Block() as block:
            @block.vector
            def _(dve):
                nc.vector.tensor_copy(IDB[:, :], w("ident")).then_inc(stored.sem, 1)
                dve.wait_ge(stored.sem, stored.at(1))

        def tile(buf, t):
            return buf[:, bass.ds(t * T, T)]

        def layer_norm(dst, src, eps, affine=None):
            a = Arena()
            FLY = 4
            SQ, LOG, INV, NRM = (a.take(FLY, T) for _ in range(4))
            with nc.Block() as block:
                @block.tensor
                def _(pe):
                    with pe.Fori(0, NT // FLY) as i:
                        for k in range(FLY):
                            pe.wait_ge(ln_normed.sem, ln_normed.at(i * FLY + (k + 1 - FLY)))
                            nc.tensor.matmul(PS[:, k, :], w("center"), tile(src, i * FLY + k),
                                             start=True, stop=True).then_inc(ln_centered.sem, 1)
                        for k in range(FLY):
                            pe.wait_ge(ln_squared.sem, ln_squared.at(i * FLY + (k + 1)))
                            nc.tensor.matmul(PS[:, FLY + k, :], w("mean64"), SQ[:, k, :],
                                             start=True, stop=True).then_inc(ln_varied.sem, 1)

                @block.scalar
                def _(act):
                    act.preload_act_table_set(LN_EXP)
                    with act.Fori(0, NT // FLY) as i:
                        for k in range(FLY):
                            act.wait_ge(ln_centered.sem, ln_centered.at(i * FLY + (k + 1)))
                            nc.scalar.activation(SQ[:, k, :], PS[:, k, :], ACT.Square)\
                                .then_inc(ln_squared.sem, 1)
                        for k in range(FLY):
                            act.wait_ge(ln_varied.sem, ln_varied.at(i * FLY + (k + 1)))
                            nc.scalar.activation(LOG[:, k, :], PS[:, FLY + k, :], ACT.Ln, bias=w(eps))\
                                .then_inc(ln_log.sem, 1)
                        for k in range(FLY):
                            act.wait_ge(ln_log.sem, ln_log.at(i * FLY + (k + 1)))
                            nc.scalar.activation(INV[:, k, :], LOG[:, k, :], ACT.Exp, scale=-0.5)\
                                .then_inc(ln_inverted.sem, 1)

                @block.vector
                def _(dve):
                    with dve.Fori(0, NT // FLY) as i:
                        for k in range(FLY):
                            dve.wait_ge(ln_inverted.sem, ln_inverted.at(i * FLY + (k + 1)))
                            if affine is None:
                                nc.vector.tensor_tensor(tile(dst, i * FLY + k), PS[:, k, :], INV[:, k, :],
                                                        ALU.mult).then_inc(ln_normed.sem, 1)
                            else:
                                nc.vector.tensor_tensor(NRM[:, k, :], PS[:, k, :], INV[:, k, :],
                                                        ALU.mult).then_inc(ln_scaled.sem, 1)
                                dve.wait_ge(ln_scaled.sem, ln_scaled.at(i * FLY + (k + 1)))
                                nc.vector.tensor_scalar(tile(dst, i * FLY + k), NRM[:, k, :], w(affine[0]),
                                                        w(affine[1]), ALU.mult, ALU.add)\
                                    .then_inc(ln_normed.sem, 1)
            for c in (ln_centered, ln_squared, ln_varied, ln_log, ln_inverted, ln_normed):
                c.base += NT
            if affine:
                ln_scaled.base += NT

        WT = ROWS[:, 0:T].bitcast(BF16).rearrange("p (a b) -> p a b", b=T)

        def experts(layer, over_all=False, norms=1):
            blocks = HIDDEN[layer]
            NB = E * blocks
            NORMS = norms
            renorm = norms == 2
            G = T // TOK
            GR = G * R
            a = Arena()
            XS, H = a.take(2, T), a.take(2, R * T)
            XE = a.take(2, T) if renorm else XS
            WB, TMP, SUM = a.take(2, T), a.take(2, T), a.take(2, T)
            SQ, CEN, VAR, INV, NEWT = (a.take(T) for _ in range(5))
            L, M, SC, S1, S2, REST = (a.take(GR, E) for _ in range(6))
            EX, EY = a.take(GR, E + 1), a.take(GR, E + 1)
            M1, M2, W1, W2 = (a.take(GR) for _ in range(4))
            D = EX[:, :, E:E + 1].rearrange("p a b -> p (a b)")
            PT = a.take(G, GW // 2).rearrange("p a b -> p (a b)").bitcast(BF16)\
                .rearrange("p (g k r e) -> p g k r e", k=PARTS, r=R, e=E)
            PTW = PT.rearrange("p g k r e -> p g (k r e)")
            NEWTON = 2 + 3 * 3
            RANK, WEIGH = 11 + (2 if over_all else 1), 8 + (6 if over_all else 2)
            SIDE = 7

            if renorm:
                pe_at = {0: "center", 2: "vary", 7: "logits", 8: "center2", 10: "vary2", 13: "turn"}
                act_at = {1: "square", 9: "bend square2", 13: "rows"}
                dve_at = {-1: "keep", 1: "start 3 3", 2: "3 norm", 3: "rank", 4: "keep2 weigh start2 3",
                          5: "3 3 norm2"}
            elif norms == 1:
                pe_at = {0: "center", 3: "vary", 8: "logits", 13: "turn"}
                act_at = {1: "square", 11: "bend", 13: "rows"}
                dve_at = {-1: "keep", 1: "start 3 3", 2: "3 norm", 4: "rank", 5: "weigh"}
            else:
                pe_at = {1: "logits", 5: "turn"}
                act_at = {3: "bend", 5: "rows"}
                dve_at = {1: "rank", 3: "weigh"}

            def over(m):
                return m.unsqueeze(2).to_broadcast([P, GR, E])

            def gr(v):
                return v.rearrange("p (g r) e -> p g r e", r=R)

            with nc.Block() as block:
                if not norms:
                    @block.sync
                    def _(sp):
                        for k in range(2):
                            sp.dma_start(XS[:, k, :], tile(XN, k)).then_inc(e_input[k].sem, 16)
                        with sp.Fori(0, NT // 2 - 1) as i:
                            for k in range(2):
                                sp.wait_ge(e_hidden.sem, e_hidden.at((i * 2 + k + 1) * NB))
                                sp.dma_start(XS[:, k, :], tile(XN, i * 2 + k + 2))\
                                    .then_inc(e_input[k].sem, 16)

                @block.gpsimd
                def _(pool):
                    nc.gpsimd.memset(ROWS[:, 0:T], 0.0).then_inc(g_cleared.sem, 1)

                    def tile_of(t, k):
                        for e in range(1, E):
                            pool.wait_ge(e_scaled.sem, e_scaled.at(t * E + (e + 1)))
                            if e > 1:
                                pool.wait_ge(e_added.sem, e_added.at(t * (E - 1) + (e - 1)))
                            nc.gpsimd.tensor_tensor(SUM[:, k, :], SUM[:, k, :], TMP[:, e % 2, :], ALU.add)\
                                .then_inc(e_added.sem, 1)

                    with pool.Fori(0, NT // 2) as i:
                        for k in range(2):
                            tile_of(i * 2 + k, k)

                @block.tensor
                def _(pe):
                    mm = nc.tensor.matmul

                    def center(p, k, n):
                        if n:
                            pe.wait_ge(g_taken.sem, g_taken.at(p + 1))
                        else:
                            pe.wait_ge(g_rows.sem, g_rows.at(p))
                        mm(PS[:, SIDE, :], w("center"), XS[:, k, :] if n else tile(X, p),
                           start=True, stop=True).then_inc(ln_centered.sem, 1)

                    def vary(p, k, n):
                        pe.wait_ge(ln_squared.sem, ln_squared.at(p * NORMS + (n + 1)))
                        mm(PS[:, SIDE, :], w("mean64"), SQ, start=True, stop=True).then_inc(ln_varied.sem, 1)

                    def logits(p, k, turn=None):
                        if norms:
                            pe.wait_ge(ln_normed.sem, ln_normed.at(p * NORMS + 1))
                        else:
                            pe.wait_ge(e_input[k].sem, e_input[k].at((turn + 1) * 16))
                            pe.wait_ge(g_rows.sem, g_rows.at(p))
                        for g in range(G):
                            last = mm(PS[:, SIDE, g * R * E:(g + 1) * R * E], XS[:, k, g * TOK:(g + 1) * TOK],
                                      w(layer + "_wg"), start=True, stop=True)
                        last.then_inc(g_logits.sem, 1)

                    def transpose(p, k):
                        if renorm:
                            pe.wait_ge(ln_taken.sem, ln_taken.at((p + 1) * (2 * NORMS)))
                        pe.wait_ge(g_split.sem, g_split.at(p + 1))
                        for g in range(G):
                            last = mm(PS[0:GW, SIDE, g * TOK:(g + 1) * TOK], PTW[:, g, :], IDB[:, :],
                                      start=True, stop=True)
                        last.then_inc(g_turned.sem, 1)

                    def prepare(what, p, k, turn):
                        if what == "center":
                            center(p, k, 0)
                        elif what == "vary":
                            vary(p, k, 0)
                        elif what == "logits":
                            logits(p, k, turn)
                        elif what == "center2":
                            center(p, k, 1)
                        elif what == "vary2":
                            vary(p, k, 1)
                        elif what == "turn":
                            transpose(p, k)

                    def up(t, k, b):
                        if norms and b == 0:
                            pe.wait_ge(ln_normed.sem, ln_normed.at((t + 1) * NORMS))
                        pe.wait_ge(e_gelu.sem, e_gelu.at(t * NB + (b - 1)))
                        for r in range(R):
                            last = mm(PS[:, (b % 2) * R + r, :], w(layer + "_w1", b * 128, (b + 1) * 128, half(r)),
                                      XE[half(r), k, :], start=True, stop=True)
                        last.then_inc(e_hidden.sem, 1)

                    def tile_of(t, k, i, more=True):
                        def down(b):
                            e, part = divmod(b, blocks)
                            if part == 0:
                                pe.wait_ge(e_wcopy.sem, e_wcopy.at(t * E + e))
                                if e == 0:
                                    pe.wait_ge(g_rows.sem, g_rows.at(t + 1))
                                mm(PS[:, 6, :], SEL[:, e, :], WT[:, k, :], start=True, stop=True)\
                                    .then_inc(e_weight.sem, 1)
                                pe.wait_ge(e_scaled.sem, e_scaled.at(t * E + (e - 1)))
                            pe.wait_ge(e_gelu.sem, e_gelu.at(t * NB + (b + 1)))
                            for r in range(R):
                                last = mm(PS[half(r), 4 + e % 2, :], w(layer + "_w2", b * C, (b + 1) * C),
                                          H[:, b % 2, r * T:(r + 1) * T], start=part == 0, stop=part == blocks - 1)
                            if part == blocks - 1:
                                last.then_inc(e_out.sem, 1)

                        for b in range(NB):
                            if b + 1 < NB:
                                up(t, k, b + 1)
                            elif more:
                                up(t + 1, 1 - k, 0)
                            down(b)
                            if more:
                                prepare(pe_at.get(b), t + 1, 1 - k, i + k)

                    for b in sorted(pe_at):
                        if pe_at[b] == "turn":
                            up(0, 0, 0)
                        prepare(pe_at[b], 0, 0, 0)
                    with pe.Fori(0, NT // 2 - 1) as i:
                        for k in range(2):
                            tile_of(i * 2 + k, k, i)
                    tile_of(NT - 2, 0, NT // 2 - 1)
                    tile_of(NT - 1, 1, NT // 2 - 1, more=False)

                @block.scalar
                def _(act):
                    f = nc.scalar.activation
                    act.preload_act_table(ACT.Gelu)

                    def square(p, n):
                        act.wait_ge(ln_taken.sem, ln_taken.at(p * (2 * NORMS) + (2 * n + 1)))
                        f(SQ, CEN, ACT.Square).then_inc(ln_squared.sem, 1)

                    def bend(p):
                        act.wait_ge(g_ranked.sem, g_ranked.at(p + 1))
                        if over_all:
                            f(EX, EX, ACT.Tanh, scale=0.5).then_inc(g_bent.sem, 1)
                        else:
                            f(D, D, ACT.Tanh, scale=0.5).then_inc(g_bent.sem, 1)

                    def rows(p, k):
                        act.wait_ge(g_cleared.sem, g_cleared.at(1))
                        act.wait_ge(g_turned.sem, g_turned.at(p + 1))
                        nc.scalar.copy(WT[0:GW, k, :], PS[0:GW, SIDE, :])\
                            .then_inc(g_rows.sem, 1)

                    def prepare(steps, p, k):
                        for what in steps.split():
                            if what == "square":
                                square(p, 0)
                            elif what == "bend":
                                bend(p)
                            elif what == "square2":
                                square(p, 1)
                            elif what == "rows":
                                rows(p, k)

                    def tile_of(t, k, more=True):
                        def weight(e):
                            act.wait_ge(e_weight.sem, e_weight.at(t * E + (e + 1)))
                            act.wait_ge(e_scaled.sem, e_scaled.at(t * E + (e - 1)))
                            nc.scalar.copy(WB[:, e % 2, :], PS[:, 6, :]).then_inc(e_wcopy.sem, 1)

                        for b in range(NB + 1):
                            if b < NB:
                                act.wait_ge(e_hidden.sem, e_hidden.at(t * NB + (b + 1)))
                                f(H[:, b % 2, :], PS[:, (b % 2) * R:(b % 2) * R + R, :].rearrange("p a b -> p (a b)"),
                                  ACT.Gelu, bias=w(layer + "_b1", b, b + 1)).then_inc(e_gelu.sem, 1)
                            if b and (b - 1) % blocks == 0:
                                weight((b - 1) // blocks)
                            if b and more:
                                prepare(act_at.get(b - 1, ""), t + 1, 1 - k)

                    for b in sorted(act_at):
                        prepare(act_at[b], 0, 0)
                    with act.Fori(0, NT // 2 - 1) as i:
                        for k in range(2):
                            tile_of(i * 2 + k, k)
                    tile_of(NT - 2, 0)
                    tile_of(NT - 1, 1, more=False)

                @block.vector
                def _(dve):
                    v = nc.vector
                    rank_of = w("rank").unsqueeze(1).to_broadcast([P, GR, E])

                    def keep(p, n):
                        dve.wait_ge(ln_centered.sem, ln_centered.at(p * NORMS + (n + 1)))
                        v.tensor_copy(CEN, PS[:, SIDE, :]).then_inc(ln_taken.sem, 1)

                    def invert(p, k, n, chain, what):
                        step = chain.step
                        if what.startswith("start"):
                            dve.wait_ge(ln_varied.sem, ln_varied.at(p * NORMS + (n + 1)))
                            v.tensor_scalar(VAR, PS[:, SIDE, :], w("eps5"), None, ALU.add).then_inc(ln_taken.sem, 1)
                            dve.wait_ge(ln_taken.sem, ln_taken.at(p * (2 * NORMS) + 2 * (n + 1)))
                            step(v.tensor_scalar(INV.bitcast(I32), VAR.bitcast(I32), 1, None,
                                                 ALU.arith_shift_right))
                            step(v.tensor_scalar(INV.bitcast(I32), INV.bitcast(I32), -1, RSQRT_MAGIC,
                                                 ALU.mult, ALU.add))
                        elif what == "3":
                            step(v.tensor_tensor(NEWT, INV, INV, ALU.mult))
                            step(v.scalar_tensor_tensor(NEWT, NEWT, -0.5, VAR, ALU.mult, ALU.mult))
                            step(v.scalar_tensor_tensor(INV, NEWT, 1.5, INV, ALU.add, ALU.mult))
                        else:
                            assert chain.n == NEWTON
                            v.tensor_tensor((XE if n else XS)[:, k, :], CEN, INV, ALU.mult)\
                                .then_inc(ln_normed.sem, 1)

                    def rank(p):
                        chain = Chain(dve, g_chain, p * (RANK + WEIGH))
                        step = chain.step
                        dve.wait_ge(g_logits.sem, g_logits.at(p + 1))
                        v.tensor_tensor(L, PS[:, SIDE, 0:GR * E].rearrange("p (a e) -> p a e", e=E),
                                        w(layer + "_bg").unsqueeze(1).to_broadcast([P, GR, E]), ALU.add)\
                            .then_inc(g_taken.sem, 1)
                        dve.wait_ge(g_taken.sem, g_taken.at(p + 1))
                        for src, m, sel in ((L, M1, S1), (M, M2, S2)):
                            step(v.tensor_reduce(m, src, AX.X, ALU.max))
                            step(v.tensor_tensor(SC, src, over(m), ALU.is_equal))
                            step(v.tensor_tensor(SC, SC, rank_of, ALU.mult))
                            step(v.tensor_reduce(W1, SC, AX.X, ALU.max))
                            step(v.tensor_tensor(sel, SC, over(W1), ALU.is_equal))
                            if sel is S1:
                                step(v.scalar_tensor_tensor(M, S1, -3.0e38, L, ALU.mult, ALU.add))
                        if over_all:
                            step(v.tensor_tensor(EX[:, :, 0:E], L, over(M1), ALU.subtract))
                        step(v.tensor_tensor(D, M2, M1, ALU.subtract))
                        assert chain.n == RANK
                        dve.sem_inc(g_ranked.sem, 1)

                    def weigh(p):
                        chain = Chain(dve, g_chain, p * (RANK + WEIGH) + RANK)
                        step = chain.step
                        dve.wait_ge(g_bent.sem, g_bent.at(p + 1))
                        if over_all:
                            step(v.tensor_scalar(EY, EX, -1.0, 1.0, ALU.mult, ALU.add))
                            step(v.reciprocal(EY, EY))
                            step(v.scalar_tensor_tensor(EX, EX, 1.0, EY, ALU.add, ALU.mult))
                            step(v.tensor_reduce(M1, EX[:, :, 0:E], AX.X, ALU.add))
                            step(v.reciprocal(W1, M1))
                            step(v.tensor_tensor(W2, D, W1, ALU.mult))
                        else:
                            step(v.tensor_scalar(W1, D, -0.5, 0.5, ALU.mult, ALU.add))
                            step(v.tensor_scalar(W2, D, 0.5, 0.5, ALU.mult, ALU.add))
                        step(v.tensor_tensor(S1, S1, over(W1), ALU.mult))
                        step(v.tensor_tensor(S2, S2, over(W2), ALU.mult))
                        step(v.tensor_tensor(L, S1, S2, ALU.add))
                        rest = L
                        for part in range(PARTS):
                            step(v.tensor_copy(PT[:, :, part, :, :], gr(rest)))
                            if part < PARTS - 1:
                                step(v.tensor_tensor(gr(REST), gr(rest), PT[:, :, part, :, :], ALU.subtract))
                                rest = REST
                        assert chain.n == WEIGH
                        dve.sem_inc(g_split.sem, 1)

                    def prepare_all(p, k):
                        chains = [Chain(dve, ln_newton, p * (NORMS * NEWTON) + n * NEWTON) for n in range(NORMS)]
                        norm = [0]

                        def run(steps):
                            for what in steps.split():
                                if what in ("keep", "keep2"):
                                    keep(p, int(what == "keep2"))
                                elif what == "rank":
                                    rank(p)
                                elif what == "weigh":
                                    weigh(p)
                                else:
                                    invert(p, k, norm[0], chains[norm[0]], what)
                                    if what == "norm":
                                        norm[0] = NORMS - 1
                        return run

                    def tile_of(t, k, more=True):
                        prepare = prepare_all(t + 1, 1 - k)
                        if more:
                            prepare(dve_at.get(-1, ""))
                        for e in range(E):
                            dve.wait_ge(e_wcopy.sem, e_wcopy.at(t * E + (e + 1)))
                            dve.wait_ge(e_out.sem, e_out.at(t * E + (e + 1)))
                            if e:
                                dve.wait_ge(e_added.sem, e_added.at(t * (E - 1) + max(e - 2, 0)))
                            v.scalar_tensor_tensor(
                                TMP[:, e % 2, :] if e else SUM[:, k, :], PS[:, 4 + e % 2, :],
                                w(layer + "_b2", e, e + 1), WB[:, e % 2, :],
                                ALU.add, ALU.mult).then_inc(e_scaled.sem, 1)
                            if more:
                                prepare(dve_at.get(e, ""))
                        dve.wait_ge(e_added.sem, e_added.at((t + 1) * (E - 1)))
                        v.tensor_tensor(tile(X, t), tile(X, t), SUM[:, k, :], ALU.add).then_inc(e_fold.sem, 1)

                    prepare = prepare_all(0, 0)
                    for e in sorted(dve_at):
                        prepare(dve_at[e])
                    with dve.Fori(0, NT // 2 - 1) as i:
                        for k in range(2):
                            tile_of(i * 2 + k, k)
                    tile_of(NT - 2, 0)
                    tile_of(NT - 1, 1, more=False)
            if not norms:
                for c in e_input:
                    c.base += NT // 2 * 16
            e_hidden.base += NT * NB
            e_gelu.base += NT * NB
            for c in (e_weight, e_wcopy, e_out, e_scaled):
                c.base += NT * E
            e_added.base += NT * (E - 1)
            e_fold.base += NT
            for c in (ln_centered, ln_squared, ln_varied, ln_normed):
                c.base += NT * NORMS
            ln_taken.base += NT * NORMS * 2
            ln_newton.base += NT * NORMS * NEWTON
            for c in (g_logits, g_taken, g_ranked, g_bent, g_split, g_turned, g_rows):
                c.base += NT
            g_chain.base += NT * (RANK + WEIGH)
            g_cleared.base += 1

        def linear_attention():
            a = Arena()
            XIN, PC, PT, XT = a.take(2, S), a.take(2, S), a.take(R, JS, 2 * P), a.take(JS, R, C)
            NM, SUM, GT, CT = a.take(2 * R), a.take(2 * R), a.take(2 * P), a.take(2 * R, P)
            B1S, MT = a.take(2 * R, C), a.take(C)
            NU = 2 * R

            def wide(bank, n=2):
                return PS[:, bank:bank + n, :].rearrange("p a b -> p (a b)")

            with nc.Block() as block:
                @block.sync
                def _(sp):
                    for k in range(2):
                        sp.dma_start(XIN[:, k, :], XN[:, k * S:(k + 1) * S]).then_inc(a_input[k].sem, 16)
                    with sp.Fori(0, Q // 2 - 1) as i:
                        for k in range(2):
                            sp.wait_ge(a_out.sem, a_out.at((i * 2 + k + 1) * 2))
                            sp.dma_start(XIN[:, k, :], XN[:, bass.ds(i * (2 * S) + (k + 2) * S, S)])\
                                .then_inc(a_input[k].sem, 16)
                    sp.wait_ge(loaded_rest.sem, loaded_rest.at(32))

                @block.tensor
                def _(pe):
                    mm = nc.tensor.matmul
                    def k_of(q, k, u):
                        r, b = divmod(u, 2)
                        pe.wait_ge(a_exp.sem, a_exp.at(q * NU + (u - 1)))
                        for h in range(2):
                            last = mm(PS[:, 2 * (u % 2) + h, :], w("l0_wkT", b * P, (b + 1) * P, half(r)),
                                      XIN[half(r), k, h * T:(h + 1) * T], start=True, stop=True)
                        last.then_inc(a_k.sem, 1)

                    def pair(q, k, i, more=True):
                        XS = XIN[:, k, :]

                        def turn(u):
                            pe.wait_ge(a_exp.sem, a_exp.at(q * NU + (u + 1)))
                            pe.wait_ge(a_pt.sem, a_pt.at(q * NU + u))
                            for j in range(JS):
                                last = nc.tensor.transpose(PS[:, 4 + j // 4, (j % 4) * TOK:(j % 4 + 1) * TOK],
                                                           PC[:, u % 2, j * TOK:(j + 1) * TOK], w("ident"))
                            last.then_inc(a_turned.sem, 1)

                        pe.wait_ge(a_done.sem, a_done.at(q * 2))
                        for j in range(JS):
                            last = nc.tensor.transpose(PS[:, 6 + j // 4, (j % 4) * TOK:(j % 4 + 1) * TOK],
                                                       XS[:, j * TOK:(j + 1) * TOK], w("ident"))
                        last.then_inc(a_xturned.sem, 1)
                        turn(0)
                        k_of(q, k, 2)
                        turn(1)
                        k_of(q, k, 3)
                        turn(2)
                        turn(3)
                        pe.wait_ge(a_xt.sem, a_xt.at(q + 1))
                        pe.wait_ge(a_pt.sem, a_pt.at((q + 1) * NU))
                        for j in range(JS):
                            for r in range(R):
                                last = mm(PS[half(r), 6, 0:2 * P], XT[:, j, r, :], PT[:, r, j, :],
                                          start=j == 0, stop=j == JS - 1)
                        last.then_inc(a_sums.sem, 1)
                        if more:
                            pe.wait_ge(a_input[1 - k].sem, a_input[1 - k].at((i + k + 1) * 16))
                            k_of(q + 1, 1 - k, 0)
                        pe.wait_ge(a_gt.sem, a_gt.at(q + 1))
                        for r in range(R):
                            for b in range(2):
                                u = r * 2 + b
                                last = mm(PS[:, 7 - 2 * r, b * P:(b + 1) * P], w("l0_wvT", b * P, (b + 1) * P, half(r)),
                                          GT[half(r), b * P:(b + 1) * P], start=True, stop=True)
                        last.then_inc(a_ctx.sem, 1)
                        if more:
                            k_of(q + 1, 1 - k, 1)
                        pe.wait_ge(a_ctxcopy.sem, a_ctxcopy.at((q + 1) * R))
                        for u in range(NU):
                            last = mm(PS[:, 6, u * C:(u + 1) * C], CT[:, u, :],
                                      w("l0_woT", (u % 2) * C, (u % 2 + 1) * C), start=True, stop=True)
                        last.then_inc(a_b1.sem, 1)
                        pe.wait_ge(a_b1copy.sem, a_b1copy.at(q + 1))
                        for b in range(2):
                            for r in range(R):
                                last = mm(PS[half(r), 7, 0:C], w("l0_wq", b * C, (b + 1) * C), B1S[:, r * 2 + b, :],
                                          start=b == 0, stop=b == 1)
                        last.then_inc(a_mt.sem, 1)
                        apart(pe)
                        pe.wait_ge(a_mtcopy.sem, a_mtcopy.at(q + 1))
                        for h in range(2):
                            for r in range(R):
                                last = mm(PS[half(r), 4 + h, :], MT[half(r), :], XS[half(r), h * T:(h + 1) * T],
                                          start=True, stop=True)
                            last.then_inc(a_out.sem, 1)

                    pe.wait_ge(a_input[0].sem, a_input[0].at(16))
                    k_of(0, 0, 0)
                    k_of(0, 0, 1)
                    with pe.Fori(0, Q // 2 - 1) as i:
                        for k in range(2):
                            pair(i * 2 + k, k, i)
                    pair(Q - 2, 0, Q // 2 - 1)
                    pair(Q - 1, 1, Q // 2 - 1, more=False)

                @block.scalar
                def _(act):
                    act.preload_act_table_set(LN_EXP)
                    with act.Fori(0, Q) as q:
                        for u in range(NU):
                            act.wait_ge(a_maxed.sem, a_maxed.at(q * NU + (u + 1)))
                            act.wait_ge(a_turned.sem, a_turned.at(q * NU + max(u - 1, 0)))
                            if u == 0:
                                act.wait_ge(a_b1copy.sem, a_b1copy.at(q))
                            nc.scalar.activation(PC[:, u % 2, :], wide(2 * (u % 2)), ACT.Exp,
                                                 bias=NM[:, u:u + 1], accum_out=SUM[:, u:u + 1])\
                                .then_inc(a_exp.sem, 1)
                            if u == 1:
                                act.wait_ge(a_xturned.sem, a_xturned.at(q + 1))
                                nc.scalar.copy(XT, wide(6).rearrange("p (j r c) -> p j r c", r=R, c=C))\
                                    .then_inc(a_xt.sem, 1)

                @block.vector
                def _(dve):
                    v = nc.vector
                    def pair(q, more=True):
                        def maximum(u, q=q):
                            dve.wait_ge(a_k.sem, a_k.at(q * NU + (u + 1)))
                            v.tensor_reduce(NM[:, u:u + 1], wide(2 * (u % 2)), AX.X, ALU.max, negate=True)\
                                .then_inc(a_maxed.sem, 1)

                        def keep(u):
                            r, b = divmod(u, 2)
                            dve.wait_ge(a_turned.sem, a_turned.at(q * NU + (u + 1)))
                            v.tensor_copy(PT[:, r, :, b * P:(b + 1) * P],
                                          wide(4).rearrange("p (j d) -> p j d", d=P)).then_inc(a_pt.sem, 1)

                        for u in range(NU):
                            keep(u)
                            if u + 2 < NU:
                                maximum(u + 2)
                        dve.wait_ge(a_exp.sem, a_exp.at((q + 1) * NU))
                        v.reciprocal(SUM, SUM).then_inc(a_inv.sem, 1)
                        dve.wait_ge(a_sums.sem, a_sums.at(q + 1))
                        v.tensor_copy(GT, PS[:, 6, 0:2 * P]).then_inc(a_gt.sem, 1)
                        dve.wait_ge(a_ctx.sem, a_ctx.at(q + 1))
                        for r in range(R):
                            v.tensor_tensor(CT[:, 2 * r:2 * r + 2, :],
                                            PS[:, 7 - 2 * r, 0:2 * P].rearrange("p (b d) -> p b d", b=2),
                                            w("heads").unsqueeze(1).to_broadcast([P, 2, P]), ALU.mult)\
                                .then_inc(a_ctxcopy.sem, 1)
                        dve.wait_ge(a_b1.sem, a_b1.at(q + 1))
                        dve.wait_ge(a_inv.sem, a_inv.at(q + 1))
                        v.tensor_tensor(B1S, PS[:, 6, 0:NU * C].rearrange("p (b c) -> p b c", b=NU),
                                        SUM.unsqueeze(2).to_broadcast([P, NU, C]), ALU.mult)\
                            .then_inc(a_b1copy.sem, 1)
                        if more:
                            maximum(0, q + 1)
                        dve.wait_ge(a_mt.sem, a_mt.at(q + 1))
                        v.tensor_copy(MT, PS[:, 7, 0:C]).then_inc(a_mtcopy.sem, 1)
                        if more:
                            maximum(1, q + 1)
                        for h in range(2):
                            dve.wait_ge(a_out.sem, a_out.at(q * 2 + (h + 1)))
                            xt = X[:, bass.ds(q * S + h * T, T)]
                            v.scalar_tensor_tensor(xt, PS[:, 4 + h, :], w("l0_bo"), xt, ALU.add, ALU.add)\
                                .then_inc(a_done.sem, 1)

                    for u in range(2):
                        dve.wait_ge(a_k.sem, a_k.at(u + 1))
                        v.tensor_reduce(NM[:, u:u + 1], wide(2 * u), AX.X, ALU.max, negate=True)\
                            .then_inc(a_maxed.sem, 1)
                    with dve.Fori(0, Q - 1) as q:
                        pair(q)
                    pair(Q - 1, more=False)

        def similarity():
            a = Arena()
            XS, XH = a.take(2, S), a.take(2, S)
            SQ, RN = a.take(S), a.take(S)
            TT = [a.take(R, JS, C) for _ in range(2)]
            RL, R2 = a.take(R, S), a.take(R, S)
            NB = JS * R

            def both(bank):
                return PS[:, bank:bank + 2, :].rearrange("p a b -> p (a b)")

            pe_at = {1: "mapped", 3: "norm"}
            act_at = {1: "square", 5: "root"}
            dve_at = {2: "shift", 4: "guard", 6: "unit"}

            def pairs(eng, body, prepare, steps):
                for at in sorted(steps):
                    prepare(steps[at], 0, 0, 0)
                with eng.Fori(0, Q // 2 - 1) as i:
                    for k in range(2):
                        body(i * 2 + k, k, lambda at, i=i, k=k:
                             at in steps and prepare(steps[at], i * 2 + (k + 1), 1 - k, i + k))
                body(Q - 2, 0, lambda at: at in steps and prepare(steps[at], Q - 1, 1, Q // 2 - 1))
                body(Q - 1, 1, lambda at: None)

            with nc.Block() as block:
                @block.sync
                def _(sp):
                    for k in range(2):
                        sp.dma_start(XS[:, k, :], XN[:, k * S:(k + 1) * S]).then_inc(s_input[k].sem, 16)
                    with sp.Fori(0, Q // 2 - 1) as i:
                        for k in range(2):
                            sp.wait_ge(s_unit.sem, s_unit.at(i * 2 + (k + 1)))
                            sp.dma_start(XS[:, k, :], XN[:, bass.ds(i * (2 * S) + (k + 2) * S, S)])\
                                .then_inc(s_input[k].sem, 16)

                @block.tensor
                def _(pe):
                    mm = nc.tensor.matmul

                    def prepare(what, q, k, turn):
                        if what == "mapped":
                            pe.wait_ge(s_input[k].sem, s_input[k].at((turn + 1) * 16))
                            pe.wait_ge(s_chain.sem, s_chain.at(q))
                            for r in range(R):
                                for m in range(JS):
                                    last = mm(PS[:, 4 + r, m * C:(m + 1) * C],
                                              XS[half(r), k, m * TOK:(m + 1) * TOK],
                                              w("l1_wT", rows=half(r)), start=True, stop=True)
                            last.then_inc(s_t.sem, 1)
                        else:
                            pe.wait_ge(s_squared.sem, s_squared.at(q + 1))
                            pe.wait_ge(s_tcopy.sem, s_tcopy.at((q + 1) * R))
                            for h in range(2):
                                last = mm(PS[:, 4 + h, :], w("ones64"), SQ[:, h * T:(h + 1) * T],
                                          start=True, stop=True)
                            last.then_inc(s_norm.sem, 1)

                    def body(q, k, beside):
                        pe.wait_ge(s_unit.sem, s_unit.at(q + 1))

                        def similar(m):
                            for r in range(R):
                                pe.wait_ge(s_relu.sem, s_relu.at(q * NB + (m * R + r - 1)))
                                for h in range(2):
                                    last = mm(PS[:, 2 * r + h, :], XH[half(r), k, m * TOK:(m + 1) * TOK],
                                              XH[half(r), k, h * T:(h + 1) * T], start=True, stop=True)
                                last.then_inc(s_sim.sem, 1)

                        def mix(m):
                            if m == 0:
                                pe.wait_ge(s_done.sem, s_done.at(q * 2))
                            for r in range(R):
                                pe.wait_ge(s_power.sem, s_power.at(q * NB + (m * R + r + 1)))
                                for h in range(2):
                                    last = mm(PS[half(r), 6 + h, :], TT[k][:, r, m, :],
                                              R2[:, r, h * T:(h + 1) * T], start=m == 0, stop=m == JS - 1)
                                last.then_inc(s_mixed.sem, 1)

                        similar(0)
                        for m in range(1, JS):
                            similar(m)
                            mix(m - 1)
                            beside(m)
                        mix(JS - 1)

                    pairs(pe, body, prepare, pe_at)

                @block.scalar
                def _(act):
                    act.preload_act_table_set(LN_EXP)

                    def prepare(what, q, k, turn):
                        if what == "square":
                            act.wait_ge(s_input[k].sem, s_input[k].at((turn + 1) * 16))
                            act.wait_ge(s_unit.sem, s_unit.at(q))
                            nc.scalar.activation(SQ, XS[:, k, :], ACT.Square).then_inc(s_squared.sem, 1)
                        else:
                            step = Chain(act, s_root, q * 2).step
                            act.wait_ge(s_chain.sem, s_chain.at(q + 1))
                            step(nc.scalar.activation(SQ, RN, ACT.Ln, scale=1.0 / C))
                            step(nc.scalar.activation(SQ, SQ, ACT.Exp, scale=-0.5))

                    def body(q, k, beside):
                        for m in range(JS):
                            for r in range(R):
                                act.wait_ge(s_sim.sem, s_sim.at(q * NB + (m * R + r + 1)))
                                act.wait_ge(s_power.sem, s_power.at(q * NB + (m * R + r - 1)))
                                nc.scalar.activation(RL[:, r, :], both(2 * r), ACT.Relu).then_inc(s_relu.sem, 1)
                            beside(m)

                    pairs(act, body, prepare, act_at)

                @block.vector
                def _(dve):
                    v = nc.vector

                    def prepare(what, q, k, turn):
                        if what == "shift":
                            dve.wait_ge(s_t.sem, s_t.at(q + 1))
                            for r in range(R):
                                v.tensor_tensor(TT[k][:, r, :, :], PS[:, 4 + r, :].rearrange("p (m c) -> p m c", c=C),
                                                w("l1_b").unsqueeze(1).to_broadcast([P, JS, C]), ALU.add)\
                                    .then_inc(s_tcopy.sem, 1)
                        elif what == "guard":
                            dve.wait_ge(s_norm.sem, s_norm.at(q + 1))
                            v.tensor_scalar(RN, both(4), 1e-16, None, ALU.max).then_inc(s_chain.sem, 1)
                        else:
                            dve.wait_ge(s_root.sem, s_root.at((q + 1) * 2))
                            v.scalar_tensor_tensor(XH[:, k, :], XS[:, k, :], C ** -0.5, SQ, ALU.mult, ALU.mult)\
                                .then_inc(s_unit.sem, 1)

                    def body(q, k, beside):
                        for m in range(JS):
                            for r in range(R):
                                dve.wait_ge(s_relu.sem, s_relu.at(q * NB + (m * R + r + 1)))
                                dve.wait_ge(s_mixed.sem, s_mixed.at(q * NB + (m * R + r - 1)))
                                v.tensor_tensor(R2[:, r, :], RL[:, r, :], RL[:, r, :], ALU.mult)\
                                    .then_inc(s_power.sem, 1)
                            beside(m)
                        dve.wait_ge(s_mixed.sem, s_mixed.at(q * NB + NB))
                        for h in range(2):
                            xt = X[:, bass.ds(q * S + h * T, T)]
                            v.tensor_tensor(xt, PS[:, 6 + h, :], xt, ALU.add).then_inc(s_done.sem, 1)

                    pairs(dve, body, prepare, dve_at)

        TM = T

        def mamba_project():
            a = Arena()
            RAW, ACC, OUT = a.take(2, S + TAPS - 1), a.take(2, S), a.take(2, S)
            WIN = a.take(R, 4 * P)
            ABS, EXPA, LN1, POS, A = a.take(S), a.take(S), a.take(S), a.take(S), a.take(1)
            DT, DEC = ROWS[:, 0:S], ROWS[:, S:2 * S]
            UNITS = [(r, k) for r in range(R) for k in (1, 2, 0, 3)]
            CONV = [unit for unit in UNITS if unit[1]]
            SILU = [(r, k) for r in range(R) for k in (1, 0, 2, 3)]
            NU, NC = len(UNITS), len(CONV)
            with nc.Block() as block:
                @block.sync
                def _(sp):
                    with sp.Fori(0, Q) as q:
                        for u, (r, k) in enumerate(SILU):
                            sp.wait_ge(m_silu.sem, m_silu.at(q * NU + (u + 1)))
                            sp.dma_start(scratch[k][bass.ds(q * R + r, 1), :, :].rearrange("a p s -> (a p) s"),
                                         OUT[:, u % 2, :]).then_inc(m_stored[u % 2].sem, 16)
                    for k in range(2):
                        sp.wait_ge(m_stored[k].sem, m_stored[k].at(Q * NU // 2 * 16))

                @block.gpsimd
                def _(pool):
                    nc.gpsimd.memset(RAW[:, :, 0:TAPS - 1], 0.0).then_inc(m_cleared.sem, 1)
                    pool.wait_ge(m_cleared.sem, m_cleared.at(1))
                    step = Chain(pool, m_padded).step
                    step(nc.gpsimd.memset(WIN, 0.0))
                    for r in range(R):
                        step(nc.gpsimd.tensor_copy(WIN[half(r), r, :], w("m_win", rows=half(r))))

                @block.tensor
                def _(pe):
                    mm = nc.tensor.matmul
                    for q in range(Q):
                        for h in range(2):
                            last = mm(PS[:, 4 + h, :], w("m_wdt", q * P, (q + 1) * P),
                                      XN[:, q * S + h * T:q * S + (h + 1) * T], start=q == 0, stop=q == Q - 1)
                    last.then_inc(m_dt.sem, 1)
                    pe.wait_ge(m_rate.sem, m_rate.at(1))
                    pe.wait_ge(m_padded.sem, m_padded.at(1 + R))
                    with pe.Fori(0, Q) as q:
                        for u, (r, k) in enumerate(UNITS):
                            pe.wait_ge(m_raw.sem, m_raw.at(q * NU + (u - 3)))
                            for h in range(2):
                                last = mm(PS[:, 2 * (u % 4) + h, :], WIN[:, r, k * P:(k + 1) * P],
                                          XN[:, bass.ds(q * S + h * T, T)], start=True, stop=True)
                            last.then_inc(m_proj.sem, 1)

                @block.scalar
                def _(act):
                    f = nc.scalar.activation
                    dt_psum = PS[:, 4:6, :].rearrange("p a b -> p (a b)")
                    act.preload_act_table_set(LN_EXP)
                    act.wait_ge(m_dt.sem, m_dt.at(1))
                    step = Chain(act, m_soft).step
                    step(f(ABS, dt_psum, ACT.Abs, bias=w("m_dtb")))
                    step(f(EXPA, ABS, ACT.Exp, scale=-1.0))
                    step(f(LN1, EXPA, ACT.Ln, bias=1.0))
                    step(f(A, w("m_alog"), ACT.Exp))
                    act.wait_ge(m_rate.sem, m_rate.at(3))
                    f(DEC, DT, ACT.Exp, scale=A).then_inc(m_soft.sem, 1)
                    act.wait_ge(m_cleared.sem, m_cleared.at(1))

                    def silu(q, r, k):
                        n = SILU.index((r, k))
                        act.wait_ge(m_stored[n % 2].sem, m_stored[n % 2].at((q * (NU // 2) + n // 2) * 16))
                        if k:
                            c = CONV.index((r, k))
                            act.wait_ge(m_conv.sem, m_conv.at(q * NC + (c + 1)))
                            f(OUT[:, n % 2, :], ACC[:, c % 2, :], ACT.Silu,
                              bias=w("m_cb", k - 1, k)).then_inc(m_silu.sem, 1)
                        else:
                            u = UNITS.index((r, k))
                            act.wait_ge(m_proj.sem, m_proj.at(q * NU + (u + 1)))
                            f(OUT[:, n % 2, :], PS[:, 2 * (u % 4):2 * (u % 4) + 2, :].rearrange("p a b -> p (a b)"),
                              ACT.Silu).then_inc(m_silu.sem, 1)

                    act.preload_act_table(ACT.Silu)
                    with act.Fori(0, Q) as q:
                        for u, (r, k) in enumerate(UNITS):
                            if k:
                                c = CONV.index((r, k))
                                act.wait_ge(m_proj.sem, m_proj.at(q * NU + (u + 1)))
                                act.wait_ge(m_conv.sem, m_conv.at(q * NC + (c - 1)))
                                f(RAW[:, c % 2, TAPS - 1:], PS[:, 2 * (u % 4):2 * (u % 4) + 2, :]
                                  .rearrange("p a b -> p (a b)"), ACT.Copy).then_inc(m_raw.sem, 1)
                                if c:
                                    silu(q, *CONV[c - 1])
                            else:
                                silu(q, r, k)
                                act.wait_ge(m_silu.sem, m_silu.at(q * NU + (SILU.index((r, k)) + 1)))
                                act.sem_inc(m_raw.sem, 1)
                        silu(q, *CONV[-1])

                @block.vector
                def _(dve):
                    v = nc.vector
                    dve.wait_ge(m_soft.sem, m_soft.at(1))
                    step = Chain(dve, m_rate).step
                    step(v.tensor_scalar(POS, PS[:, 4:6, :].rearrange("p a b -> p (a b)"), w("m_dtb"), 0.0,
                                         ALU.add, ALU.max))
                    dve.wait_ge(m_soft.sem, m_soft.at(4))
                    step(v.tensor_tensor(DT, POS, LN1, ALU.add))
                    step(v.tensor_scalar(A, A, -1.0, None, ALU.mult))
                    with dve.Fori(0, Q) as q:
                        for u, (r, k) in enumerate(UNITS):
                            if k == 0:
                                continue
                            n = CONV.index((r, k))
                            raw, acc = RAW[:, n % 2, :], ACC[:, n % 2, :]
                            dve.wait_ge(m_raw.sem, m_raw.at(q * NU + (u + 1)))
                            used = SILU.index(CONV[n - 2]) + 1 - (NU if n < 2 else 0)
                            dve.wait_ge(m_silu.sem, m_silu.at(q * NU + used))
                            step = Chain(dve, m_taps, (q * NC + n) * (TAPS - 1)).step
                            for tap in range(TAPS):
                                cw = w("m_cw", (k - 1) * TAPS + tap, (k - 1) * TAPS + tap + 1)
                                if tap == 0:
                                    step(v.tensor_scalar(acc, raw[:, 0:S], cw, None, ALU.mult))
                                else:
                                    ins = v.scalar_tensor_tensor(acc, raw[:, tap:tap + S], cw, acc,
                                                                 ALU.mult, ALU.add)
                                    if tap < TAPS - 1:
                                        step(ins)
                                    else:
                                        ins.then_inc(m_conv.sem, 1)

        def mamba_scan():
            a = Arena()
            XP, DXP = a.take(2 * HD, TM), a.take(2 * HD, TM)
            U, ST, Z, BT, CT = (a.take(4, TM), a.take(4, TM), a.take(2, TM), a.take(2, TM), a.take(2, TM))
            LAST = a.take(2, HD)
            DT, DEC, CARRY = ROWS[:, 0:S], ROWS[:, S:2 * S], ROWS[:, 2 * S:2 * S + P]
            SKIP = w("m_wdt", 0, P)
            x_rows = scratch[1].rearrange("b (g p) s -> (b g) p s", p=HD)
            y_rows = ys_dram.rearrange("b (g p) s -> (b g) p s", p=HD)
            bc_rows = [scratch[k].rearrange("b (g n) s -> (b g) n s", n=DST) for k in (2, 3)]
            HALVES, STEPS, TURN = S // TM, HD * DST, 2 * HD

            with nc.Block() as block:
                @block.sync
                def _(sp):
                    def load_bc(th, n, k):
                        now = slice(th * TM, (th + 1) * TM)
                        for rows, dst in zip(bc_rows, (BT, CT)):
                            for head in range(NH):
                                sp.dma_start(dst[head:P - 1 + head:NH, k, :],
                                             rows[:, bass.ds(n, 1), now].rearrange("g a s -> g (a s)"))\
                                    .then_inc(c_bc[k].sem, 16)

                    def load_x(th):
                        sp.dma_start(XP[:, th * HD:(th + 1) * HD, :], x_rows[:, :, th * TM:(th + 1) * TM])\
                            .then_inc(c_x[th].sem, 16)

                    def store_y(th):
                        sp.wait_ge(c_ycopy.sem, c_ycopy.at((th + 1) * HD))
                        sp.dma_start(y_rows[:, :, th * TM:(th + 1) * TM], XP[:, th * HD:(th + 1) * HD, :])\
                            .then_inc(c_stored.sem, 16)

                    load_x(0)
                    for k in range(2):
                        load_bc(0, k, k)
                    load_x(1)
                    for th in range(HALVES):
                        if th:
                            for k in range(2):
                                sp.wait_ge(c_u.sem, c_u.at(th * STEPS - (1 - k) * HD))
                                sp.wait_ge(c_z.sem, c_z.at(th * STEPS - (1 - k) * HD))
                                load_bc(th, k, k)
                            store_y(th - 1)
                        with sp.Fori(0, DST // 2 - 1) as i:
                            for k in range(2):
                                sp.wait_ge(c_u.sem, c_u.at(i * TURN + (th * STEPS + (k + 1) * HD)))
                                sp.wait_ge(c_z.sem, c_z.at(i * TURN + (th * STEPS + (k + 1) * HD)))
                                load_bc(th, i * 2 + (k + 2), k)
                    store_y(HALVES - 1)
                    sp.wait_ge(c_stored.sem, c_stored.at(HALVES * 16))

                @block.gpsimd
                def _(pool):
                    for th in range(HALVES):
                        with pool.Fori(0, DST // 2) as i:
                            for k in range(2):
                                pool.wait_ge(c_bc[k].sem, c_bc[k].at(i * 64 + (th * (DST // 2) + 1) * 64))
                                for p in range(HD):
                                    j = k * HD + p
                                    if k == 0:
                                        pool.wait_ge(c_dtx.sem, c_dtx.at(th * (HD // 2) + p // 2 + 1))
                                    pool.wait_ge(c_scan.sem, c_scan.at(i * TURN + (th * STEPS + j - 3)))
                                    nc.gpsimd.tensor_tensor(U[:, j % 4, :], DXP[:, th * HD + p, :], BT[:, k, :],
                                                            ALU.mult).then_inc(c_u.sem, 1)

                @block.vector
                def _(dve):
                    v = nc.vector
                    v.tensor_scalar(SKIP, w("ident"), w("m_dh"), None, ALU.mult).then_inc(c_skip.sem, 1)
                    for th in range(HALVES):
                        now = slice(th * TM, (th + 1) * TM)
                        dve.wait_ge(c_x[th].sem, c_x[th].at(16))
                        for p in range(0, HD, 2):
                            two = slice(th * HD + p, th * HD + p + 2)
                            v.tensor_tensor(DXP[:, two, :], XP[:, two, :],
                                            DT[:, now].unsqueeze(1).to_broadcast([P, 2, TM]), ALU.mult)\
                                .then_inc(c_dtx.sem, 1)
                        with dve.Fori(0, DST // 2) as i:
                            def scan(j):
                                at = i * TURN + (th * STEPS + j)
                                dve.wait_ge(c_u.sem, c_u.at(at + 1))
                                dve.wait_ge(c_z.sem, c_z.at(at - 3))
                                if th + 1 < HALVES:
                                    dve.wait_ge(c_kept.sem, c_kept.at(at - 3))
                                first = CARRY[:, bass.ds(i * TURN + j, 1)] if th else 0.0
                                v.tensor_tensor_scan(ST[:, j % 4, :], DEC[:, now], U[:, j % 4, :], first,
                                                     ALU.mult, ALU.add).then_inc(c_scan.sem, 1)

                            def weigh(j):
                                at = i * TURN + (th * STEPS + j)
                                dve.wait_ge(c_scan.sem, c_scan.at(at + 1))
                                dve.wait_ge(c_sum.sem, c_sum.at(at - 1))
                                v.tensor_tensor(Z[:, j % 2, :], ST[:, j % 4, :], CT[:, j // HD, :], ALU.mult)\
                                    .then_inc(c_z.sem, 1)

                            def carry(k):
                                dve.wait_ge(c_kept.sem, c_kept.at(i * TURN + (k + 1) * HD))
                                v.tensor_scalar(CARRY[:, bass.ds(i * TURN + k * HD, HD)], LAST[:, k, :], 1.0, None,
                                                ALU.mult).then_inc(c_carry.sem, 1)

                            for j in range(TURN):
                                scan(j)
                                if j % HD == 1:
                                    dve.wait_ge(c_bc[j // HD].sem,
                                                c_bc[j // HD].at(i * 64 + (th * (DST // 2) + 1) * 64))
                                if j:
                                    weigh(j - 1)
                                if j == HD + 1 and th + 1 < HALVES:
                                    carry(0)
                            weigh(TURN - 1)
                            if th + 1 < HALVES:
                                carry(1)
                        if th + 1 < HALVES:
                            dve.wait_ge(c_carry.sem, c_carry.at(DST))

                @block.tensor
                def _(pe):
                    mm = nc.tensor.matmul
                    pe.wait_ge(c_skip.sem, c_skip.at(1))
                    for th in range(HALVES):
                        pe.wait_ge(c_x[th].sem, c_x[th].at(16))
                        for p in range(HD):
                            if th:
                                pe.wait_ge(c_ycopy.sem, c_ycopy.at(p + 1))
                            mm(PS[:, p, :], SKIP, XP[:, th * HD + p, :], start=True, stop=False)

                        def turn(i, last=False):
                            for j in range(TURN):
                                pe.wait_ge(c_z.sem, c_z.at(i * TURN + (th * STEPS + j + 1)))
                                mm(PS[:, j % HD, :], w("ident"), Z[:, j % 2, :], start=False,
                                   stop=last and j >= HD).then_inc(c_sum.sem, 1)

                        with pe.Fori(0, DST // 2 - 1) as i:
                            turn(i)
                        turn(DST // 2 - 1, last=True)

                @block.scalar
                def _(act):
                    for th in range(HALVES):
                        if th + 1 < HALVES:
                            with act.Fori(0, DST // 2) as i:
                                for j in range(TURN):
                                    act.wait_ge(c_scan.sem, c_scan.at(i * TURN + (j + 1)))
                                    if j % HD == 0:
                                        act.wait_ge(c_carry.sem, c_carry.at(i * 2 + (j // HD - 1)))
                                    nc.scalar.copy(LAST[:, j // HD, j % HD:j % HD + 1], ST[:, j % 4, TM - 1:TM])\
                                        .then_inc(c_kept.sem, 1)
                        for p in range(HD):
                            act.wait_ge(c_sum.sem, c_sum.at((th + 1) * STEPS - (HD - 1 - p)))
                            if p == 0:
                                act.wait_ge(c_dtx.sem, c_dtx.at((th + 1) * (HD // 2)))
                            nc.scalar.copy(XP[:, th * HD + p, :], PS[:, p, :]).then_inc(c_ycopy.sem, 1)

        def fold_shift(pe):
            for b in range(E * HIDDEN["L3"]):
                last = nc.tensor.matmul(PS[:, 7, b:b + 1], w("L3_w1", b * 128, (b + 1) * 128, slice(0, C)),
                                        w("l3_b", b // HIDDEN["L3"], b // HIDDEN["L3"] + 1, slice(0, C)),
                                        start=True, stop=True)
            last.then_inc(f_shift.sem, 1)

        def fold_gain(dve):
            v, width = nc.vector, HIDDEN["L3"] * 128
            dve.wait_ge(f_shift.sem, f_shift.at(1))
            v.tensor_tensor(w("L3_b1"), w("L3_b1"), PS[:, 7, 0:E * HIDDEN["L3"]], ALU.add).then_inc(f_done.sem, 1)
            for e in range(E):
                v.tensor_scalar(w("L3_w1", e * width, (e + 1) * width), w("L3_w1", e * width, (e + 1) * width),
                                w("l3_g", e, e + 1), None, ALU.mult).then_inc(f_done.sem, 1)

        def mamba_gate():
            a = Arena()
            YL, ZL, G, SQ, ROOT, YN = (a.take(R, S) for _ in range(6))
            WO = a.take(C)
            with nc.Block() as block:
                @block.sync
                def _(sp):
                    with sp.Fori(0, Q) as q:
                        for r in range(R):
                            sp.wait_ge(o_gated.sem, o_gated.at(q * R + (r - 1)))
                            for src, dst in ((ys_dram, YL), (scratch[0], ZL)):
                                sp.dma_start(dst[:, r, :], src[bass.ds(q * R + r, 1), :, :]
                                             .rearrange("a p s -> (a p) s")).then_inc(o_input[r].sem, 16)

                @block.tensor
                def _(pe):
                    mm = nc.tensor.matmul
                    fold_shift(pe)
                    with pe.Fori(0, Q) as q:
                        for r in range(R):
                            n = q * R + r
                            pe.wait_ge(o_squared.sem, o_squared.at(n + 1))
                            for h in range(2):
                                last = mm(PS[:, 2 * r + h, :], w("mean16"), SQ[:, r, h * T:(h + 1) * T],
                                          start=True, stop=True)
                            last.then_inc(o_mean.sem, 1)
                        pe.wait_ge(o_done.sem, o_done.at(q * 2 + 1))
                        for r in range(R):
                            n = q * R + r
                            pe.wait_ge(o_normed.sem, o_normed.at(n + 1))
                            for h in range(2):
                                last = mm(PS[half(r), 4 + h, :], WO, YN[:, r, h * T:(h + 1) * T],
                                          start=True, stop=True)
                            last.then_inc(o_out.sem, 1)

                @block.scalar
                def _(act):
                    act.preload_act_table_set(LN_EXP)
                    with act.Fori(0, Q) as q:
                        for r in range(R):
                            act.wait_ge(o_gated.sem, o_gated.at(q * R + (r + 1)))
                            nc.scalar.activation(SQ[:, r, :], G[:, r, :], ACT.Square).then_inc(o_squared.sem, 1)
                        for r in range(R):
                            n = q * R + r
                            act.wait_ge(o_mean.sem, o_mean.at(n + 1))
                            step = Chain(act, o_root, n * 2).step
                            step(nc.scalar.activation(ROOT[:, r, :],
                                                      PS[:, 2 * r:2 * r + 2, :].rearrange("p a b -> p (a b)"),
                                                      ACT.Ln, bias=w("eps5")))
                            step(nc.scalar.activation(ROOT[:, r, :], ROOT[:, r, :], ACT.Exp, scale=-0.5))

                @block.vector
                def _(dve):
                    v = nc.vector
                    v.tensor_scalar(WO, w("m_wout"), w("m_rms"), None, ALU.mult).then_inc(o_done.sem, 1)
                    fold_gain(dve)

                    def multiply(q):
                        for r in range(R):
                            dve.wait_ge(o_input[r].sem, o_input[r].at((q + 1) * 32))
                            v.tensor_tensor(G[:, r, :], YL[:, r, :], ZL[:, r, :], ALU.mult).then_inc(o_gated.sem, 1)

                    def pair(q, more=True):
                        dve.wait_ge(o_gated.sem, o_gated.at(q * R + R))
                        for r in range(R):
                            n = q * R + r
                            dve.wait_ge(o_root.sem, o_root.at((n + 1) * 2))
                            dve.wait_ge(o_out.sem, o_out.at(q * R))
                            v.tensor_tensor(YN[:, r, :], G[:, r, :], ROOT[:, r, :], ALU.mult)\
                                .then_inc(o_normed.sem, 1)
                        if more:
                            dve.wait_ge(o_normed.sem, o_normed.at(q * R + R))
                            multiply(q + 1)
                        dve.wait_ge(o_out.sem, o_out.at((q + 1) * R))
                        for h in range(2):
                            xt = XN[:, bass.ds(q * S + h * T, T)]
                            v.scalar_tensor_tensor(xt, xt, w("m_skip"), PS[:, 4 + h, :], ALU.mult, ALU.add)\
                                .then_inc(o_done.sem, 1)

                    multiply(0)
                    with dve.Fori(0, Q - 1) as q:
                        pair(q)
                    pair(Q - 1, more=False)

        def mamba_output():
            FLY = 4
            with nc.Block() as block:
                @block.tensor
                def _(pe):
                    with pe.Fori(0, NT // FLY) as i:
                        for k in range(FLY):
                            t = i * FLY + k
                            pe.wait_ge(p_done.sem, p_done.at(t + 1 - FLY))
                            nc.tensor.matmul(PS[:, k, :], w("m_proj"), tile(XN, t), start=True, stop=True)\
                                .then_inc(p_out.sem, 1)

                @block.vector
                def _(dve):
                    with dve.Fori(0, NT // FLY) as i:
                        for k in range(FLY):
                            t = i * FLY + k
                            dve.wait_ge(p_out.sem, p_out.at(t + 1))
                            nc.vector.scalar_tensor_tensor(tile(X, t), PS[:, k, :], w("m_projb"), tile(X, t),
                                                           ALU.add, ALU.add).then_inc(p_done.sem, 1)

        def involution():
            a = Arena()
            RR, RN = a.take(Q * S), a.take(Q * S)
            XP = a.take(2, PAD * PAD).rearrange("p k (a b) -> p k a b", b=PAD)
            TMP, SUM, OSUM, OTMP = a.take(5, T), a.take(2, T), a.take(T), a.take(T)
            TOTAL, NEGM, SS, SD, SCALE, SHIFT, VAR = (a.take(1) for _ in range(7))
            ROWS_T = T // IMG
            with nc.Block() as block:
                @block.tensor
                def _(pe):
                    mm = nc.tensor.matmul
                    for t in range(NT):
                        last = mm(PS[:, t, :], w("i_wr"), XN[:, t * T:(t + 1) * T], start=True, stop=True)
                    last.then_inc(b_reduced.sem, 1)
                    for src, done in ((TOTAL, 1), (SS, 2)):
                        pe.wait_ge(b_total.sem, b_total.at(done))
                        mm(PS[:, 0, 0:1], w("pairs"), src, start=True, stop=True).then_inc(b_moment.sem, 1)

                @block.scalar
                def _(act):
                    f = nc.scalar.activation
                    act.wait_ge(b_reduced.sem, b_reduced.at(1))
                    f(RR, PS[:, :, :].rearrange("p a b -> p (a b)"), ACT.Identity, accum_out=TOTAL)\
                        .then_inc(b_total.sem, 1)
                    act.wait_ge(b_chain.sem, b_chain.at(1))
                    f(RN, RR, ACT.Square, bias=NEGM, accum_out=SS).then_inc(b_total.sem, 1)
                    act.wait_ge(b_moment.sem, b_moment.at(2))
                    f(SD, PS[:, 0, 0:1], ACT.Sqrt, bias=w("eps5")).then_inc(b_total.sem, 1)
                    act.wait_ge(b_chain.sem, b_chain.at(9))
                    f(RN, RR, ACT.Relu, bias=SHIFT, scale=SCALE).then_inc(b_total.sem, 1)

                @block.vector
                def _(dve):
                    v = nc.vector
                    step = Chain(dve, b_chain).step
                    dve.wait_ge(b_moment.sem, b_moment.at(1))
                    step(v.tensor_scalar(NEGM, PS[:, 0, 0:1], -1.0, None, ALU.mult))
                    dve.wait_ge(b_total.sem, b_total.at(3))
                    step(v.reciprocal(SD, SD))
                    step(v.tensor_scalar(VAR, PS[:, 0, 0:1], w("eps5"), None, ALU.add))
                    step(v.tensor_tensor(SCALE, SD, SD, ALU.mult))
                    step(v.scalar_tensor_tensor(SCALE, SCALE, -0.5, VAR, ALU.mult, ALU.mult))
                    step(v.scalar_tensor_tensor(SD, SCALE, 1.5, SD, ALU.add, ALU.mult))
                    step(v.tensor_tensor(SCALE, SD, w("i_gamma"), ALU.mult))
                    step(v.tensor_tensor(SHIFT, NEGM, SCALE, ALU.mult))
                    step(v.tensor_tensor(SHIFT, SHIFT, w("i_beta"), ALU.add))

                @block.gpsimd
                def _(pool):
                    nc.gpsimd.memset(XP, 0.0).then_inc(b_cleared.sem, 1)

            OWN = (2, 4, 7)
            NADD = WIN3 - len(OWN) - 1
            with nc.Block() as block:
                @block.sync
                def _(sp):
                    def load(q, k):
                        sp.dma_start(XP[:, k, 1:1 + IMG, 1:1 + IMG],
                                     XN[:, bass.ds(q * S, S)].rearrange("p (a b) -> p a b", b=IMG))\
                            .then_inc(i_input[k].sem, 16)

                    for k in range(2):
                        load(k, k)
                    with sp.Fori(0, Q // 2 - 1) as i:
                        for k in range(2):
                            sp.wait_ge(i_scaled.sem, i_scaled.at((i * 2 + (k + 1)) * (2 * WIN3)))
                            load(i * 2 + (k + 2), k)

                @block.tensor
                def _(pe):
                    with pe.Fori(0, Q) as q:
                        for h in range(2):
                            for tap in range(WIN3):
                                n = h * WIN3 + tap
                                pe.wait_ge(i_scaled.sem, i_scaled.at(q * (2 * WIN3) + (n - 3)))
                                nc.tensor.matmul(PS[:, n % 6, :], w("i_ws", tap * P, (tap + 1) * P),
                                                 RN[:, bass.ds(q * S + h * T, T)], start=True, stop=True)\
                                    .then_inc(i_kern.sem, 1)

                @block.vector
                def _(dve):
                    v = nc.vector
                    with dve.Fori(0, Q // 2) as i:
                        for k in range(2):
                            q = i * 2 + k
                            dve.wait_ge(i_input[k].sem, i_input[k].at((i + 1) * 16))
                            for h in range(2):
                                xt = X[:, bass.ds(q * S + h * T, T)]
                                own, others = Chain(dve, i_own, q * 6 + h * 3), 0
                                for tap in range(WIN3):
                                    n = h * WIN3 + tap
                                    dve.wait_ge(i_kern.sem, i_kern.at(q * (2 * WIN3) + (n + 1)))
                                    if tap in OWN:
                                        dst = OSUM if tap == OWN[0] else OTMP
                                    elif others == 0:
                                        dst, others = SUM[:, h, :], 1
                                    else:
                                        m = h * NADD + others - 1
                                        dve.wait_ge(i_added.sem, i_added.at(q * (2 * NADD) + (m - 3)))
                                        dst, others = TMP[:, others - 1, :], others + 1
                                    dy, dx = divmod(tap, 3)
                                    v.tensor_tensor(dst.rearrange("p (a b) -> p a b", b=IMG),
                                                    XP[:, k, h * ROWS_T + dy:h * ROWS_T + dy + ROWS_T, dx:dx + IMG],
                                                    PS[:, n % 6, :].rearrange("p (a b) -> p a b", b=IMG), ALU.mult)\
                                        .then_inc(i_scaled.sem, 1)
                                    if tap in OWN[1:]:
                                        dve.wait_ge(i_scaled.sem, i_scaled.at(q * (2 * WIN3) + (n + 1)))
                                        own.step(v.tensor_tensor(OSUM, OSUM, OTMP, ALU.add))
                                own.step(v.scalar_tensor_tensor(xt, OSUM, 2.0, xt, ALU.mult, ALU.add))
                                dve.wait_ge(i_added.sem, i_added.at(q * (2 * NADD) + (h + 1) * NADD))
                                v.scalar_tensor_tensor(xt, SUM[:, h, :], 2.0, xt, ALU.mult, ALU.add)\
                                    .then_inc(i_done.sem, 1)

                @block.gpsimd
                def _(pool):
                    mine = [tap for tap in range(WIN3) if tap not in OWN]
                    with pool.Fori(0, Q) as q:
                        for h in range(2):
                            for j, tap in enumerate(mine[1:]):
                                m = h * NADD + j
                                pool.wait_ge(i_scaled.sem, i_scaled.at(q * (2 * WIN3) + (h * WIN3 + tap + 1)))
                                if j:
                                    pool.wait_ge(i_added.sem, i_added.at(q * (2 * NADD) + m))
                                nc.gpsimd.tensor_tensor(SUM[:, h, :], SUM[:, h, :], TMP[:, j, :], ALU.add)\
                                    .then_inc(i_added.sem, 1)

        layer_norm(XN, X, "eps6")
        linear_attention()
        experts("L0")
        layer_norm(XN, X, "eps6")
        similarity()
        layer_norm(XN, X, "eps5")
        experts("L1", over_all=True, norms=0)
        layer_norm(XN, X, "eps6")
        layer_norm(XN, XN, "eps5", ("m_lnw", "m_lnb"))
        mamba_project()
        mamba_scan()
        mamba_gate()
        layer_norm(XN, XN, "eps5", ("m_lnw", "m_lnb"))
        mamba_output()
        experts("L2")
        layer_norm(XN, X, "eps6")
        involution()
        experts("L3", norms=2)

        with nc.Block() as block:
            @block.sync
            def _(sp):
                for r in range(R):
                    dst = out_dram.rearrange("(q r) c s -> r c q s", r=R)[r]
                    sp.dma_start(dst, X[half(r), :].rearrange("c (q s) -> c q s", q=Q))\
                        .then_inc(loaded.sem, 16)
                sp.wait_ge(loaded.sem, loaded.at(32))




def packed(inputs):
    import numpy as _np
    f = {k: _np.asarray(v) for k, v in inputs.items()}
    W = _np.zeros((P, NCOLS), _np.float32)

    def put(name, a, rows=slice(None)):
        at, n = COLS[name]
        W[rows, at:at + n] = a.reshape(a.shape[0], n)

    p = _np.arange(P)
    eye = _np.eye(P, dtype=_np.float32)
    same = (p[:, None] // C == p[None, :] // C).astype(_np.float32)
    put("ident", eye)
    put("center", eye - same / C)
    put("mean64", same / C)
    put("ones64", same)
    put("mean16", (p[:, None] // DIN == p[None, :] // DIN).astype(_np.float32) / DIN)
    put("pairs", (p[:, None] % C == p[None, :] % C).astype(_np.float32) / (B * S))
    put("heads", (p[:, None] // 32 == p[None, :] // 32).astype(_np.float32))
    put("rank", _np.tile(_np.arange(E, 0, -1, dtype=_np.float32), (P, 1)))
    put("eps5", _np.full((P, 1), 1e-5, _np.float32))
    put("eps6", _np.full((P, 1), 1e-6, _np.float32))

    def both(a):
        return _np.concatenate([a] * R)

    def diagonal(a, n):
        out = _np.zeros((n, a.shape[0], n, a.shape[1]), _np.float32)
        for i in range(n):
            out[i, :, i] = a
        return out.reshape(n * a.shape[0], n * a.shape[1])

    qkv = f["L0_conv_w_qkv"]
    put("l0_wkT", both(qkv[256:512].T))
    put("l0_wvT", both(qkv[512:768].T))
    put("l0_wq", qkv[0:256].reshape(2, P, C).transpose(1, 0, 2))
    put("l0_woT", f["L0_conv_w_out"].T.reshape(2, P, C).transpose(1, 0, 2))
    put("l0_bo", both(f["L0_conv_b_out"][:, None]))
    put("l1_wT", both(f["L1_conv_W"].T))
    put("l1_b", _np.tile(f["L1_conv_b"], (P, 1)))
    gates = {"L0": ("Wg", "bg"), "L1": ("gate_w", "gate_b"), "L2": ("Wg", "bg"), "L3": ("Wr", "br")}
    for name, blocks in HIDDEN.items():
        g = {k: f[f"{name}_ffn_{k}"] for k in gates[name] + ("W1", "b1", "W2", "b2")}
        put(name + "_wg", diagonal(g[gates[name][0]], R))
        put(name + "_bg", _np.tile(g[gates[name][1]], (P, 1)))
        put(name + "_w1", both(g["W1"].transpose(1, 0, 2)))
        put(name + "_b1", g["b1"].reshape(E * blocks, 128).T)
        put(name + "_w2", g["W2"].reshape(E * blocks, 128, C).transpose(1, 0, 2))
        put(name + "_b2", both(g["b2"].T))
    m = {k[8:]: v for k, v in f.items() if k.startswith("L2_conv_")}
    put("m_lnw", both(m["ln_w"][:, None]))
    put("m_lnb", both(m["ln_b"][:, None]))
    win = _np.stack([diagonal(m["W_in"][:, k * DIN:(k + 1) * DIN], SPLIT) for k in range(4)], 1)
    put("m_win", both(win))
    put("m_cw", _np.tile(m["conv_w"].reshape(3, DIN, TAPS).transpose(1, 0, 2).reshape(DIN, -1), (SPLIT, 1)))
    put("m_cb", _np.tile(m["conv_b"].reshape(3, DIN).T, (SPLIT, 1)))
    wdt = _np.zeros((R, SPLIT, DM, Q, B, SPLIT, NH), _np.float32)
    for q in range(Q):
        for r in range(R):
            for s in range(SPLIT):
                wdt[r, s, :, q, q * R + r, s] = m["W_in"][:, 4 * DIN:]
    put("m_wdt", wdt.reshape(P, Q * P))
    put("m_dtb", _np.tile(m["dt_bias"][:, None], (P // NH, 1)))
    put("m_alog", _np.tile(m["A_log"][:, None], (P // NH, 1)))
    put("m_dh", _np.tile(m["D"][:, None], (P // NH, 1)))
    put("m_rms", _np.tile(m["rms_w"][:, None], (SPLIT, 1)))
    put("m_wout", diagonal(m["W_out"], SPLIT))
    put("m_skip", _np.tile(m["skip_scale"][:, None], (P, 1)))
    put("m_proj", diagonal(m["proj_w"], R))
    put("m_projb", both(m["proj_b"][:, None]))
    put("i_wr", diagonal(f["L3_conv_w_reduce"].T, R))
    put("i_ws", _np.stack([diagonal(_np.repeat(f["L3_conv_w_span"][k][:, None], C, 1), R)
                           for k in range(WIN3)], 1))
    put("i_gamma", both(f["L3_conv_gamma"][:, None]))
    put("i_beta", both(f["L3_conv_beta"][:, None]))
    put("l3_g", both(f["L3_ffn_ln_g"].T))
    put("l3_b", both(f["L3_ffn_ln_b"].T))
    return W


def selectors():
    import numpy as _np
    sel = _np.zeros((PARTS, R, E, E, R, C), _np.float32)
    for r in range(R):
        for e in range(E):
            sel[:, r, e, e, r] = 1
    return _np.concatenate([sel.reshape(GW, E, P), _np.zeros((P - GW, E, P), _np.float32)])


def kernel(**inputs):
    import numpy as _np
    import ml_dtypes as _ml
    import concourse.bacc as _bacc
    from concourse import mybir as _mybir
    from concourse.bass_utils import run_bass_kernel_spmd as _run

    nc = _bacc.Bacc("TRN2", target_bir_lowering=False, num_devices=1)
    arrays = {
        "x_dram": _np.ascontiguousarray(_np.asarray(inputs["x"]).reshape(B, C, S)),
        "w_dram": packed(inputs),
        "sel_dram": selectors().astype(_ml.bfloat16),
    }
    args = [nc.dram_tensor(n, a.shape, _mybir.dt.from_np(a.dtype), kind="ExternalInput").ap()
            for n, a in arrays.items()]
    out = nc.dram_tensor("out_dram", (B, C, S), _mybir.dt.float32, kind="ExternalOutput").ap()
    build(nc, *args, out)
    r = _run(nc, [arrays], core_ids=[0])
    return r.results[0]["out_dram"].reshape(B, C, IMG, IMG)
```
